# Optimizing a Trainium2 kernel written in Bass

```python
import numpy as np
import jax
import jax.numpy as jnp

def _softmax(x, axis=-1):
    return jax.nn.softmax(x, axis=axis)

def _gelu(x):
    return jax.nn.gelu(x, approximate=True)

def _silu(x):
    return jax.nn.silu(x)

def _sigmoid(x):
    return jax.nn.sigmoid(x)

def _layernorm(x, axis=-1, eps=1e-05):
    m = jnp.mean(x, axis=axis, keepdims=True)
    v = jnp.var(x, axis=axis, keepdims=True)
    return (x - m) / jnp.sqrt(v + eps)

def _scatter_add(tgt, idx, src, axis=0):
    return tgt.at[idx].add(src)

def _segment_sum(src, seg, n):
    return jax.ops.segment_sum(src, seg, n)
kernel_name = 'mk_xattn_ffn_d1_seqx_r8_98c636'

def setup_inputs(seed: int=0):
    np.random.seed(seed)
    _w = jnp.asarray

    def _rec_inputs():
        import jax
        import jax.numpy as jnp
        _rk = jax.random.key(seed)
        x = -0.000125 + 0.9999 * jax.random.normal(jax.random.fold_in(_rk, 1), (4, 256, 128), jnp.float32)
        _lenS = 256 - jax.random.randint(jax.random.fold_in(_rk, 7), (4,), 0, max(1, 256 // 4) + 1, jnp.int32)
        _lenS2 = 512 - jax.random.randint(jax.random.fold_in(_rk, 8), (4,), 0, max(1, 512 // 4) + 1, jnp.int32)
        _ctx_2048P = jax.random.normal(jax.random.fold_in(_rk, 11), (4, 16, 256), jnp.float32)
        _ctx_2048c = jax.random.dirichlet(jax.random.fold_in(_rk, 511), 0.3 * jnp.ones((16,), jnp.float32), (4, 512))
        _ctx_2048t = jnp.einsum('bsk,bkd->bsd', _ctx_2048c, _ctx_2048P)
        _ctx_2048t = _ctx_2048t * jax.lax.rsqrt(jnp.mean(jnp.square(_ctx_2048t)) + 1e-12) * 0.953939
        ctx_2048 = -1.39393e-06 + 0.999914 * (_ctx_2048t + 0.3 * jax.random.normal(jax.random.fold_in(_rk, 611), (4, 512, 256), jnp.float32))
        return (x, ctx_2048)
    x, ctx_2048 = _rec_inputs()

    def _L0_xattn_setup():
        import jax, jax.numpy as jnp
        import numpy as np
        B, N, DIM = (8, 512, 128)
        M, CTX = (32, 256)
        HEADS, DH = (16, 64)
        INNER = HEADS * DH
        EPS = 1e-06

        def _split_heads(t):
            b, n, _ = t.shape
            return t.reshape(b, n, HEADS, DH).transpose(0, 2, 1, 3)
        key = jax.random.key(seed)
        ks = jax.random.split(key, 6)
        x = jax.random.normal(ks[0], (B, N, DIM), dtype=jnp.float32)
        context = jax.random.normal(ks[1], (B, M, CTX), dtype=jnp.float32)
        Wq = jax.random.normal(ks[2], (DIM, INNER), dtype=jnp.float32) / np.sqrt(DIM)
        Wkv = jax.random.normal(ks[3], (CTX, 2 * INNER), dtype=jnp.float32) / np.sqrt(CTX)
        null_kv = jax.random.normal(ks[4], (2, DH), dtype=jnp.float32) / np.sqrt(2.0)
        Wout = jax.random.normal(ks[5], (INNER, DIM), dtype=jnp.float32) / np.sqrt(INNER)
        ln_scale = jnp.ones((DIM,), dtype=jnp.float32)
        ln_bias = jnp.zeros((DIM,), dtype=jnp.float32)
        return {'x': x, 'context': context, 'Wq': Wq, 'Wkv': Wkv, 'null_kv': null_kv, 'Wout': Wout, 'ln_scale': ln_scale, 'ln_bias': ln_bias}
    _L0_xattn_all = _L0_xattn_setup()
    _L0_xattn_in = {k: v for k, v in _L0_xattn_all.items() if k in ('Wq', 'Wkv', 'null_kv', 'Wout', 'ln_scale', 'ln_bias')}
    del _L0_xattn_all

    def _L0_ffn_setup():
        import jax, jax.numpy as jnp
        import numpy as np
        D = 128
        H = 16
        KV = 8
        HD = D // H
        M = 448
        E = 8
        TOPK = 2
        EPS = 1e-06
        ROPE_THETA = 10000.0

        def _rmsnorm(x, w, eps=EPS):
            xf = x.astype(jnp.float32)
            var = jnp.mean(xf * xf, axis=-1, keepdims=True)
            return (xf * jax.lax.rsqrt(var + eps)).astype(x.dtype) * w

        def _rope(q, k):
            S = q.shape[1]
            inv_freq = 1.0 / ROPE_THETA ** (jnp.arange(0, HD, 2, dtype=jnp.float32) / HD)
            ang = jnp.arange(S, dtype=jnp.float32)[:, None] * inv_freq[None, :]
            cos = jnp.concatenate([jnp.cos(ang), jnp.cos(ang)], axis=-1)[None, :, None, :]
            sin = jnp.concatenate([jnp.sin(ang), jnp.sin(ang)], axis=-1)[None, :, None, :]

            def rot_half(t):
                t1, t2 = jnp.split(t, 2, axis=-1)
                return jnp.concatenate([-t2, t1], axis=-1)
            return (q * cos + rot_half(q) * sin, k * cos + rot_half(k) * sin)
        key = jax.random.key(seed)
        ks = jax.random.split(key, 12)
        s = 0.02
        B, S = (2, 128)
        return {'x': jax.random.normal(ks[0], (B, S, D), jnp.float32), 'ln1_w': jnp.ones((D,), jnp.float32), 'ln2_w': jnp.ones((D,), jnp.float32), 'wq': jax.random.normal(ks[1], (D, H * HD), jnp.float32) * s, 'wk': jax.random.normal(ks[2], (D, KV * HD), jnp.float32) * s, 'wv': jax.random.normal(ks[3], (D, KV * HD), jnp.float32) * s, 'wo': jax.random.normal(ks[4], (H * HD, D), jnp.float32) * s, 'router_w': jax.random.normal(ks[5], (D, E), jnp.float32) * s, 'w_gate': jax.random.normal(ks[6], (E, D, M), jnp.float32) * s, 'w_up': jax.random.normal(ks[7], (E, D, M), jnp.float32) * s, 'w_down': jax.random.normal(ks[8], (E, M, D), jnp.float32) * s}
    _L0_ffn_all = _L0_ffn_setup()
    _L0_ffn_in = {k: v for k, v in _L0_ffn_all.items() if k in ('ln1_w', 'ln2_w', 'wq', 'wk', 'wv', 'wo', 'router_w', 'w_gate', 'w_up', 'w_down')}
    del _L0_ffn_all
    return {'x': x, 'ctx_2048': ctx_2048, 'L0_xattn_Wq': _L0_xattn_in['Wq'], 'L0_xattn_Wkv': _L0_xattn_in['Wkv'], 'L0_xattn_null_kv': _L0_xattn_in['null_kv'], 'L0_xattn_Wout': _L0_xattn_in['Wout'], 'L0_xattn_ln_scale': _L0_xattn_in['ln_scale'], 'L0_xattn_ln_bias': _L0_xattn_in['ln_bias'], 'L0_ffn_ln1_w': _L0_ffn_in['ln1_w'], 'L0_ffn_ln2_w': _L0_ffn_in['ln2_w'], 'L0_ffn_wq': _L0_ffn_in['wq'], 'L0_ffn_wk': _L0_ffn_in['wk'], 'L0_ffn_wv': _L0_ffn_in['wv'], 'L0_ffn_wo': _L0_ffn_in['wo'], 'L0_ffn_router_w': _L0_ffn_in['router_w'], 'L0_ffn_w_gate': _L0_ffn_in['w_gate'], 'L0_ffn_w_up': _L0_ffn_in['w_up'], 'L0_ffn_w_down': _L0_ffn_in['w_down']}

def reference(x, ctx_2048, L0_xattn_Wq, L0_xattn_Wkv, L0_xattn_null_kv, L0_xattn_Wout, L0_xattn_ln_scale, L0_xattn_ln_bias, L0_ffn_ln1_w, L0_ffn_ln2_w, L0_ffn_wq, L0_ffn_wk, L0_ffn_wv, L0_ffn_wo, L0_ffn_router_w, L0_ffn_w_gate, L0_ffn_w_up, L0_ffn_w_down):
    import jax
    import jax.numpy as jnp

    def _L0_xattn_ref(x, context, Wq, Wkv, null_kv, Wout, ln_scale, ln_bias):
        import jax, jax.numpy as jnp
        import numpy as np
        B, N, DIM = (8, 512, 128)
        M, CTX = (32, 256)
        HEADS, DH = (16, 64)
        INNER = HEADS * DH
        EPS = 1e-06

        def _split_heads(t):
            b, n, _ = t.shape
            return t.reshape(b, n, HEADS, DH).transpose(0, 2, 1, 3)
        scale = DH ** (-0.5)
        b = x.shape[0]
        q = _split_heads(jnp.einsum('bnd,df->bnf', x, Wq))
        kv = jnp.einsum('bmc,cf->bmf', context, Wkv)
        k, v = jnp.split(kv, 2, axis=-1)
        k, v = (_split_heads(k), _split_heads(v))
        nk = jnp.broadcast_to(null_kv[0], (b, HEADS, 1, DH))
        nv = jnp.broadcast_to(null_kv[1], (b, HEADS, 1, DH))
        k = jnp.concatenate((nk, k), axis=-2)
        v = jnp.concatenate((nv, v), axis=-2)
        q = q * scale
        sim = jnp.einsum('bhid,bhjd->bhij', q, k)
        attn = jax.nn.softmax(sim, axis=-1)
        out = jnp.einsum('bhij,bhjd->bhid', attn, v)
        out = out.transpose(0, 2, 1, 3).reshape(b, -1, INNER)
        out = jnp.einsum('bnf,fd->bnd', out, Wout)
        mu = jnp.mean(out, axis=-1, keepdims=True)
        var = jnp.var(out, axis=-1, keepdims=True)
        out = (out - mu) * jax.lax.rsqrt(var + EPS) * ln_scale + ln_bias
        return out

    def _L0_ffn_ref(x, ln1_w, ln2_w, wq, wk, wv, wo, router_w, w_gate, w_up, w_down):
        import jax, jax.numpy as jnp
        import numpy as np
        D = 128
        H = 16
        KV = 8
        HD = D // H
        M = 448
        E = 8
        TOPK = 2
        EPS = 1e-06
        ROPE_THETA = 10000.0

        def _rmsnorm(x, w, eps=EPS):
            xf = x.astype(jnp.float32)
            var = jnp.mean(xf * xf, axis=-1, keepdims=True)
            return (xf * jax.lax.rsqrt(var + eps)).astype(x.dtype) * w

        def _rope(q, k):
            S = q.shape[1]
            inv_freq = 1.0 / ROPE_THETA ** (jnp.arange(0, HD, 2, dtype=jnp.float32) / HD)
            ang = jnp.arange(S, dtype=jnp.float32)[:, None] * inv_freq[None, :]
            cos = jnp.concatenate([jnp.cos(ang), jnp.cos(ang)], axis=-1)[None, :, None, :]
            sin = jnp.concatenate([jnp.sin(ang), jnp.sin(ang)], axis=-1)[None, :, None, :]

            def rot_half(t):
                t1, t2 = jnp.split(t, 2, axis=-1)
                return jnp.concatenate([-t2, t1], axis=-1)
            return (q * cos + rot_half(q) * sin, k * cos + rot_half(k) * sin)
        B, S, _ = x.shape
        h = _rmsnorm(x, ln1_w)
        q = (h @ wq).reshape(B, S, H, HD)
        k = (h @ wk).reshape(B, S, KV, HD)
        v = (h @ wv).reshape(B, S, KV, HD)
        q, k = _rope(q, k)
        rep = H // KV
        k = jnp.repeat(k, rep, axis=2)
        v = jnp.repeat(v, rep, axis=2)
        scores = jnp.einsum('bqhd,bkhd->bhqk', q, k) / jnp.sqrt(jnp.float32(HD))
        causal = jnp.tril(jnp.ones((S, S), bool))
        scores = jnp.where(causal[None, None], scores, jnp.finfo(scores.dtype).min)
        attn = jax.nn.softmax(scores, axis=-1)
        ao = jnp.einsum('bhqk,bkhd->bqhd', attn, v).reshape(B, S, H * HD)
        x = x + ao @ wo
        h = _rmsnorm(x, ln2_w)
        logits = h @ router_w
        probs = jax.nn.softmax(logits, axis=-1)
        topv, topi = jax.lax.top_k(probs, TOPK)
        topv = topv / jnp.sum(topv, axis=-1, keepdims=True)
        weights = jnp.sum(jax.nn.one_hot(topi, E, dtype=h.dtype) * topv[..., None], axis=-2)
        gate = jnp.einsum('bsd,edm->bsem', h, w_gate)
        up = jnp.einsum('bsd,edm->bsem', h, w_up)
        act = jax.nn.silu(gate) * up * weights[..., None]
        moe = jnp.einsum('bsem,emd->bsd', act, w_down)
        return x + moe
    x = x + _L0_xattn_ref(_layernorm(x, axis=-1), ctx_2048, L0_xattn_Wq, L0_xattn_Wkv, L0_xattn_null_kv, L0_xattn_Wout, L0_xattn_ln_scale, L0_xattn_ln_bias)
    x = x + _L0_ffn_ref(_layernorm(x, axis=-1), L0_ffn_ln1_w, L0_ffn_ln2_w, L0_ffn_wq, L0_ffn_wk, L0_ffn_wv, L0_ffn_wo, L0_ffn_router_w, L0_ffn_w_gate, L0_ffn_w_up, L0_ffn_w_down)
    return x

_drawn_inputs = setup_inputs


def setup_inputs(seed=0):
    import zlib

    import numpy as np

    out = dict(_drawn_inputs(seed))
    spreads = {'L0_xattn_ln_scale': (1.0, 0.2),
     'L0_xattn_ln_bias': (0.0, 0.1),
     'L0_ffn_ln1_w': (1.0, 0.6),
     'L0_ffn_ln2_w': (1.0, 0.6)}
    factors = {'L0_xattn_null_kv': 8.0,
     'L0_ffn_wq': 8.0,
     'L0_ffn_wk': 8.0,
     'L0_ffn_wv': 3.926,
     'L0_ffn_wo': 3.835,
     'L0_ffn_router_w': 8.0,
     'L0_ffn_w_gate': 8.0,
     'L0_ffn_w_up': 8.0,
     'L0_ffn_w_down': 8.0}
    for name, (base, spread) in spreads.items():
        noise = np.random.default_rng([zlib.crc32(name.encode()), seed]).standard_normal(out[name].shape)
        drawn = base * np.exp(spread * noise) if base else spread * noise
        out[name] = jnp.asarray(drawn.astype(out[name].dtype))
    for name, factor in factors.items():
        out[name] = (out[name] * factor).astype(out[name].dtype)
    return out
```

```python
from contextlib import ExitStack

import concourse.bass as bass
from concourse import mybir

F32 = mybir.dt.float32
F32R = mybir.dt.float32r
BF16 = mybir.dt.bfloat16
U32 = mybir.dt.uint32
ALU = mybir.AluOpType
ACT = mybir.ActivationFunctionType
AX_X = mybir.AxisListType.X

P = 128
BANK = 512

B, N, D = 4, 256, 128
TOK = B * N
TT = TOK // P
QT = N // P
M, C = 512, 256
KT = M // P
CT = C // P
H, DH = 16, 64
INNER = H * DH
X_SCALE = DH ** -0.5
PROJ = 5

FH, KV, HD = 16, 8, 8
REP = FH // KV
F_SCALE = float(HD) ** -0.5
E, HID = 8, 448
PAIRS = E // 2
SLABS = 2 * HID // P
CH = TOK // BANK
MASKED = -1e30


def f(ap):
    return ap.bitcast(F32)


def in_tiles(dram):
    return dram.rearrange("b (t p) d -> p (b t) d", p=P)


class Kernel:
    pass


def layer_stats(dve, sems, src, stats, mean_var, tiles=TT):
    for t in range(tiles):
        last = dve.bn_stats(stats[:, t, :], src[:, t, :])
    last.then_inc(sems["stats"], 1)
    dve.wait_ge(sems["stats"], 1)
    for t in range(tiles):
        last = dve.bn_aggr(mean_var[:, t, :], stats[:, t, :])
    last.then_inc(sems["var"], 1)


def normalise(dve, sems, src, mean_var, std, rstd, dst, tiles=TT):
    dve.wait_ge(sems["std"], 1)
    dve.reciprocal(rstd[:, 0:tiles], std[:, 0:tiles]).then_inc(sems["rstd"], 1)
    dve.wait_ge(sems["rstd"], 1)
    for t in range(tiles):
        last = dve.tensor_scalar(dst[:, t, :], src[:, t, :], mean_var[:, t, 0:1], rstd[:, t:t + 1],
                                 ALU.subtract, ALU.mult)
    return last


def norm_sems(sem, name):
    return {k: sem(f"{name}_{k}") for k in ("stats", "var", "std", "rstd")}


def load_and_split(nc, k, dram):
    with ExitStack() as ctx:
        def sb(name, shape, dt=F32):
            return ctx.enter_context(nc.sbuf_tensor(name, shape, dt))

        def sem(name):
            return ctx.enter_context(nc.semaphore(name))

        wq_raw = sb("wq_raw", [P, H, 2, DH])
        wkv_raw = sb("wkv_raw", [P, CT, 2 * INNER])
        wout_raw = sb("wout_raw", [P, H, D])
        nk_row = sb("nk_row", [P, DH])
        nv_col = sb("nv_col", [DH, 1])
        nv_diag = sb("nv_diag", [DH, H, H])
        nk_wq = sb("nk_wq", [P, H, DH])
        w0 = sb("w0", [P, H])
        xn = sb("xn", [P, TT, D])
        xnT = sb("xnT", [P, TOK])
        stats = sb("stats1", [P, TT, 6])
        mean_var = sb("mean_var1", [P, TT, 2])
        std, rstd = sb("std1", [P, TT]), sb("rstd1", [P, TT])
        pT = [ctx.enter_context(nc.psum_tensor(f"p_xnT{i}", [P, BANK], F32)) for i in range(2)]
        pS0 = ctx.enter_context(nc.psum_tensor("p_s0", [P, TT, H], F32))
        pU = ctx.enter_context(nc.psum_tensor("p_u", [H, D], F32))

        x_in, wq_in, wkv_in = sem("x_in"), sem("wq_in"), sem("wkv_in")
        wout_in, null_in, const_in = sem("wout_in"), sem("null_in"), sem("const_in")
        eps_set, diag_zero, diag_set = sem("eps_set"), sem("diag_zero"), sem("diag_set")
        norm = norm_sems(sem, "ln1")
        xn_ready, xnT_ps, xnT_ready, xnT_hi = sem("xn_ready"), sem("xnT_ps"), sem("xnT_ready"), sem("xnT_hi_s")
        w0_mul, w0_ready, s0_ps, u_ps, u_hi_s = sem("w0_mul"), sem("w0_ready"), sem("s0_ps"), sem("u_ps"), sem("u_hi_s")
        wq_hi_s, wkv_hi_s, wout_hi_s = sem("wq_hi_s"), sem("wkv_hi_s"), sem("wout_hi_s")

        block = ctx.enter_context(nc.Block())

        @block.sync
        def _(sp):
            sp.dma_start(k.x[:, :, :], in_tiles(dram["x"])).then_inc(x_in, 16)
            sp.dma_start(k.ident[:, :], dram["identity"]).then_inc(const_in, 16)
            for c in range(CT):
                sp.dma_start(wkv_raw[:, c, :], dram["L0_xattn_Wkv"][c * P:(c + 1) * P, :]).then_inc(wkv_in, 16)
            for half in range(2):
                sp.dma_start(wout_raw[half * DH:(half + 1) * DH, :, :],
                             dram["L0_xattn_Wout"].rearrange("(h r) d -> r h d", h=H)).then_inc(wout_in, 16)

        @block.scalar
        def _(act):
            act.dma_start(nk_row[:, :], dram["L0_xattn_null_kv"][0, :].partition_broadcast(P)).then_inc(null_in, 16)
            act.dma_start(nv_col[:, :], dram["L0_xattn_null_kv"][1, :].rearrange("(d o) -> d o", o=1)).then_inc(null_in, 16)
            for half in range(2):
                act.dma_start(wq_raw[:, :, half, :],
                              dram["L0_xattn_Wq"].rearrange("c (h d) -> c h d", h=H)).then_inc(wq_in, 16)
            act.wait_ge(norm["var"], 1)
            act.wait_ge(eps_set, 1)
            act.activation(std[:, :], mean_var[:, :, 1], ACT.Sqrt, bias=k.eps[:, 0:1]).then_inc(norm["std"], 1)
            act.wait_ge(wq_in, 32)
            act.activation(k.wq_hi[:, :, :, :], wq_raw[:, :, :, :], ACT.Copy).then_inc(wq_hi_s, 1)
            act.wait_ge(xnT_ps, 2)
            for i in range(2):
                last = act.activation(xnT[:, i * BANK:(i + 1) * BANK], pT[i][:, :], ACT.Copy)
            last.then_inc(xnT_ready, 1)
            act.wait_ge(xnT_ready, 1)
            act.activation(k.xnT_hi[:, :], xnT[:, :], ACT.Copy).then_inc(xnT_hi, 1)
            act.wait_ge(wkv_in, 32)
            act.activation(k.wkv_hi[:, :, :], wkv_raw[:, :, :], ACT.Copy).then_inc(wkv_hi_s, 1)
            act.wait_ge(wout_in, 32)
            act.activation(k.wout_hi[:, :, :], wout_raw[:, :, :], ACT.Copy).then_inc(wout_hi_s, 1)
            act.wait_ge(u_ps, 1)
            act.activation(k.u_hi[:, :], pU[:, :], ACT.Copy).then_inc(u_hi_s, 1)

        @block.gpsimd
        def _(pool):
            for i, eps in enumerate((1e-5, 1e-6, 1.0)):
                last = pool.memset(k.eps[:, i:i + 1], eps)
            last.then_inc(eps_set, 1)
            pool.memset(nv_diag[:, :, :], 0.0).then_inc(diag_zero, 1)
            pool.wait_ge(wq_hi_s, 1)
            pool.tensor_tensor(k.wq_lo[:, :, :, :], wq_raw[:, :, :, :], f(k.wq_hi[:, :, :, :]), ALU.subtract)
            pool.wait_ge(wout_hi_s, 1)
            pool.tensor_tensor(k.wout_lo[:, :, :], wout_raw[:, :, :], f(k.wout_hi[:, :, :]), ALU.subtract)

        @block.vector
        def _(dve):
            dve.wait_ge(x_in, 16)
            layer_stats(dve, norm, k.x, stats, mean_var)
            normalise(dve, norm, k.x, mean_var, std, rstd, xn).then_inc(xn_ready, 1)
            dve.wait_ge(null_in, 32)
            dve.wait_ge(diag_zero, 1)
            diagonal = nv_diag[:, :, :].rearrange("p a b -> p (a b)")[:, 0:H * H:H + 1]
            dve.tensor_copy(diagonal, nv_col[:, :].broadcast_to([DH, H])).then_inc(diag_set, 1)
            dve.wait_ge(wq_in, 32)
            dve.tensor_tensor(nk_wq[:, :, :], wq_raw[:, :, 0, :], nk_row[:, :].unsqueeze(1).broadcast_to([P, H, DH]),
                              ALU.mult).then_inc(w0_mul, 1)
            dve.wait_ge(w0_mul, 1)
            dve.tensor_reduce(w0[:, :], nk_wq[:, :, :], AX_X, ALU.add).then_inc(w0_ready, 1)
            dve.wait_ge(xnT_hi, 1)
            dve.tensor_tensor(k.xnT_lo[:, :], xnT[:, :], f(k.xnT_hi[:, :]), ALU.subtract)
            dve.wait_ge(s0_ps, 1)
            dve.tensor_scalar(k.s0n[:, :, :], pS0[:, :, :], -X_SCALE, None, ALU.mult)
            dve.wait_ge(wkv_hi_s, 1)
            dve.tensor_tensor(k.wkv_lo[:, :, :], wkv_raw[:, :, :], f(k.wkv_hi[:, :, :]), ALU.subtract)
            dve.wait_ge(u_hi_s, 1)
            dve.tensor_tensor(k.u_lo[:, :], pU[:, :], f(k.u_hi[:, :]), ALU.subtract)

        @block.tensor
        def _(pe):
            pe.wait_ge(xn_ready, 1)
            pe.wait_ge(const_in, 16)
            for t in range(TT):
                last = pe.transpose(pT[t // 4][:, (t % 4) * P:(t % 4 + 1) * P], xn[:, t, :], k.ident[:, :])
                if t % 4 == 3:
                    last.then_inc(xnT_ps, 1)
            pe.wait_ge(w0_ready, 1)
            pe.wait_ge(xnT_ready, 1)
            for t in range(TT):
                last = pe.matmul(pS0[:, t, :], xnT[:, t * P:(t + 1) * P], w0[:, :], start=True, stop=True)
            last.then_inc(s0_ps, 1)
            pe.wait_ge(diag_set, 1)
            pe.wait_ge(wout_in, 32)
            for h in range(H):
                last = pe.matmul(pU[:, :], nv_diag[:, h, :], wout_raw[0:DH, h, :], start=h == 0, stop=h == H - 1)
            last.then_inc(u_ps, 1)


def cross_attention(nc, k, dram):
    with ExitStack() as ctx:
        def sb(name, shape, dt=F32):
            return ctx.enter_context(nc.sbuf_tensor(name, shape, dt))

        def sem(name):
            return ctx.enter_context(nc.semaphore(name))

        def bank(name):
            return ctx.enter_context(nc.psum_tensor(name, [P, BANK], F32))

        ctx_raw = sb("ctx_raw", [P, KT, C])
        cT_hi, cT_lo = (sb(f"cT_{s}", [P, CT, M], F32R) for s in ("hi", "lo"))
        keys = sb("keys", [P, H, M], F32R)
        vals = sb("vals", [P, KT, H, 2 * DH], F32R)
        q_hi, q_lo = (sb(f"q_{s}", [P, 2, N], F32R) for s in ("hi", "lo"))
        neg_max, bias, d0, e0, row_sum, total, rinv = (
            sb(n, [P, H, QT]) for n in ("neg_max", "bias", "d0", "e0", "row_sum", "total", "rinv"))
        p0, p0_batch = sb("p0", [P, TT, H]), sb("p0_batch", [P, QT, H])
        p0T_hi, p0T_lo = (sb(f"p0T_{s}", [H, N], F32R) for s in ("hi", "lo"))
        p_raw = sb("p_raw", [P, 2, QT, M])
        p_norm = sb("p_norm", [P, 2, QT, M])
        pT_hi, pT_lo = (sb(f"pT_{s}", [P, 2, KT, N], F32R) for s in ("hi", "lo"))
        o_hi, o_lo = (sb(f"o_{s}", [P, 2, N], F32R) for s in ("hi", "lo"))

        banks = [bank(f"bank{i}") for i in range(8)]
        s_bank, t_bank, y_bank, proj_bank = banks[0:2], banks[2:4], banks[6], banks[7]
        q_bank, o_bank = banks[4][:, 0:N], banks[5][:, 0:N]

        ctx_in = sem("ctx_in")
        proj_ps, proj_hi, proj_lo = sem("proj_ps"), sem("proj_hi"), sem("proj_lo")
        q_ps, q_hi_s, q_lo_s = sem("q_ps"), sem("q_hi_s"), sem("q_lo_s")
        s_ps, max_s, bias_s, d0_s = (sem(n) for n in ("s_ps", "max_s", "bias_s", "d0_s"))
        p_exp, e0_s, total_s, rinv_s, p0_s, p0_batch_s, p_norm_s = (
            sem(n) for n in ("p_exp", "e0_s", "total_s", "rinv_s", "p0_s", "p0_batch_s", "p_norm_s"))
        t_ps, t_hi_s, t_lo_s = sem("t_ps"), sem("t_hi_s"), sem("t_lo_s")
        o_ps, o_hi_s, o_lo_s, wout_ps = sem("o_ps"), sem("o_hi_s"), sem("o_lo_s"), sem("wout_ps")
        p0_ps, p0_hi_s, p0_lo_s, y_ps, y_out = (sem(n) for n in ("p0_ps", "p0_hi_s", "p0_lo_s", "y_ps", "y_out"))

        FIRST, BODY = range(-4, 2), range(2, H + 2)
        UNITS = [("c", 0), ("c", 1), ("k", 0), ("v", 0, 0), ("v", 0, 1), ("k", 1), ("v", 0, 2), ("k", 2), ("v", 0, 3), ("k", 3),
                 ("k", 4), ("v", 1, 0), ("k", 5), ("v", 1, 1), ("k", 6), ("v", 1, 2), ("v", 1, 3), ("k", 7)]
        NU = len(UNITS)
        AT = {2: [10], 3: [11], 4: [12], 5: [13], 6: [14], 7: [15], 8: [16, 17], 9: [NU, NU + 1], 10: [NU + 2],
              11: [NU + 3], 12: [NU + 4], 13: [NU + 5], 14: [NU + 6], 15: [NU + 7], 16: [None, NU + 8], 17: [NU + 9]}
        FIRST_AT = {-4: [3, 4], -3: [5, 6], -2: [7, 8], -1: [9]}
        BEFORE = [0, 1, 2]

        def units(h, place, last_batch):
            at = (FIRST_AT if h < 2 else AT).get(h, [])[place:place + 1]
            return [u for u in at if u is not None and not (last_batch and u >= NU)]

        def unit_bank(u):
            return y_bank if u < 10 and u % 2 else proj_bank

        block = ctx.enter_context(nc.Block())

        @block.sync
        def _(sp):
            context = dram["ctx_2048"].rearrange("b (t p) c -> p b t c", p=P)
            sp.dma_start(ctx_raw[:, :, :], context[:, 0, :, :]).then_inc(ctx_in, 16)
            with sp.Fori(0, B - 1) as b:
                sp.wait_ge(proj_ps, b * NU + CT)
                sp.dma_start(ctx_raw[:, :, :], context[:, bass.ds(b + 1, 1), :, :].rearrange("p b t c -> p (b t) c")).then_inc(ctx_in, 16)

        @block.tensor
        def _(pe):
            def unit(b, u):
                out = unit_bank(u)
                if u >= 10:
                    pe.wait_ge(proj_lo, b * NU + u)
                    if u == NU + 8:
                        pe.wait_ge(p0_lo_s, b + 1)
                elif u >= 2:
                    pe.wait_ge(proj_lo, u if u == CT else u - 1)
                kind, i, *t = UNITS[u % NU]
                if kind == "c":
                    if i == 0:
                        pe.wait_ge(ctx_in, (b + u // NU + 1) * 16)
                    for t in range(KT):
                        last = pe.transpose(out[:, t * P:(t + 1) * P], ctx_raw[:, t, i * P:(i + 1) * P], k.ident[:, :])
                    last.then_inc(proj_ps, 1)
                    return
                n = 0
                for c in range(CT):
                    for x, w in ((cT_hi, k.wkv_hi), (cT_lo, k.wkv_hi), (cT_hi, k.wkv_lo)):
                        if kind == "k":
                            last = pe.matmul(out[:, :], w[:, c, i * P:(i + 1) * P], x[:, c, :], start=n == 0, stop=n == 3 * CT - 1)
                        else:
                            last = pe.matmul(out[:, :], x[:, c, t[0] * P:(t[0] + 1) * P],
                                             w[:, c, INNER + i * BANK:INNER + (i + 1) * BANK], start=n == 0, stop=n == 3 * CT - 1)
                        n += 1
                last.then_inc(proj_ps, 1)

            def project_q(b, h):
                if h >= 1:
                    pe.wait_ge(q_lo_s, b * H + h)
                for i, (w, x) in enumerate(((k.wq_hi, k.xnT_hi), (k.wq_hi, k.xnT_lo), (k.wq_lo, k.xnT_hi))):
                    last = pe.matmul(q_bank, w[:, h % H, :, :].rearrange("p a d -> p (a d)"),
                                     x[:, bass.ts(b + h // H, N)], start=i == 0, stop=i == 2)
                last.then_inc(q_ps, 1)

            def scores(b, h):
                pe.wait_ge(q_lo_s, b * H + h + 1)
                if h % 2 == 0:
                    pe.wait_ge(proj_lo, (b + h // H) * NU + UNITS.index(("k", h % H // 2)) + 1)
                for t in range(QT):
                    if h >= 1:
                        pe.wait_ge(p_exp, b * H * QT + QT * (h - 1) + t + 1)
                    for i, q in enumerate((q_hi, q_lo)):
                        last = pe.matmul(s_bank[t][:, :], q[:, h % 2, t * P:(t + 1) * P], keys[:, h % H, :],
                                         start=i == 0, stop=i == 1)
                    last.then_inc(s_ps, 1)

            def transpose_probs(b, h):
                pe.wait_ge(p_norm_s, b * H * QT + QT * (h + 1))
                for half in range(2):
                    g = 2 * h + half
                    if h >= 1:
                        pe.wait_ge(t_lo_s, b * 2 * H + g - 1)
                    for j in range(2):
                        for t in range(QT):
                            kt = 2 * half + j
                            last = pe.transpose(t_bank[half][:, j * N + t * P:j * N + (t + 1) * P],
                                                p_norm[:, h % 2, t, kt * P:(kt + 1) * P], k.ident[:, :])
                    last.then_inc(t_ps, 1)

            def weighted_values(b, h):
                pe.wait_ge(t_lo_s, b * 2 * H + 2 * h + 2)
                if h % (H // 2) == 0:
                    pe.wait_ge(proj_lo, (b + h // H) * NU + UNITS.index(("v", h % H // (H // 2), KT - 1)) + 1)
                if h >= 1:
                    pe.wait_ge(o_lo_s, b * H + h)
                for kt in range(KT):
                    for i, x in enumerate((pT_hi, pT_lo)):
                        last = pe.matmul(o_bank, vals[:, kt, h % H, :], x[:, h % 2, kt, :],
                                         start=kt == 0 and i == 0, stop=kt == KT - 1 and i == 1)
                last.then_inc(o_ps, 1)

            def project_out(b, h):
                pe.wait_ge(o_lo_s, b * H + h + 1)
                if h == 0:
                    pe.wait_ge(y_out, b + 1)
                for i, (w, x) in enumerate(((k.wout_hi, o_hi), (k.wout_hi, o_lo), (k.wout_lo, o_hi))):
                    last = pe.matmul(y_bank[:, 0:N], w[:, h, :], x[:, h % 2, :],
                                     start=h == 0 and i == 0, stop=False)
                last.then_inc(wout_ps, 1)

            def null_probs(b, last_batch):
                pe.wait_ge(p0_batch_s, b + 1)
                pe.wait_ge(proj_lo, (b + 1) * NU + (0 if last_batch else 8))
                for t in range(QT):
                    last = pe.transpose(proj_bank[0:H, t * P:(t + 1) * P], p0_batch[:, t, :], k.ident[:, :])
                last.then_inc(p0_ps, 1)

            def null_values(b):
                pe.wait_ge(p0_lo_s, b + 1)
                for i, (w, x) in enumerate(((k.u_hi, p0T_hi), (k.u_hi, p0T_lo), (k.u_lo, p0T_hi))):
                    last = pe.matmul(y_bank[:, 0:N], w[:, :], x[:, :], start=False, stop=i == 2)
                last.then_inc(y_ps, 1)

            def steps(b, which, last_batch=False):
                end = H if last_batch else which.stop + 4
                for h in which:
                    if 0 <= h < end:
                        transpose_probs(b, h)
                    if h == H:
                        null_probs(b, last_batch)
                    for u in units(h, 0, last_batch):
                        unit(b, u)
                    if 0 <= h - 1 < end:
                        weighted_values(b, h - 1)
                    if 0 <= h - 2 < end:
                        project_out(b, h - 2)
                    if h + 4 < end:
                        project_q(b, h + 4)
                    if 0 <= h + 3 < end:
                        scores(b, h + 3)
                    for u in units(h, 1, last_batch):
                        unit(b, u)
                    if h == H + 1:
                        null_values(b)

            for u in BEFORE:
                unit(0, u)
            steps(0, FIRST)
            with pe.Fori(0, B - 1) as b:
                steps(b, BODY)
            steps(B - 1, BODY, True)

        @block.scalar
        def _(act):
            def unit(b, u):
                src = unit_bank(u)
                kind, i, *t = UNITS[u % NU]
                act.wait_ge(proj_ps, b * NU + u + 1)
                if kind == "c":
                    last = act.activation(cT_hi[:, i, :], src[:, :], ACT.Copy)
                elif kind == "k":
                    act.activation(keys[0:DH, 2 * i, :], src[0:DH, :], ACT.Copy)
                    last = act.activation(keys[DH:P, 2 * i + 1, :], src[DH:P, :], ACT.Copy)
                else:
                    last = act.activation(vals[:, t[0], i * (H // 2):(i + 1) * (H // 2), 0:DH],
                                          src[:, :].rearrange("p (h d) -> p h d", d=DH), ACT.Copy)
                last.then_inc(proj_hi, 1)

            def q_head(b, h):
                act.wait_ge(q_ps, b * H + h + 1)
                if h >= 2:
                    act.wait_ge(s_ps, b * H * QT + QT * (h - 1))
                act.activation(q_hi[:, h % 2, :], q_bank, ACT.Copy).then_inc(q_hi_s, 1)

            def exponential(b, h, t):
                act.wait_ge(bias_s, b * H * QT + QT * h + t + 1)
                if h >= 2:
                    act.wait_ge(p_norm_s, b * H * QT + QT * (h - 2) + t + 1)
                act.activation(p_raw[:, h % 2, t, :], s_bank[t][:, :], ACT.Exp,
                               bias=bias[:, h % H, t:t + 1], scale=X_SCALE, accum_out=row_sum[:, h % H, t:t + 1]).then_inc(p_exp, 1)

            def null_exponential(b, h):
                act.wait_ge(d0_s, b * H + h + 1)
                act.activation(e0[:, h % H, :], d0[:, h % H, :], ACT.Exp).then_inc(e0_s, 1)

            def o_head(b, h):
                act.wait_ge(o_ps, b * H + h + 1)
                if h >= 2:
                    act.wait_ge(wout_ps, b * H + h - 1)
                act.activation(o_hi[:, h % 2, :], o_bank, ACT.Copy).then_inc(o_hi_s, 1)

            def probs_head(b, h, half):
                g = 2 * h + half
                act.wait_ge(t_ps, b * 2 * H + g + 1)
                if h >= 2:
                    act.wait_ge(o_ps, b * H + h - 1)
                act.activation(pT_hi[:, h % 2, 2 * half:2 * half + 2, :],
                               t_bank[half][:, :].rearrange("p (j n) -> p j n", j=2), ACT.Copy).then_inc(t_hi_s, 1)

            def steps(b, which, last_batch=False):
                end = H if last_batch else which.stop + 3
                for h in which:
                    if 0 <= h + 3 < end:
                        q_head(b, h + 3)
                    if 0 <= h < end:
                        probs_head(b, h, 0)
                        probs_head(b, h, 1)
                    if h == H:
                        act.wait_ge(p0_ps, b + 1)
                        act.activation(p0T_hi[:, :], proj_bank[0:H, 0:N], ACT.Copy).then_inc(p0_hi_s, 1)
                    for u in units(h, 0, last_batch):
                        unit(b, u)
                    if 0 <= h + 2 < end:
                        exponential(b, h + 2, 0)
                        exponential(b, h + 2, 1)
                        null_exponential(b, h + 2)
                    if 0 <= h - 1 < end:
                        o_head(b, h - 1)
                    for u in units(h, 1, last_batch):
                        unit(b, u)
                    if h == H + 1:
                        act.wait_ge(y_ps, b + 1)
                        act.activation(k.yT[:, bass.ts(b, N)], y_bank[:, 0:N], ACT.Copy).then_inc(y_out, 1)

            act.sem_inc(y_out, 1)
            for u in BEFORE:
                unit(0, u)
            steps(0, FIRST)
            with act.Fori(0, B - 1) as b:
                steps(b, BODY)
            steps(B - 1, BODY, True)

        @block.vector
        def _(dve):
            def unit(b, u):
                src = unit_bank(u)
                kind, i, *t = UNITS[u % NU]
                dve.wait_ge(proj_hi, b * NU + u + 1)
                if kind == "c":
                    last = dve.tensor_tensor(cT_lo[:, i, :], src[:, :], f(cT_hi[:, i, :]), ALU.subtract)
                elif kind == "k":
                    h = 2 * i
                    dve.tensor_tensor(keys[DH:P, h, :], src[0:DH, :], f(keys[0:DH, h, :]), ALU.subtract)
                    last = dve.tensor_tensor(keys[0:DH, h + 1, :], src[DH:P, :], f(keys[DH:P, h + 1, :]), ALU.subtract)
                else:
                    v = vals[:, t[0], i * (H // 2):(i + 1) * (H // 2), :]
                    last = dve.tensor_tensor(v[:, :, DH:2 * DH], src[:, :].rearrange("p (h d) -> p h d", d=DH),
                                             f(v[:, :, 0:DH]), ALU.subtract)
                last.then_inc(proj_lo, 1)

            def q_tail(b, h):
                dve.wait_ge(q_hi_s, b * H + h + 1)
                if h >= 2:
                    dve.wait_ge(s_ps, b * H * QT + QT * (h - 1))
                dve.tensor_tensor(q_lo[:, h % 2, :], q_bank, f(q_hi[:, h % 2, :]), ALU.subtract)\
                    .then_inc(q_lo_s, 1)

            def null_score(b, h, t, n=1):
                tiles = k.s0n[:, bass.ds((b + h // H) * QT + t, n), h % H:h % H + 1]
                return tiles.rearrange("p t h -> p (t h)")

            def maxima(b, h):
                at = b * H * QT + QT * h + 1
                for t in range(QT):
                    dve.wait_ge(s_ps, at + t)
                    dve.tensor_reduce(neg_max[:, h % H, t:t + 1], s_bank[t][:, :], AX_X, ALU.max, negate=True)\
                        .then_inc(max_s, 1)
                for t in range(QT):
                    dve.wait_ge(max_s, at + t)
                    dve.scalar_tensor_tensor(bias[:, h % H, t:t + 1], neg_max[:, h % H, t:t + 1], X_SCALE, null_score(b, h, t),
                                             ALU.mult, ALU.min).then_inc(bias_s, 1)

            def null_shift(b, h):
                dve.wait_ge(bias_s, b * H * QT + QT * (h + 1))
                dve.tensor_tensor(d0[:, h % H, :], bias[:, h % H, :], null_score(b, h, 0, QT), ALU.subtract).then_inc(d0_s, 1)

            def inverse_sum(b, h):
                dve.wait_ge(total_s, b * H + h + 1)
                dve.reciprocal(rinv[:, h % H, :], total[:, h % H, :]).then_inc(rinv_s, 1)

            def o_tail(b, h):
                dve.wait_ge(o_hi_s, b * H + h + 1)
                if h >= 2:
                    dve.wait_ge(wout_ps, b * H + h - 1)
                dve.tensor_tensor(o_lo[:, h % 2, :], o_bank, f(o_hi[:, h % 2, :]), ALU.subtract)\
                    .then_inc(o_lo_s, 1)

            def probs_tail(b, h, half):
                g = 2 * h + half
                dve.wait_ge(t_hi_s, b * 2 * H + g + 1)
                if h >= 2:
                    dve.wait_ge(o_ps, b * H + h - 1)
                dve.tensor_tensor(pT_lo[:, h % 2, 2 * half:2 * half + 2, :],
                                  t_bank[half][:, :].rearrange("p (j n) -> p j n", j=2),
                                  f(pT_hi[:, h % 2, 2 * half:2 * half + 2, :]), ALU.subtract).then_inc(t_lo_s, 1)

            def steps(b, which, last_batch=False):
                end = H if last_batch else which.stop + 3
                for h in which:
                    if 0 <= h + 2 < end:
                        maxima(b, h + 2)
                    if 0 <= h + 3 < end:
                        q_tail(b, h + 3)
                    if 0 <= h + 2 < end:
                        null_shift(b, h + 2)
                    if 0 <= h < end:
                        probs_tail(b, h, 0)
                        probs_tail(b, h, 1)
                    if h == H - 1:
                        dve.wait_ge(p0_s, (b + 1) * H)
                        dve.tensor_copy(p0_batch[:, :, :], p0[:, bass.ts(b, QT), :]).then_inc(p0_batch_s, 1)
                    if h == H:
                        dve.wait_ge(p0_hi_s, b + 1)
                        dve.tensor_tensor(p0T_lo[:, :], proj_bank[0:H, 0:N], f(p0T_hi[:, :]), ALU.subtract).then_inc(p0_lo_s, 1)
                    for u in units(h, 0, last_batch):
                        unit(b, u)
                    if 0 <= h + 2 < end:
                        inverse_sum(b, h + 2)
                    if 0 <= h - 1 < end:
                        o_tail(b, h - 1)
                    for u in units(h, 1, last_batch):
                        unit(b, u)

            for u in BEFORE:
                unit(0, u)
            steps(0, FIRST)
            with dve.Fori(0, B - 1) as b:
                steps(b, BODY)
            steps(B - 1, BODY, True)

        @block.gpsimd
        def _(pool):
            def normalise_probs(b, h):
                pool.wait_ge(p_exp, b * H * QT + QT * (h + 1))
                pool.wait_ge(e0_s, b * H + h + 1)
                pool.tensor_tensor(total[:, h % H, :], row_sum[:, h % H, :], e0[:, h % H, :], ALU.add).then_inc(total_s, 1)
                if h >= 2:
                    pool.wait_ge(t_ps, b * 2 * H + 2 * (h - 1))
                pool.wait_ge(rinv_s, b * H + h + 1)
                pool.tensor_tensor(p0[:, bass.ds((b + h // H) * QT, QT), h % H:h % H + 1].rearrange("p t h -> p (t h)"),
                                   e0[:, h % H, :], rinv[:, h % H, :], ALU.mult).then_inc(p0_s, 1)
                for t in range(QT):
                    pool.tensor_scalar(p_norm[:, h % 2, t, :], p_raw[:, h % 2, t, :], rinv[:, h % H, t:t + 1], 1.0,
                                       ALU.mult, ALU.mult).then_inc(p_norm_s, 1)

            for h in range(2):
                normalise_probs(0, h)
            with pool.Fori(0, B - 1) as b:
                for h in BODY:
                    normalise_probs(b, h)
            for h in range(2, H):
                normalise_probs(B - 1, h)


def stage_helpers(nc, ctx):
    def sb(name, shape, dt=F32):
        return ctx.enter_context(nc.sbuf_tensor(name, shape, dt))

    def sem(name):
        return ctx.enter_context(nc.semaphore(name))

    def bank(name, shape=(P, BANK)):
        return ctx.enter_context(nc.psum_tensor(name, list(shape), F32))

    return sb, sem, bank


def over_tiles(row, tiles=TT):
    return row[:, :].unsqueeze(1).broadcast_to([P, tiles, D])


def over_width(col, tiles=TT):
    return col[:, 0:tiles].unsqueeze(2).broadcast_to([P, tiles, D])


def residual_and_projections(nc, k, dram):
    with ExitStack() as ctx:
        sb, sem, bank = stage_helpers(nc, ctx)
        scale_row, bias_row, ln1_row = sb("scale_row", [P, D]), sb("bias_row", [P, D]), sb("ln1_row", [P, D])
        wqkv = sb("wqkv", [P, FH + 2 * KV, HD])
        cos, sin = sb("cos", [P, QT, HD]), sb("sin", [P, QT, HD])
        x_bias, yn, h, sq = (sb(n, [P, TT, D]) for n in ("x_bias", "yn", "h_rms", "sq"))
        hT = sb("hT", [P, TOK])
        stats, mean_var = sb("stats3", [P, TT, 6]), sb("mean_var3", [P, TT, 2])
        std, rstd = sb("std3", [P, TT]), sb("rstd3", [P, TT])
        sum_sq, rms, rrms = sb("sum_sq", [P, TT]), sb("rms", [P, TT]), sb("rrms", [P, TT])
        qkv = sb("qkv", [P, TT, FH + 2 * KV, HD])
        turned = sb("turned", [P, TT, FH + KV, HD])
        pY = [bank(f"p_y{i}", (P, 4, D)) for i in range(2)]
        pH = [bank(f"p_h{i}") for i in range(2)]
        pQ = [bank(f"p_qkv{i}", (P, 2, FH + 2 * KV, HD)) for i in range(4)]
        rows_in, w_in, rope_in = sem("rows_in"), sem("w_in"), sem("rope_in")
        x_bias_s, y_ps, y_var, y_std, x1_var, x1_std, sq_s, rms_s = (
            sem(n) for n in ("x_bias_s", "y_ps3", "y_var", "y_std", "x1_var", "x1_std", "sq_s", "rms_s"))
        h_s, hT_ps, hT_s, qkv_ps, qkv_s, step = (
            sem(n) for n in ("h_s", "hT_ps", "hT_s", "qkv_ps", "qkv_s", "dve_step3"))
        block = ctx.enter_context(nc.Block())

        @block.sync
        def _(sp):
            sp.dma_start(scale_row[:, :], dram["L0_xattn_ln_scale"].partition_broadcast(P)).then_inc(rows_in, 16)
            sp.dma_start(bias_row[:, :], dram["L0_xattn_ln_bias"].partition_broadcast(P)).then_inc(rows_in, 16)
            sp.dma_start(ln1_row[:, :], dram["L0_ffn_ln1_w"].partition_broadcast(P)).then_inc(rows_in, 16)
            at = 0
            for name, heads in (("L0_ffn_wq", FH), ("L0_ffn_wk", KV), ("L0_ffn_wv", KV)):
                sp.dma_start(wqkv[:, at:at + heads, :], dram[name].rearrange("c (h d) -> c h d", d=HD)).then_inc(w_in, 16)
                at += heads
            for table, name in ((cos, "rope_cos"), (sin, "rope_sin")):
                sp.dma_start(table[:, :, :], dram[name].rearrange("(t p) d -> p t d", p=P)).then_inc(rope_in, 16)

        @block.gpsimd
        def _(pool):
            pool.wait_ge(rows_in, 48)
            pool.tensor_tensor(x_bias[:, :, :], k.x[:, :, :], over_tiles(bias_row), ALU.add).then_inc(x_bias_s, 1)

        @block.scalar
        def _(act):
            act.wait_ge(y_var, 1)
            act.activation(std[:, :], mean_var[:, :, 1], ACT.Sqrt, bias=k.eps[:, 1:2]).then_inc(y_std, 1)
            act.wait_ge(x1_var, 1)
            act.activation(std[:, :], mean_var[:, :, 1], ACT.Sqrt, bias=k.eps[:, 0:1]).then_inc(x1_std, 1)
            act.wait_ge(sq_s, 1)
            act.activation(rms[:, :], sum_sq[:, :], ACT.Sqrt, bias=k.eps[:, 1:2], scale=1.0 / D).then_inc(rms_s, 1)
            for i in range(2):
                act.wait_ge(hT_ps, i + 1)
                act.activation(hT[:, i * BANK:(i + 1) * BANK], pH[i][:, :], ACT.Copy).then_inc(hT_s, 1)
            for i in range(4):
                act.wait_ge(qkv_ps, i + 1)
                act.activation(qkv[:, 2 * i:2 * i + 2, :, :], pQ[i][:, :, :, :], ACT.Copy).then_inc(qkv_s, 1)

        @block.tensor
        def _(pe):
            for t in range(TT):
                last = pe.transpose(pY[t // 4][:, t % 4, :], k.yT[:, t * P:(t + 1) * P], k.ident[:, :])
            last.then_inc(y_ps, 1)
            pe.wait_ge(h_s, 1)
            for t in range(TT):
                last = pe.transpose(pH[t // 4][:, (t % 4) * P:(t % 4 + 1) * P], h[:, t, :], k.ident[:, :])
                if t % 4 == 3:
                    last.then_inc(hT_ps, 1)
            pe.wait_ge(w_in, 48)
            for t in range(TT):
                if t % 4 == 0:
                    pe.wait_ge(hT_s, t // 4 + 1)
                last = pe.matmul(pQ[t // 2][:, t % 2, :, :], hT[:, t * P:(t + 1) * P], wqkv[:, :, :], start=True, stop=True)
                if t % 2:
                    last.then_inc(qkv_ps, 1)

        @block.vector
        def _(dve):
            count = [0]

            def link(ins):
                count[0] += 1
                ins.then_inc(step, 1)
                dve.wait_ge(step, count[0])

            def stats_of(tile):
                for t in range(TT):
                    last = dve.bn_stats(stats[:, t, :], tile(t))
                link(last)
                for t in range(TT):
                    last = dve.bn_aggr(mean_var[:, t, :], stats[:, t, :])
                return last

            def normalised(dst, tile):
                link(dve.reciprocal(rstd[:, :], std[:, :]))
                for t in range(TT):
                    last = dve.tensor_scalar(dst[:, t, :], tile(t), mean_var[:, t, 0:1], rstd[:, t:t + 1],
                                             ALU.subtract, ALU.mult)
                link(last)

            dve.wait_ge(y_ps, 1)
            stats_of(lambda t: pY[t // 4][:, t % 4, :]).then_inc(y_var, 1)
            dve.wait_ge(y_std, 1)
            normalised(yn, lambda t: pY[t // 4][:, t % 4, :])
            dve.wait_ge(rows_in, 48)
            link(dve.tensor_tensor(yn[:, :, :], yn[:, :, :], over_tiles(scale_row), ALU.mult))
            dve.wait_ge(x_bias_s, 1)
            link(dve.tensor_tensor(k.x1[:, :, :], yn[:, :, :], x_bias[:, :, :], ALU.add))
            stats_of(lambda t: k.x1[:, t, :]).then_inc(x1_var, 1)
            dve.wait_ge(x1_std, 1)
            normalised(k.z, lambda t: k.x1[:, t, :])
            link(dve.tensor_tensor(sq[:, :, :], k.z[:, :, :], k.z[:, :, :], ALU.mult))
            dve.tensor_reduce(sum_sq[:, :], sq[:, :, :], AX_X, ALU.add).then_inc(sq_s, 1)
            dve.wait_ge(rms_s, 1)
            link(dve.reciprocal(rrms[:, :], rms[:, :]))
            link(dve.tensor_tensor(sq[:, :, :], k.z[:, :, :], over_width(rrms), ALU.mult))
            dve.tensor_tensor(h[:, :, :], sq[:, :, :], over_tiles(ln1_row), ALU.mult).then_inc(h_s, 1)
            dve.wait_ge(qkv_s, 4)
            dve.wait_ge(rope_in, 32)
            NQK = FH + KV
            for par in range(QT):
                src, dst = qkv[:, par::QT, 0:NQK, :], turned[:, par::QT, :, :]
                sin_b = sin[:, par, :].unsqueeze(1).unsqueeze(1)
                for a, b in ((0, HD // 2), (HD // 2, 0)):
                    last = dve.tensor_tensor(dst[:, :, :, a:a + HD // 2], src[:, :, :, b:b + HD // 2],
                                             sin_b[:, :, :, a:a + HD // 2].broadcast_to([P, TT // QT, NQK, HD // 2]), ALU.mult)
            link(last)
            dve.tensor_copy(k.v[:, :, :, :], qkv[:, :, NQK:, :])
            for par in range(QT):
                cos_b = cos[:, par, :].unsqueeze(1).unsqueeze(1).broadcast_to([P, TT // QT, NQK, HD])
                src = qkv[:, par::QT, 0:NQK, :]
                last = dve.tensor_tensor(src, src, cos_b, ALU.mult)
            link(last)
            dve.tensor_tensor(k.rq[:, :, :, :], qkv[:, :, 0:FH, :], turned[:, :, 0:FH, :], ALU.add)
            link(dve.tensor_tensor(k.rk[:, :, :, :], qkv[:, :, FH:NQK, :], turned[:, :, FH:NQK, :], ALU.add))


def self_attention(nc, k, dram):
    with ExitStack() as ctx:
        sb, sem, bank = stage_helpers(nc, ctx)
        STACK = 4 * HD
        GROUPS = FH * STACK // P
        q_quad = sb("q_quad", [P, QT, FH, 4, HD], F32R)
        k_quad = sb("k_quad", [P, QT, FH, 4, HD], F32R)
        v_pair = sb("v_pair", [P, QT, KV, 2, HD], F32R)
        qT, kT = sb("qT", [P, GROUPS, N], F32R), sb("kT", [P, GROUPS, N], F32R)
        mask_f, mask = sb("mask_f", [P, BANK]), sb("mask", [P, BANK], BF16)
        ident_b = sb("ident_b", [P, P], BF16)
        neg_max, row_sum, rinv = sb("neg_max4", [P, FH, QT]), sb("row_sum4", [P, QT, FH]), sb("rinv4", [P, QT, FH])
        p_raw = sb("p_raw4", [P, 2, REP, QT, N])
        KEYS0, KEYS1 = REP * N, REP * P
        pT_hi, pT_lo = sb("pT_hi4", [P, 2, KEYS0 + KEYS1], F32R), sb("pT_lo4", [P, 2, KEYS0 + KEYS1], F32R)
        oT = sb("oT", [2 * HD, KV, REP, N])
        ao_sum = sb("ao_sum", [P, QT, FH, HD])
        banks = [bank(f"bank4_{i}") for i in range(8)]
        s_bank, a_bank, b_bank, o_bank = banks[0:4], banks[4:6], banks[6], banks[7]
        g_bank = a_bank[0]

        mask_in, consts_s = sem("mask_in"), sem("consts_s")
        quad_hi, quad_lo, qkT_ps, qT_s, kT_s, v_hi_s, v_lo_s = (
            sem(n) for n in ("quad_hi", "quad_lo", "qkT_ps", "qT_s", "kT_s", "v_hi_s4", "v_lo_s4"))
        s_ps, max_s, p_exp, t_ps, t_hi_s, t_lo_s, o_ps, o_s, g_ps, rinv_s, sum_s, ao_s = (
            sem(f"{n}4") for n in ("s_ps", "max_s", "p_exp", "t_ps", "t_hi_s", "t_lo_s", "o_ps", "o_s", "g_ps",
                                   "rinv_s", "sum_s", "ao_s"))
        block = ctx.enter_context(nc.Block())

        def keys1(ap):
            return ap.rearrange("p (j t n) -> p j t n", j=REP, t=QT)[:, :, 1, :]

        def key_slot(a):
            return k_quad[:, :, :, a, :].rearrange("p t (g r) d -> p (t g) r d", r=REP)

        def key_heads(b):
            return k.rk[:, bass.ts(b, QT), :, :].rearrange("p t g d -> p (t g) d").unsqueeze(2)\
                .broadcast_to([P, QT * KV, REP, HD])

        @block.sync
        def _(sp):
            sp.dma_start(mask_f[:, :], dram["causal"]).then_inc(mask_in, 16)
            fetch_pair(sp, k, dram, 0)

        @block.gpsimd
        def _(pool):
            split_pair(pool, k, 0, 0)

        @block.tensor
        def _(pe):
            def features_first(b, u):
                src = q_quad if u < 2 else k_quad
                pe.wait_ge(quad_lo, b + 1)
                for i in range(2):
                    g = 2 * (u % 2) + i
                    for t in range(QT):
                        last = pe.transpose(s_bank[u][:, i * N + t * P:i * N + (t + 1) * P],
                                            f(src[:, t, 4 * g:4 * g + 4, :, :]).rearrange("p h a d -> p (h a d)"),
                                            k.ident[:, :])
                last.then_inc(qkT_ps, 1)

            def scores(b, p):
                if p == 0:
                    pe.wait_ge(qT_s, b + 1)
                    pe.wait_ge(kT_s, b + 1)
                if p >= 2:
                    pe.wait_ge(p_exp, b * KV + p - 1)
                for j in range(REP):
                    r = STACK * ((REP * p + j) % 4)
                    out = s_bank[(p % 2) * REP + j]
                    for t in range(QT):
                        pe.matmul(out[:, t * N:(t + 1) * N], qT[r:r + STACK, p // 2, t * P:(t + 1) * P],
                                  kT[r:r + STACK, p // 2, :], start=t == 0, stop=False)
                for j in range(REP):
                    last = pe.matmul(s_bank[(p % 2) * REP + j][:, :], ident_b[:, :], mask[:, :], start=False, stop=True)
                last.then_inc(s_ps, 1)

            def transpose_probs(b, p):
                pe.wait_ge(p_exp, b * KV + p + 1)
                if p >= 2:
                    pe.wait_ge(t_lo_s, b * 2 * KV + 2 * (p - 1) - 1)
                for j in range(REP):
                    for t in range(QT):
                        last = pe.transpose(a_bank[p % 2][:, j * N + t * P:j * N + (t + 1) * P], p_raw[:, p % 2, j, t, 0:P],
                                            k.ident[:, :])
                last.then_inc(t_ps, 1)
                if p >= 1:
                    pe.wait_ge(t_lo_s, b * 2 * KV + 2 * p)
                for j in range(REP):
                    last = pe.transpose(b_bank[:, j * P:(j + 1) * P], p_raw[:, p % 2, j, 1, P:2 * P], k.ident[:, :])
                last.then_inc(t_ps, 1)

            def weighted_values(b, p):
                if p == 0:
                    pe.wait_ge(v_lo_s, b + 1)
                pe.wait_ge(t_lo_s, b * 2 * KV + 2 * p + 2)
                if p >= 1:
                    pe.wait_ge(o_s, b * KV + p)
                for i, x in enumerate((pT_hi, pT_lo)):
                    pe.matmul(o_bank[0:2 * HD, :], v_pair[:, 0, p, :, :].rearrange("p a d -> p (a d)"),
                              x[:, p % 2, 0:KEYS0], start=i == 0, stop=False)
                for i, x in enumerate((pT_hi, pT_lo)):
                    last = pe.matmul(keys1(o_bank[0:2 * HD, :]), v_pair[:, 1, p, :, :].rearrange("p a d -> p (a d)"),
                                     x[:, p % 2, KEYS0:], start=False, stop=i == 1)
                last.then_inc(o_ps, 1)

            def tokens_first(b):
                pe.wait_ge(o_s, (b + 1) * KV)
                for p in range(KV):
                    for j in range(REP):
                        for t in range(QT):
                            at = (t * FH + REP * p + j) * 2 * HD
                            tile = oT[:, p, j, t * P:(t + 1) * P]
                            if p + j + t == 0:
                                pe.matmul(g_bank[:, at:at + 2 * HD], tile, k.ident[0:2 * HD, 0:2 * HD], start=True, stop=True)
                            else:
                                last = pe.transpose(g_bank[:, at:at + 2 * HD], tile, k.ident[0:2 * HD, 0:2 * HD])
                last.then_inc(g_ps, 1)

            def batch(b, last_batch):
                for p in range(KV + 1):
                    if p < KV:
                        if p == 0:
                            pe.wait_ge(sum_s, b + 1)
                        transpose_probs(b, p)
                    if 0 <= p - 1:
                        weighted_values(b, p - 1)
                    if p + 2 < KV:
                        scores(b, p + 2)
                    elif p < KV and not last_batch:
                        pe.wait_ge(p_exp, b * KV + p + 1)
                        features_first(b + 1, 2 * (p + 2 - KV))
                        features_first(b + 1, 2 * (p + 2 - KV) + 1)
                if not last_batch:
                    scores(b + 1, 0)
                    scores(b + 1, 1)
                tokens_first(b)

            pe.wait_ge(consts_s, 2)
            for u in range(4):
                features_first(0, u)
            scores(0, 0)
            scores(0, 1)
            with pe.Fori(0, B - 1) as b:
                batch(b, False)
            batch(B - 1, True)

        @block.scalar
        def _(act):
            def quad_heads(b):
                for a in (0, 2):
                    act.activation(q_quad[:, :, :, a, :], k.rq[:, bass.ts(b, QT), :, :], ACT.Copy, scale=F_SCALE)
                for a in (0, 1):
                    last = act.activation(key_slot(a), key_heads(b), ACT.Copy)
                last.then_inc(quad_hi, 1)

            def value_heads(b):
                act.activation(v_pair[:, :, :, 0, :], k.v[:, bass.ts(b, QT), :, :], ACT.Copy).then_inc(v_hi_s, 1)

            def queries_first(b):
                for i in range(2):
                    act.wait_ge(qkT_ps, b * 4 + i + 1)
                    last = act.activation(qT[:, 2 * i:2 * i + 2, :], s_bank[i][:, :].rearrange("p (g n) -> p g n", g=2), ACT.Copy)
                last.then_inc(qT_s, 1)

            def exponentials(b, p):
                act.wait_ge(max_s, b * KV + p + 1)
                if p >= 2:
                    act.wait_ge(t_ps, b * 2 * KV + 2 * (p - 1))
                for j in range(REP):
                    for t in range(QT):
                        n = (t + 1) * P
                        last = act.activation(p_raw[:, p % 2, j, t, 0:n], s_bank[(p % 2) * REP + j][:, t * N:t * N + n], ACT.Exp,
                                              bias=neg_max[:, REP * p + j, t:t + 1],
                                              accum_out=row_sum[:, t, REP * p + j:REP * p + j + 1])
                last.then_inc(p_exp, 1)

            def probs_head(b, p):
                act.wait_ge(t_ps, b * 2 * KV + 2 * p + 1)
                if p >= 2:
                    act.wait_ge(o_ps, b * KV + p - 1)
                act.activation(pT_hi[:, p % 2, 0:KEYS0], a_bank[p % 2][:, :], ACT.Copy).then_inc(t_hi_s, 1)
                act.wait_ge(t_ps, b * 2 * KV + 2 * p + 2)
                act.activation(pT_hi[:, p % 2, KEYS0:], b_bank[:, 0:KEYS1], ACT.Copy).then_inc(t_hi_s, 1)

            def batch(b, last_batch):
                for p in range(KV + 1):
                    if p < KV:
                        probs_head(b, p)
                    if p + 1 < KV:
                        exponentials(b, p + 1)
                    if not last_batch:
                        if p == 2:
                            quad_heads(b + 1)
                        if p == KV - 1:
                            queries_first(b + 1)
                        if p == KV:
                            act.wait_ge(o_ps, (b + 1) * KV)
                            value_heads(b + 1)
                            act.wait_ge(rinv_s, b + 1)
                            exponentials(b + 1, 0)

            act.wait_ge(mask_in, 16)
            act.activation(mask[:, :], mask_f[:, :], ACT.Copy).then_inc(consts_s, 1)
            act.activation(ident_b[:, :], k.ident[:, :], ACT.Copy).then_inc(consts_s, 1)
            quad_heads(0)
            value_heads(0)
            queries_first(0)
            exponentials(0, 0)
            with act.Fori(0, B - 1) as b:
                batch(b, False)
            batch(B - 1, True)

        @block.vector
        def _(dve):
            def quad_tails(b):
                dve.wait_ge(quad_hi, b + 1)
                for a in (1, 3):
                    dve.scalar_tensor_tensor(q_quad[:, :, :, a, :].rearrange("p t h d -> p (t h) d"),
                                             k.rq[:, bass.ts(b, QT), :, :].rearrange("p t h d -> p (t h) d"), F_SCALE,
                                             f(q_quad[:, :, :, 0, :]).rearrange("p t h d -> p (t h) d"),
                                             ALU.mult, ALU.subtract)
                for a in (2, 3):
                    last = dve.tensor_tensor(key_slot(a), key_heads(b), f(key_slot(0)), ALU.subtract)
                last.then_inc(quad_lo, 1)

            def value_tails(b):
                dve.wait_ge(v_hi_s, b + 1)
                dve.tensor_tensor(v_pair[:, :, :, 1, :], k.v[:, bass.ts(b, QT), :, :], f(v_pair[:, :, :, 0, :]),
                                  ALU.subtract).then_inc(v_lo_s, 1)

            def keys_first(b):
                for i in range(2):
                    dve.wait_ge(qkT_ps, b * 4 + i + 3)
                    last = dve.tensor_copy(kT[:, 2 * i:2 * i + 2, :], s_bank[2 + i][:, :].rearrange("p (g n) -> p g n", g=2))
                last.then_inc(kT_s, 1)

            def maxima(b, p):
                dve.wait_ge(s_ps, b * KV + p + 1)
                for j in range(REP):
                    last = dve.tensor_reduce(neg_max[:, REP * p + j, :], s_bank[(p % 2) * REP + j][:, :].rearrange("p (t n) -> p t n", t=QT),
                                             AX_X, ALU.max, negate=True)
                last.then_inc(max_s, 1)

            def probs_tail(b, p):
                dve.wait_ge(t_hi_s, b * 2 * KV + 2 * p + 1)
                if p >= 2:
                    dve.wait_ge(o_ps, b * KV + p - 1)
                dve.tensor_tensor(pT_lo[:, p % 2, 0:KEYS0], a_bank[p % 2][:, :], f(pT_hi[:, p % 2, 0:KEYS0]), ALU.subtract)\
                    .then_inc(t_lo_s, 1)
                dve.wait_ge(t_hi_s, b * 2 * KV + 2 * p + 2)
                dve.tensor_tensor(pT_lo[:, p % 2, KEYS0:], b_bank[:, 0:KEYS1], f(pT_hi[:, p % 2, KEYS0:]), ALU.subtract)\
                    .then_inc(t_lo_s, 1)

            def output_copy(b, p):
                dve.wait_ge(o_ps, b * KV + p + 1)
                dve.tensor_copy(oT[:, p, :, :].rearrange("p j n -> p (j n)"), o_bank[0:2 * HD, :]).then_inc(o_s, 1)

            def attention_out(b):
                dve.wait_ge(g_ps, b + 1)
                dve.tensor_reduce(ao_sum[:, :, :, :].rearrange("p t h d -> p (t h) d"),
                                  g_bank[:, :].rearrange("p (g a d) -> p g d a", a=2, d=HD), AX_X, ALU.add).then_inc(sum_s, 1)
                dve.wait_ge(sum_s, b + 2)
                dve.tensor_tensor(k.ao[:, bass.ts(b, QT), :, :].rearrange("p t h d -> p (t h) d"),
                                  ao_sum[:, :, :, :].rearrange("p t h d -> p (t h) d"),
                                  rinv[:, :, :].rearrange("p t h -> p (t h)").unsqueeze(2).broadcast_to([P, QT * FH, HD]),
                                  ALU.mult).then_inc(ao_s, 1)
                dve.wait_ge(ao_s, b + 1)

            def batch(b, last_batch):
                for p in range(KV + 1):
                    if p + 1 < KV:
                        maxima(b, p + 1)
                    if p < KV:
                        probs_tail(b, p)
                    if 0 <= p - 1:
                        output_copy(b, p - 1)
                    if p == 2 and not last_batch:
                        quad_tails(b + 1)
                dve.wait_ge(p_exp, (b + 1) * KV)
                dve.reciprocal(rinv[:, :, :], row_sum[:, :, :]).then_inc(rinv_s, 1)
                dve.wait_ge(rinv_s, b + 1)
                if not last_batch:
                    keys_first(b + 1)
                    value_tails(b + 1)
                    maxima(b + 1, 0)
                attention_out(b)

            dve.sem_inc(sum_s, 1)
            quad_tails(0)
            value_tails(0)
            keys_first(0)
            maxima(0, 0)
            with dve.Fori(0, B - 1) as b:
                batch(b, False)
            batch(B - 1, True)


def route(nc, k, dram):
    with ExitStack() as ctx:
        sb, sem, bank = stage_helpers(nc, ctx)
        wo, router, ln2_row, iota = sb("wo", [P, D]), sb("router", [P, E]), sb("ln2_row", [P, D]), sb("iota", [P, E])
        aoT, h2T = sb("aoT", [P, TOK]), sb("h2T", [P, TOK])
        sq, h2 = sb("sq5", [P, TT, D]), sb("h2", [P, TT, D])
        sum_sq, rms, rrms = sb("sum_sq5", [P, TT]), sb("rms5", [P, TT]), sb("rrms5", [P, TT])
        logits, expd, probs, pick, pick2 = (sb(n, [P, TT, E]) for n in ("logits", "expd", "probs", "pick", "pick2"))
        top, top_at, top_at_f = sb("top", [P, TT, 8]), sb("top_at", [P, TT, 8], U32), sb("top_at_f", [P, TT, 2])
        lmax, lsum, lrec, tsum, trec = (sb(n, [P, TT]) for n in ("lmax", "lsum", "lrec", "tsum", "trec"))
        topn = sb("topn", [P, TT, 2])
        pT = [bank(f"p_aoT{i}") for i in range(2)]
        pA = [bank(f"p_att{i}", (P, 4, D)) for i in range(2)]
        pH = [bank(f"p_h2T{i}") for i in range(2)]
        pL = bank("p_logits", (P, TT, E))
        w_in, aoT_ps, aoT_s, att_ps, x2_s, sq_s, rms_s, h2_s, h2T_ps, h2T_s, h2T_hi_s, logit_ps, shifted_s, exp_s, step = (
            sem(f"{n}5") for n in ("w_in", "aoT_ps", "aoT_s", "att_ps", "x2_s", "sq_s", "rms_s", "h2_s", "h2T_ps", "h2T_s",
                                   "h2T_hi_s", "logit_ps", "shifted_s", "exp_s", "step"))
        block = ctx.enter_context(nc.Block())

        @block.sync
        def _(sp):
            sp.dma_start(wo[:, :], dram["L0_ffn_wo"]).then_inc(w_in, 16)
            sp.dma_start(router[:, :], dram["L0_ffn_router_w"]).then_inc(w_in, 16)
            sp.dma_start(ln2_row[:, :], dram["L0_ffn_ln2_w"].partition_broadcast(P)).then_inc(w_in, 16)
            sp.dma_start(iota[:, :], dram["expert_ids"].partition_broadcast(P)).then_inc(w_in, 16)

        @block.tensor
        def _(pe):
            for t in range(TT):
                last = pe.transpose(pT[t // 4][:, (t % 4) * P:(t % 4 + 1) * P],
                                    k.ao[:, t, :, :].rearrange("p h d -> p (h d)"), k.ident[:, :])
            last.then_inc(aoT_ps, 1)
            pe.wait_ge(w_in, 64)
            pe.wait_ge(aoT_s, 1)
            for t in range(TT):
                last = pe.matmul(pA[t // 4][:, t % 4, :], aoT[:, t * P:(t + 1) * P], wo[:, :], start=True, stop=True)
            last.then_inc(att_ps, 1)
            pe.wait_ge(h2_s, 1)
            for t in range(TT):
                last = pe.transpose(pH[t // 4][:, (t % 4) * P:(t % 4 + 1) * P], h2[:, t, :], k.ident[:, :])
            last.then_inc(h2T_ps, 1)
            pe.wait_ge(h2T_s, 1)
            for t in range(TT):
                last = pe.matmul(pL[:, t, :], h2T[:, t * P:(t + 1) * P], router[:, :], start=True, stop=True)
            last.then_inc(logit_ps, 1)

        @block.scalar
        def _(act):
            act.wait_ge(aoT_ps, 1)
            for i in range(2):
                last = act.activation(aoT[:, i * BANK:(i + 1) * BANK], pT[i][:, :], ACT.Copy)
            last.then_inc(aoT_s, 1)
            act.wait_ge(sq_s, 1)
            act.activation(rms[:, :], sum_sq[:, :], ACT.Sqrt, bias=k.eps[:, 1:2], scale=1.0 / D).then_inc(rms_s, 1)
            act.wait_ge(h2T_ps, 1)
            for i in range(2):
                last = act.activation(h2T[:, i * BANK:(i + 1) * BANK], pH[i][:, :], ACT.Copy)
            last.then_inc(h2T_s, 1)
            for i in range(2):
                last = act.activation(k.h2T_hi[:, i * BANK:(i + 1) * BANK], pH[i][:, :], ACT.Copy)
            last.then_inc(h2T_hi_s, 1)
            act.wait_ge(shifted_s, 1)
            act.activation(expd[:, :, :], logits[:, :, :], ACT.Exp).then_inc(exp_s, 1)

        @block.vector
        def _(dve):
            count = [0]

            def link(ins):
                count[0] += 1
                ins.then_inc(step, 1)
                dve.wait_ge(step, count[0])

            dve.wait_ge(att_ps, 1)
            for i in range(2):
                last = dve.tensor_tensor(k.x2[:, 4 * i:4 * i + 4, :], k.z[:, 4 * i:4 * i + 4, :], pA[i][:, :, :], ALU.add)
            last.then_inc(x2_s, 1)
            dve.wait_ge(x2_s, 1)
            link(dve.tensor_tensor(sq[:, :, :], k.x2[:, :, :], k.x2[:, :, :], ALU.mult))
            dve.tensor_reduce(sum_sq[:, :], sq[:, :, :], AX_X, ALU.add).then_inc(sq_s, 1)
            dve.wait_ge(rms_s, 1)
            link(dve.reciprocal(rrms[:, :], rms[:, :]))
            link(dve.tensor_tensor(sq[:, :, :], k.x2[:, :, :], over_width(rrms), ALU.mult))
            dve.wait_ge(w_in, 64)
            dve.tensor_tensor(h2[:, :, :], sq[:, :, :], over_tiles(ln2_row), ALU.mult).then_inc(h2_s, 1)
            dve.wait_ge(h2T_hi_s, 1)
            for i in range(2):
                dve.tensor_tensor(k.h2T_lo[:, i * BANK:(i + 1) * BANK], pH[i][:, :], f(k.h2T_hi[:, i * BANK:(i + 1) * BANK]), ALU.subtract)

            def wide(col, n=E):
                return col.unsqueeze(2).broadcast_to([P, TT, n])

            dve.wait_ge(logit_ps, 1)
            link(dve.tensor_reduce(lmax[:, :], pL[:, :, :], AX_X, ALU.max))
            dve.tensor_tensor(logits[:, :, :], pL[:, :, :], wide(lmax[:, :]), ALU.subtract).then_inc(shifted_s, 1)
            dve.wait_ge(exp_s, 1)
            link(dve.tensor_reduce(lsum[:, :], expd[:, :, :], AX_X, ALU.add))
            link(dve.reciprocal(lrec[:, :], lsum[:, :]))
            link(dve.tensor_tensor(probs[:, :, :], expd[:, :, :], wide(lrec[:, :]), ALU.mult))
            for t in range(TT):
                last = dve.max(top[:, t, :], probs[:, t, :])
            link(last)
            for t in range(TT):
                last = dve.max_index(top_at[:, t, :], top[:, t, :], probs[:, t, :])
            link(last)
            dve.tensor_copy(top_at_f[:, :, :], top_at[:, :, 0:2])
            link(dve.tensor_tensor(tsum[:, :], top[:, :, 0], top[:, :, 1], ALU.add))
            link(dve.reciprocal(trec[:, :], tsum[:, :]))
            link(dve.tensor_tensor(topn[:, :, :], top[:, :, 0:2], wide(trec[:, :], 2), ALU.mult))
            ids = iota[:, :].unsqueeze(1).broadcast_to([P, TT, E])
            for i, one in enumerate((pick, pick2)):
                link(dve.tensor_tensor(one[:, :, :], ids, wide(top_at_f[:, :, i]), ALU.is_equal))
                link(dve.tensor_tensor(one[:, :, :], one[:, :, :], wide(topn[:, :, i]), ALU.mult))
            link(dve.tensor_tensor(k.weights[:, :, :], pick[:, :, :], pick2[:, :, :], ALU.add))


def fetch_pair(sp, k, dram, g):
    for which, name in enumerate(("L0_ffn_w_gate", "L0_ffn_w_up")):
        sp.dma_start(k.gu_raw[:, which, :, :], dram[name][bass.ds(2 * g, 2), :, :].rearrange("e d m -> d e m"))\
            .then_inc(k.raw_in, 16)
    rows = dram["L0_ffn_w_down"].rearrange("(g e) m d -> g (e m) d", e=2)
    sp.dma_start(k.dn_raw[:, :, :], rows[bass.ds(g, 1), :, :].rearrange("g (s r) d -> r (g s) d", r=P)).then_inc(k.raw_in, 16)


def split_pair(pool, k, g, slot, free=None):
    pool.wait_ge(k.raw_in, (g + 1) * 48)
    if free is not None:
        pool.wait_ge(*free)
    pool.tensor_tensor(k.dn_hi[:, slot, :, :], k.dn_raw[:, :, :], k.eps[:, 2:3].unsqueeze(2).broadcast_to([P, SLABS, D]),
                       ALU.mult)
    pool.tensor_scalar(k.gu_hi[:, slot, :, :], k.gu_raw[:, :, :, :].rearrange("p a e m -> p a (e m)"), 1.0, 1.0,
                       ALU.mult, ALU.mult).then_inc(k.hi_made, 1)
    pool.wait_ge(k.hi_made, g + 1)
    pool.tensor_tensor(k.gu_lo[:, slot, :, :], k.gu_raw[:, :, :, :].rearrange("p a e m -> p a (e m)"),
                       f(k.gu_hi[:, slot, :, :]), ALU.subtract)
    pool.tensor_tensor(k.dn_lo[:, slot, :, :], k.dn_raw[:, :, :], f(k.dn_hi[:, slot, :, :]), ALU.subtract)\
        .then_inc(k.split_s, 1)


def experts(nc, k, dram, out):
    with ExitStack() as ctx:
        sb, sem, bank = stage_helpers(nc, ctx)
        wcol = sb("wcol", [P, E, TT])
        wide = sb("wide", [P, E, TOK])
        up_w = sb("up_w", [P, 2, BANK])
        gate = sb("gate", [P, 2, BANK])
        act_f = sb("act_f", [P, 2, BANK])
        act_hi, act_lo = sb("act_hi", [P, 2, BANK], F32R), sb("act_lo", [P, 2, BANK], F32R)
        sumT, res = sb("sumT", [P, TOK]), sb("res", [P, TT, D])
        g_bank, u_bank = ([bank(f"{n}_bank{i}") for i in range(3)] for n in "gu")
        d_bank = [bank(f"d_bank{i}") for i in range(2)]
        w_bank = g_bank + u_bank
        wcol_s, w_ps, w_s, w_s2, sum_ps, out_ps, out_s = (
            sem(n) for n in ("wcol_s", "w_ps", "w_s", "w_s2", "sum_ps", "out_ps", "out_s"))
        sumT_s, res_s = ([sem(f"{n}{c}") for c in range(CH)] for n in ("sumT_s", "res_s"))
        gu_ps, silu_s, weighed_s, mul_s, a_hi_s, a_lo_s, down_ps = (
            sem(n) for n in ("gu_ps", "silu_s", "weighed_s", "mul_s", "a_hi_s", "a_lo_s", "down_ps"))
        U = CH * SLABS
        ROWS = E * CH
        block = ctx.enter_context(nc.Block())

        def where(n):
            return n // U, (n % U) // SLABS, n % SLABS

        @block.sync
        def _(sp):
            with sp.Fori(1, PAIRS) as g:
                sp.wait_ge(k.split_s, g)
                fetch_pair(sp, k, dram, g)
            for c in range(CH):
                sp.wait_ge(res_s[c], 1)
                sp.dma_start(in_tiles(out)[:, 4 * c:4 * c + 4, :], res[:, 4 * c:4 * c + 4, :]).then_inc(out_s, 16)
            sp.wait_ge(out_s, CH * 16)

        @block.gpsimd
        def _(pool):
            split_pair(pool, k, 1, 1)
            with pool.Fori(1, PAIRS // 2) as g:
                for slot in range(2):
                    split_pair(pool, k, g * 2 + slot, slot, (down_ps, (g * 2 + slot - 1) * U))

        @block.tensor
        def _(pe):
            def weight_row(r):
                e, c = divmod(r, CH)
                if r >= len(w_bank):
                    pe.wait_ge(*((w_s, (r - 6) // 2 + 1) if r % 2 == 0 else (w_s2, (r - 6) // 2 + 1)))
                for t in range(4):
                    last = pe.transpose(w_bank[r % 6][:, t * P:(t + 1) * P],
                                        wcol[:, e, 4 * c + t:4 * c + t + 1].broadcast_to([P, P]), k.ident[:, :])
                last.then_inc(w_ps, 1)

            def residual(c, x, first):
                for t in range(4):
                    last = pe.matmul(d_bank[c][:, t * P:(t + 1) * P], x[:, 4 * c + t, :], k.ident[:, :],
                                     start=first and t == 0, stop=not first and t == 3)
                return last

            for c in range(CH):
                residual(c, k.x2, True)
            pe.wait_ge(wcol_s, 1)
            for r in range(ROWS):
                weight_row(r)
            pe.wait_ge(w_s, ROWS // 2)
            pe.wait_ge(w_s2, ROWS // 2)
            with pe.Fori(0, PAIRS // 2) as g:
                def gate_up(n):
                    slot, c, s = where(n)
                    if n >= 3:
                        pe.wait_ge(silu_s, g * 2 * U + n - 2)
                        pe.wait_ge(weighed_s, g * 2 * U + n - 2)
                    for which, out in ((0, g_bank[n % 3]), (1, u_bank[n % 3])):
                        for m, (w, x) in enumerate(((k.gu_hi, k.h2T_hi), (k.gu_hi, k.h2T_lo), (k.gu_lo, k.h2T_hi))):
                            last = pe.matmul(out[:, :], w[:, slot, which, s * P:(s + 1) * P],
                                             x[:, c * BANK:(c + 1) * BANK], start=m == 0, stop=m == 2)
                    last.then_inc(gu_ps, 1)

                def down(n):
                    slot, c, s = where(n)
                    pe.wait_ge(a_lo_s, g * 2 * U + n + 1)
                    for m, (w, x) in enumerate(((k.dn_hi, act_hi), (k.dn_hi, act_lo), (k.dn_lo, act_hi))):
                        last = pe.matmul(d_bank[c][:, :], w[:, slot, s, :], x[:, n % 2, :], start=False, stop=False)
                    last.then_inc(down_ps, 1)

                for n in range(2 * U + 2):
                    if n < 2 * U:
                        if n % U == 0:
                            pe.wait_ge(k.split_s, g * 2 + n // U + 1)
                        gate_up(n)
                    if n >= 2:
                        down(n - 2)
            for c in range(CH):
                residual(c, k.x1, False).then_inc(sum_ps, 1)
            for c in range(CH):
                pe.wait_ge(sumT_s[c], 1)
                for t in range(4):
                    last = pe.transpose(g_bank[c][:, t * P:(t + 1) * P], sumT[:, c * BANK + t * P:c * BANK + (t + 1) * P],
                                        k.ident[:, :])
                last.then_inc(out_ps, 1)

        @block.scalar
        def _(act):
            for r in range(0, ROWS, 2):
                e, c = divmod(r, CH)
                act.wait_ge(w_ps, r + 1)
                act.activation(wide[:, e, c * BANK:(c + 1) * BANK], w_bank[r % 6][:, :], ACT.Copy).then_inc(w_s, 1)
            with act.Fori(0, PAIRS // 2) as g:
                def silu(n):
                    act.wait_ge(gu_ps, g * 2 * U + n + 1)
                    if n >= 2:
                        act.wait_ge(mul_s, g * 2 * U + n - 1)
                    act.activation(gate[:, n % 2, :], g_bank[n % 3][:, :], ACT.Silu).then_inc(silu_s, 1)

                def head(n):
                    act.wait_ge(mul_s, g * 2 * U + n + 1)
                    if n >= 2:
                        act.wait_ge(down_ps, g * 2 * U + n - 1)
                    act.activation(act_hi[:, n % 2, :], act_f[:, n % 2, :], ACT.Copy).then_inc(a_hi_s, 1)

                for n in range(2 * U + 1):
                    if n >= 1:
                        head(n - 1)
                    if n < 2 * U:
                        silu(n)
            act.wait_ge(sum_ps, 1)
            act.activation(sumT[:, 0:BANK], d_bank[0][:, :], ACT.Copy).then_inc(sumT_s[0], 1)
            act.wait_ge(out_ps, 1)
            act.activation(res[:, 0:4, :], g_bank[0][:, :].rearrange("p (t d) -> p t d", t=4), ACT.Copy).then_inc(res_s[0], 1)

        @block.vector
        def _(dve):
            dve.tensor_copy(wcol[:, :, :], k.weights[:, :, :].rearrange("p t e -> p e t")).then_inc(wcol_s, 1)
            for r in range(1, ROWS, 2):
                e, c = divmod(r, CH)
                dve.wait_ge(w_ps, r + 1)
                dve.tensor_copy(wide[:, e, c * BANK:(c + 1) * BANK], w_bank[r % 6][:, :]).then_inc(w_s2, 1)
            dve.wait_ge(w_s, ROWS // 2)
            dve.wait_ge(w_s2, ROWS // 2)
            with dve.Fori(0, PAIRS // 2) as g:
                def weigh(n):
                    slot, c, s = where(n)
                    dve.wait_ge(gu_ps, g * 2 * U + n + 1)
                    if n >= 2:
                        dve.wait_ge(mul_s, g * 2 * U + n - 1)
                    first = min(max(HID - s * P, 0), P)
                    for i, rows in ((0, slice(0, first)), (1, slice(first, P))):
                        if rows.stop > rows.start:
                            w = wide[rows, bass.ds(g * 4 + slot * 2 + i, 1), c * BANK:(c + 1) * BANK]
                            last = dve.tensor_tensor(up_w[rows, n % 2, :], u_bank[n % 3][rows, :],
                                                     w.rearrange("p e n -> p (e n)"), ALU.mult)
                    last.then_inc(weighed_s, 1)

                def product(n):
                    if n >= 2:
                        dve.wait_ge(a_lo_s, g * 2 * U + n - 1)
                    dve.wait_ge(silu_s, g * 2 * U + n + 1)
                    dve.wait_ge(weighed_s, g * 2 * U + n + 1)
                    dve.tensor_tensor(act_f[:, n % 2, :], up_w[:, n % 2, :], gate[:, n % 2, :], ALU.mult).then_inc(mul_s, 1)

                def tail(n):
                    dve.wait_ge(a_hi_s, g * 2 * U + n + 1)
                    dve.tensor_tensor(act_lo[:, n % 2, :], act_f[:, n % 2, :], f(act_hi[:, n % 2, :]), ALU.subtract).then_inc(a_lo_s, 1)

                for n in range(2 * U + 1):
                    if n < 2 * U:
                        weigh(n)
                    if n >= 1:
                        tail(n - 1)
                    if n < 2 * U:
                        product(n)
            dve.wait_ge(sum_ps, 2)
            dve.tensor_copy(sumT[:, BANK:TOK], d_bank[1][:, :]).then_inc(sumT_s[1], 1)
            dve.wait_ge(out_ps, 2)
            dve.tensor_copy(res[:, 4:8, :], g_bank[1][:, :].rearrange("p (t d) -> p t d", t=4)).then_inc(res_s[1], 1)


def build(nc, dram, out):
    k = Kernel()
    with ExitStack() as ctx:
        def sb(name, shape, dt=F32):
            return ctx.enter_context(nc.sbuf_tensor(name, shape, dt))

        k.x, k.ident, k.eps = sb("x", [P, TT, D]), sb("ident", [P, P]), sb("eps", [P, 3])
        k.yT = sb("yT", [P, TOK])
        with ExitStack() as own:
            def sw(name, shape, dt=F32R):
                return own.enter_context(nc.sbuf_tensor(name, shape, dt))

            k.wq_hi, k.wq_lo = (sw(f"wq_{s}", [P, H, 2, DH]) for s in ("hi", "lo"))
            k.wkv_hi, k.wkv_lo = (sw(f"wkv_{s}", [P, CT, 2 * INNER]) for s in ("hi", "lo"))
            k.wout_hi, k.wout_lo = (sw(f"wout_{s}", [P, H, D]) for s in ("hi", "lo"))
            k.xnT_hi, k.xnT_lo = (sw(f"xnT_{s}", [P, TOK]) for s in ("hi", "lo"))
            k.u_hi, k.u_lo = (sw(f"u_{s}", [H, D]) for s in ("hi", "lo"))
            k.s0n = sw("s0n", [P, TT, H], F32)
            load_and_split(nc, k, dram)
            cross_attention(nc, k, dram)
        k.x1, k.x2, k.z = (sb(n, [P, TT, D]) for n in ("x1", "x2", "z"))
        k.rq, k.rk, k.v = sb("rq", [P, TT, FH, HD]), sb("rk", [P, TT, KV, HD]), sb("v", [P, TT, KV, HD])
        k.ao = sb("ao", [P, TT, FH, HD])
        k.h2T_hi, k.h2T_lo = sb("h2T_hi", [P, TOK], F32R), sb("h2T_lo", [P, TOK], F32R)
        k.weights = sb("weights", [P, TT, E])
        k.gu_raw, k.dn_raw = sb("gu_raw", [P, 2, 2, HID]), sb("dn_raw", [P, SLABS, D])
        k.gu_hi, k.gu_lo = (sb(f"gu_{s}", [P, 2, 2, 2 * HID], F32R) for s in ("hi", "lo"))
        k.dn_hi, k.dn_lo = (sb(f"dn_{s}", [P, 2, SLABS, D], F32R) for s in ("hi", "lo"))
        k.raw_in, k.hi_made, k.split_s = (ctx.enter_context(nc.semaphore(n)) for n in ("raw_in", "hi_made", "split_s"))
        residual_and_projections(nc, k, dram)
        self_attention(nc, k, dram)
        route(nc, k, dram)
        experts(nc, k, dram, out)


def shape_constants():
    import numpy as np

    angle = np.arange(N, dtype=np.float32)[:, None] * (1.0 / 10000.0 ** (np.arange(0, HD, 2, dtype=np.float32) / HD)).astype(np.float32)
    cos, sin = np.cos(angle), np.sin(angle)
    hidden = np.triu(np.full((P, P), MASKED, np.float32), 1)
    none, every = np.zeros((P, P), np.float32), np.full((P, P), MASKED, np.float32)
    return {
        "identity": np.eye(P, dtype=np.float32),
        "rope_cos": np.concatenate([cos, cos], -1).astype(np.float32),
        "rope_sin": np.concatenate([-sin, sin], -1).astype(np.float32),
        "causal": np.concatenate([hidden, every, none, hidden], -1),
        "expert_ids": np.arange(E, dtype=np.float32),
    }


def kernel(**inputs):
    import numpy as np
    import concourse.bacc as bacc
    from concourse.bass_utils import run_bass_kernel_spmd

    nc = bacc.Bacc("TRN2", target_bir_lowering=False, num_devices=1)
    arrays = {name: np.ascontiguousarray(a) for name, a in {**inputs, **shape_constants()}.items()}
    dram = {name: nc.dram_tensor(f"in_{name}", a.shape, mybir.dt.from_np(a.dtype), kind="ExternalInput").ap()
            for name, a in arrays.items()}
    out = nc.dram_tensor("out", (B, N, D), F32, kind="ExternalOutput").ap()
    build(nc, dram, out)
    r = run_bass_kernel_spmd(nc, [{f"in_{name}": a for name, a in arrays.items()}], core_ids=[0])
    return r.results[0]["out"]
```

```python
from contextlib import ExitStack

import concourse.bass as bass
from concourse import mybir

F32 = mybir.dt.float32
F32R = mybir.dt.float32r
BF16 = mybir.dt.bfloat16
U32 = mybir.dt.uint32
ALU = mybir.AluOpType
ACT = mybir.ActivationFunctionType
AX_X = mybir.AxisListType.X

P = 128
BANK = 512

B, N, D = 4, 256, 128
TOK = B * N
TT = TOK // P
QT = N // P
M, C = 512, 256
KT = M // P
CT = C // P
H, DH = 16, 64
INNER = H * DH
X_SCALE = DH ** -0.5
PROJ = 5

FH, KV, HD = 16, 8, 8
REP = FH // KV
F_SCALE = float(HD) ** -0.5
E, HID = 8, 448
PAIRS = E // 2
SLABS = 2 * HID // P
CH = TOK // BANK
MASKED = -1e30


def f(ap):
    return ap.bitcast(F32)


def in_tiles(dram):
    return dram.rearrange("b (t p) d -> p (b t) d", p=P)


class Kernel:
    pass


def layer_stats(dve, sems, src, stats, mean_var, tiles=TT):
    for t in range(tiles):
        last = dve.bn_stats(stats[:, t, :], src[:, t, :])
    last.then_inc(sems["stats"], 1)
    dve.wait_ge(sems["stats"], 1)
    for t in range(tiles):
        last = dve.bn_aggr(mean_var[:, t, :], stats[:, t, :])
    last.then_inc(sems["var"], 1)


def normalise(dve, sems, src, mean_var, std, rstd, dst, tiles=TT):
    dve.wait_ge(sems["std"], 1)
    dve.reciprocal(rstd[:, 0:tiles], std[:, 0:tiles]).then_inc(sems["rstd"], 1)
    dve.wait_ge(sems["rstd"], 1)
    for t in range(tiles):
        last = dve.tensor_scalar(dst[:, t, :], src[:, t, :], mean_var[:, t, 0:1], rstd[:, t:t + 1],
                                 ALU.subtract, ALU.mult)
    return last


def norm_sems(sem, name):
    return {k: sem(f"{name}_{k}") for k in ("stats", "var", "std", "rstd")}


def load_and_split(nc, k, dram):
    with ExitStack() as ctx:
        def sb(name, shape, dt=F32):
            return ctx.enter_context(nc.sbuf_tensor(name, shape, dt))

        def sem(name):
            return ctx.enter_context(nc.semaphore(name))

        wq_raw = sb("wq_raw", [P, H, 2, DH])
        wkv_raw = sb("wkv_raw", [P, CT, 2 * INNER])
        wout_raw = sb("wout_raw", [P, H, D])
        nk_row = sb("nk_row", [P, DH])
        nv_col = sb("nv_col", [DH, 1])
        nv_diag = sb("nv_diag", [DH, H, H])
        nk_wq = sb("nk_wq", [P, H, DH])
        w0 = sb("w0", [P, H])
        xn = sb("xn", [P, TT, D])
        xnT = sb("xnT", [P, TOK])
        stats = sb("stats1", [P, TT, 6])
        mean_var = sb("mean_var1", [P, TT, 2])
        std, rstd = sb("std1", [P, TT]), sb("rstd1", [P, TT])
        pT = [ctx.enter_context(nc.psum_tensor(f"p_xnT{i}", [P, BANK], F32)) for i in range(2)]
        pS0 = ctx.enter_context(nc.psum_tensor("p_s0", [P, TT, H], F32))
        pU = ctx.enter_context(nc.psum_tensor("p_u", [H, D], F32))

        x_in, wq_in, wkv_in = sem("x_in"), sem("wq_in"), sem("wkv_in")
        wout_in, null_in, const_in = sem("wout_in"), sem("null_in"), sem("const_in")
        eps_set, diag_zero, diag_set = sem("eps_set"), sem("diag_zero"), sem("diag_set")
        norm = norm_sems(sem, "ln1")
        xn_ready, xnT_ps, xnT_ready, xnT_hi = sem("xn_ready"), sem("xnT_ps"), sem("xnT_ready"), sem("xnT_hi_s")
        w0_mul, w0_ready, s0_ps, u_ps, u_hi_s = sem("w0_mul"), sem("w0_ready"), sem("s0_ps"), sem("u_ps"), sem("u_hi_s")
        wq_hi_s, wkv_hi_s, wout_hi_s = sem("wq_hi_s"), sem("wkv_hi_s"), sem("wout_hi_s")

        block = ctx.enter_context(nc.Block())

        @block.sync
        def _(sp):
            sp.dma_start(k.x[:, :, :], in_tiles(dram["x"])).then_inc(x_in, 16)
            sp.dma_start(k.ident[:, :], dram["identity"]).then_inc(const_in, 16)
            for c in range(CT):
                sp.dma_start(wkv_raw[:, c, :], dram["L0_xattn_Wkv"][c * P:(c + 1) * P, :]).then_inc(wkv_in, 16)
            for half in range(2):
                sp.dma_start(wout_raw[half * DH:(half + 1) * DH, :, :],
                             dram["L0_xattn_Wout"].rearrange("(h r) d -> r h d", h=H)).then_inc(wout_in, 16)

        @block.scalar
        def _(act):
            act.dma_start(nk_row[:, :], dram["L0_xattn_null_kv"][0, :].partition_broadcast(P)).then_inc(null_in, 16)
            act.dma_start(nv_col[:, :], dram["L0_xattn_null_kv"][1, :].rearrange("(d o) -> d o", o=1)).then_inc(null_in, 16)
            for half in range(2):
                act.dma_start(wq_raw[:, :, half, :],
                              dram["L0_xattn_Wq"].rearrange("c (h d) -> c h d", h=H)).then_inc(wq_in, 16)
            act.wait_ge(norm["var"], 1)
            act.wait_ge(eps_set, 1)
            act.activation(std[:, :], mean_var[:, :, 1], ACT.Sqrt, bias=k.eps[:, 0:1]).then_inc(norm["std"], 1)
            act.wait_ge(wq_in, 32)
            act.activation(k.wq_hi[:, :, :, :], wq_raw[:, :, :, :], ACT.Copy).then_inc(wq_hi_s, 1)
            act.wait_ge(xnT_ps, 2)
            for i in range(2):
                last = act.activation(xnT[:, i * BANK:(i + 1) * BANK], pT[i][:, :], ACT.Copy)
            last.then_inc(xnT_ready, 1)
            act.wait_ge(xnT_ready, 1)
            act.activation(k.xnT_hi[:, :], xnT[:, :], ACT.Copy).then_inc(xnT_hi, 1)
            act.wait_ge(wkv_in, 32)
            act.activation(k.wkv_hi[:, :, :], wkv_raw[:, :, :], ACT.Copy).then_inc(wkv_hi_s, 1)
            act.wait_ge(wout_in, 32)
            act.activation(k.wout_hi[:, :, :], wout_raw[:, :, :], ACT.Copy).then_inc(wout_hi_s, 1)
            act.wait_ge(u_ps, 1)
            act.activation(k.u_hi[:, :], pU[:, :], ACT.Copy).then_inc(u_hi_s, 1)

        @block.gpsimd
        def _(pool):
            for i, eps in enumerate((1e-5, 1e-6, 1.0)):
                last = pool.memset(k.eps[:, i:i + 1], eps)
            last.then_inc(eps_set, 1)
            pool.memset(nv_diag[:, :, :], 0.0).then_inc(diag_zero, 1)
            pool.wait_ge(wq_hi_s, 1)
            pool.tensor_tensor(k.wq_lo[:, :, :, :], wq_raw[:, :, :, :], f(k.wq_hi[:, :, :, :]), ALU.subtract)
            pool.wait_ge(wout_hi_s, 1)
            pool.tensor_tensor(k.wout_lo[:, :, :], wout_raw[:, :, :], f(k.wout_hi[:, :, :]), ALU.subtract)

        @block.vector
        def _(dve):
            dve.wait_ge(x_in, 16)
            layer_stats(dve, norm, k.x, stats, mean_var)
            normalise(dve, norm, k.x, mean_var, std, rstd, xn).then_inc(xn_ready, 1)
            dve.wait_ge(null_in, 32)
            dve.wait_ge(diag_zero, 1)
            diagonal = nv_diag[:, :, :].rearrange("p a b -> p (a b)")[:, 0:H * H:H + 1]
            dve.tensor_copy(diagonal, nv_col[:, :].broadcast_to([DH, H])).then_inc(diag_set, 1)
            dve.wait_ge(wq_in, 32)
            dve.tensor_tensor(nk_wq[:, :, :], wq_raw[:, :, 0, :], nk_row[:, :].unsqueeze(1).broadcast_to([P, H, DH]),
                              ALU.mult).then_inc(w0_mul, 1)
            dve.wait_ge(w0_mul, 1)
            dve.tensor_reduce(w0[:, :], nk_wq[:, :, :], AX_X, ALU.add).then_inc(w0_ready, 1)
            dve.wait_ge(xnT_hi, 1)
            dve.tensor_tensor(k.xnT_lo[:, :], xnT[:, :], f(k.xnT_hi[:, :]), ALU.subtract)
            dve.wait_ge(s0_ps, 1)
            dve.tensor_scalar(k.s0n[:, :, :], pS0[:, :, :], -X_SCALE, None, ALU.mult)
            dve.wait_ge(wkv_hi_s, 1)
            dve.tensor_tensor(k.wkv_lo[:, :, :], wkv_raw[:, :, :], f(k.wkv_hi[:, :, :]), ALU.subtract)
            dve.wait_ge(u_hi_s, 1)
            dve.tensor_tensor(k.u_lo[:, :], pU[:, :], f(k.u_hi[:, :]), ALU.subtract)

        @block.tensor
        def _(pe):
            pe.wait_ge(xn_ready, 1)
            pe.wait_ge(const_in, 16)
            for t in range(TT):
                last = pe.transpose(pT[t // 4][:, (t % 4) * P:(t % 4 + 1) * P], xn[:, t, :], k.ident[:, :])
                if t % 4 == 3:
                    last.then_inc(xnT_ps, 1)
            pe.wait_ge(w0_ready, 1)
            pe.wait_ge(xnT_ready, 1)
            for t in range(TT):
                last = pe.matmul(pS0[:, t, :], xnT[:, t * P:(t + 1) * P], w0[:, :], start=True, stop=True)
            last.then_inc(s0_ps, 1)
            pe.wait_ge(diag_set, 1)
            pe.wait_ge(wout_in, 32)
            for h in range(H):
                last = pe.matmul(pU[:, :], nv_diag[:, h, :], wout_raw[0:DH, h, :], start=h == 0, stop=h == H - 1)
            last.then_inc(u_ps, 1)


def cross_attention(nc, k, dram):
    with ExitStack() as ctx:
        def sb(name, shape, dt=F32):
            return ctx.enter_context(nc.sbuf_tensor(name, shape, dt))

        def sem(name):
            return ctx.enter_context(nc.semaphore(name))

        def bank(name):
            return ctx.enter_context(nc.psum_tensor(name, [P, BANK], F32))

        ctx_raw = sb("ctx_raw", [P, KT, C])
        cT_hi, cT_lo = (sb(f"cT_{s}", [P, CT, M], F32R) for s in ("hi", "lo"))
        keys = sb("keys", [P, H, M], F32R)
        vals = sb("vals", [P, KT, H, 2 * DH], F32R)
        q_hi, q_lo = (sb(f"q_{s}", [P, 2, N], F32R) for s in ("hi", "lo"))
        neg_max, bias, d0, e0, row_sum, total, rinv = (
            sb(n, [P, H, QT]) for n in ("neg_max", "bias", "d0", "e0", "row_sum", "total", "rinv"))
        p0, p0_batch = sb("p0", [P, TT, H]), sb("p0_batch", [P, QT, H])
        p0T_hi, p0T_lo = (sb(f"p0T_{s}", [H, N], F32R) for s in ("hi", "lo"))
        p_raw = sb("p_raw", [P, 2, QT, M])
        p_norm = sb("p_norm", [P, 2, QT, M])
        pT_hi, pT_lo = (sb(f"pT_{s}", [P, 2, KT, N], F32R) for s in ("hi", "lo"))
        o_hi, o_lo = (sb(f"o_{s}", [P, 2, N], F32R) for s in ("hi", "lo"))

        banks = [bank(f"bank{i}") for i in range(8)]
        s_bank, t_bank, y_bank, proj_bank = banks[0:2], banks[2:4], banks[6], banks[7]
        q_bank, o_bank = banks[4][:, 0:N], banks[5][:, 0:N]

        ctx_in = sem("ctx_in")
        proj_ps, proj_hi, proj_lo = sem("proj_ps"), sem("proj_hi"), sem("proj_lo")
        q_ps, q_hi_s, q_lo_s = sem("q_ps"), sem("q_hi_s"), sem("q_lo_s")
        s_ps, max_s, bias_s, d0_s = (sem(n) for n in ("s_ps", "max_s", "bias_s", "d0_s"))
        p_exp, e0_s, total_s, rinv_s, p0_s, p0_batch_s, p_norm_s = (
            sem(n) for n in ("p_exp", "e0_s", "total_s", "rinv_s", "p0_s", "p0_batch_s", "p_norm_s"))
        t_ps, t_hi_s, t_lo_s = sem("t_ps"), sem("t_hi_s"), sem("t_lo_s")
        o_ps, o_hi_s, o_lo_s, wout_ps = sem("o_ps"), sem("o_hi_s"), sem("o_lo_s"), sem("wout_ps")
        p0_ps, p0_hi_s, p0_lo_s, y_ps, y_out = (sem(n) for n in ("p0_ps", "p0_hi_s", "p0_lo_s", "y_ps", "y_out"))

        FIRST, BODY = range(-4, 2), range(2, H + 2)
        UNITS = [("c", 0), ("c", 1), ("k", 0), ("v", 0, 0), ("v", 0, 1), ("k", 1), ("v", 0, 2), ("k", 2), ("v", 0, 3), ("k", 3),
                 ("k", 4), ("v", 1, 0), ("k", 5), ("v", 1, 1), ("k", 6), ("v", 1, 2), ("v", 1, 3), ("k", 7)]
        NU = len(UNITS)
        AT = {2: [10], 3: [11], 4: [12], 5: [13], 6: [14], 7: [15], 8: [16, 17], 9: [NU, NU + 1], 10: [NU + 2],
              11: [NU + 3], 12: [NU + 4], 13: [NU + 5], 14: [NU + 6], 15: [NU + 7], 16: [None, NU + 8], 17: [NU + 9]}
        FIRST_AT = {-4: [3, 4], -3: [5, 6], -2: [7, 8], -1: [9]}
        BEFORE = [0, 1, 2]

        def units(h, place, last_batch):
            at = (FIRST_AT if h < 2 else AT).get(h, [])[place:place + 1]
            return [u for u in at if u is not None and not (last_batch and u >= NU)]

        def unit_bank(u):
            return y_bank if u < 10 and u % 2 else proj_bank

        block = ctx.enter_context(nc.Block())

        @block.sync
        def _(sp):
            context = dram["ctx_2048"].rearrange("b (t p) c -> p b t c", p=P)
            sp.dma_start(ctx_raw[:, :, :], context[:, 0, :, :]).then_inc(ctx_in, 16)
            with sp.Fori(0, B - 1) as b:
                sp.wait_ge(proj_ps, b * NU + CT)
                sp.dma_start(ctx_raw[:, :, :], context[:, bass.ds(b + 1, 1), :, :].rearrange("p b t c -> p (b t) c")).then_inc(ctx_in, 16)

        @block.tensor
        def _(pe):
            def unit(b, u):
                out = unit_bank(u)
                if u >= 10:
                    pe.wait_ge(proj_lo, b * NU + u)
                    if u == NU + 8:
                        pe.wait_ge(p0_lo_s, b + 1)
                elif u >= 2:
                    pe.wait_ge(proj_lo, u if u == CT else u - 1)
                kind, i, *t = UNITS[u % NU]
                if kind == "c":
                    if i == 0:
                        pe.wait_ge(ctx_in, (b + u // NU + 1) * 16)
                    for t in range(KT):
                        last = pe.transpose(out[:, t * P:(t + 1) * P], ctx_raw[:, t, i * P:(i + 1) * P], k.ident[:, :])
                    last.then_inc(proj_ps, 1)
                    return
                n = 0
                for c in range(CT):
                    for x, w in ((cT_hi, k.wkv_hi), (cT_lo, k.wkv_hi), (cT_hi, k.wkv_lo)):
                        if kind == "k":
                            last = pe.matmul(out[:, :], w[:, c, i * P:(i + 1) * P], x[:, c, :], start=n == 0, stop=n == 3 * CT - 1)
                        else:
                            last = pe.matmul(out[:, :], x[:, c, t[0] * P:(t[0] + 1) * P],
                                             w[:, c, INNER + i * BANK:INNER + (i + 1) * BANK], start=n == 0, stop=n == 3 * CT - 1)
                        n += 1
                last.then_inc(proj_ps, 1)

            def project_q(b, h):
                if h >= 1:
                    pe.wait_ge(q_lo_s, b * H + h)
                for i, (w, x) in enumerate(((k.wq_hi, k.xnT_hi), (k.wq_hi, k.xnT_lo), (k.wq_lo, k.xnT_hi))):
                    last = pe.matmul(q_bank, w[:, h % H, :, :].rearrange("p a d -> p (a d)"),
                                     x[:, bass.ts(b + h // H, N)], start=i == 0, stop=i == 2)
                last.then_inc(q_ps, 1)

            def scores(b, h):
                pe.wait_ge(q_lo_s, b * H + h + 1)
                if h % 2 == 0:
                    pe.wait_ge(proj_lo, (b + h // H) * NU + UNITS.index(("k", h % H // 2)) + 1)
                for t in range(QT):
                    if h >= 1:
                        pe.wait_ge(p_exp, b * H * QT + QT * (h - 1) + t + 1)
                    for i, q in enumerate((q_hi, q_lo)):
                        last = pe.matmul(s_bank[t][:, :], q[:, h % 2, t * P:(t + 1) * P], keys[:, h % H, :],
                                         start=i == 0, stop=i == 1)
                    last.then_inc(s_ps, 1)

            def transpose_probs(b, h):
                pe.wait_ge(p_norm_s, b * H * QT + QT * (h + 1))
                for half in range(2):
                    g = 2 * h + half
                    if h >= 1:
                        pe.wait_ge(t_lo_s, b * 2 * H + g - 1)
                    for j in range(2):
                        for t in range(QT):
                            kt = 2 * half + j
                            last = pe.transpose(t_bank[half][:, j * N + t * P:j * N + (t + 1) * P],
                                                p_norm[:, h % 2, t, kt * P:(kt + 1) * P], k.ident[:, :])
                    last.then_inc(t_ps, 1)

            def weighted_values(b, h):
                pe.wait_ge(t_lo_s, b * 2 * H + 2 * h + 2)
                if h % (H // 2) == 0:
                    pe.wait_ge(proj_lo, (b + h // H) * NU + UNITS.index(("v", h % H // (H // 2), KT - 1)) + 1)
                if h >= 1:
                    pe.wait_ge(o_lo_s, b * H + h)
                for kt in range(KT):
                    for i, x in enumerate((pT_hi, pT_lo)):
                        last = pe.matmul(o_bank, vals[:, kt, h % H, :], x[:, h % 2, kt, :],
                                         start=kt == 0 and i == 0, stop=kt == KT - 1 and i == 1)
                last.then_inc(o_ps, 1)

            def project_out(b, h):
                pe.wait_ge(o_lo_s, b * H + h + 1)
                if h == 0:
                    pe.wait_ge(y_out, b + 1)
                for i, (w, x) in enumerate(((k.wout_hi, o_hi), (k.wout_hi, o_lo), (k.wout_lo, o_hi))):
                    last = pe.matmul(y_bank[:, 0:N], w[:, h, :], x[:, h % 2, :],
                                     start=h == 0 and i == 0, stop=False)
                last.then_inc(wout_ps, 1)

            def null_probs(b, last_batch):
                pe.wait_ge(p0_batch_s, b + 1)
                pe.wait_ge(proj_lo, (b + 1) * NU + (0 if last_batch else 8))
                for t in range(QT):
                    last = pe.transpose(proj_bank[0:H, t * P:(t + 1) * P], p0_batch[:, t, :], k.ident[:, :])
                last.then_inc(p0_ps, 1)

            def null_values(b):
                pe.wait_ge(p0_lo_s, b + 1)
                for i, (w, x) in enumerate(((k.u_hi, p0T_hi), (k.u_hi, p0T_lo), (k.u_lo, p0T_hi))):
                    last = pe.matmul(y_bank[:, 0:N], w[:, :], x[:, :], start=False, stop=i == 2)
                last.then_inc(y_ps, 1)

            def steps(b, which, last_batch=False):
                end = H if last_batch else which.stop + 4
                for h in which:
                    if 0 <= h < end:
                        transpose_probs(b, h)
                    if h == H:
                        null_probs(b, last_batch)
                    for u in units(h, 0, last_batch):
                        unit(b, u)
                    if 0 <= h - 1 < end:
                        weighted_values(b, h - 1)
                    if 0 <= h - 2 < end:
                        project_out(b, h - 2)
                    if h + 4 < end:
                        project_q(b, h + 4)
                    if 0 <= h + 3 < end:
                        scores(b, h + 3)
                    for u in units(h, 1, last_batch):
                        unit(b, u)
                    if h == H + 1:
                        null_values(b)

            for u in BEFORE:
                unit(0, u)
            steps(0, FIRST)
            with pe.Fori(0, B - 1) as b:
                steps(b, BODY)
            steps(B - 1, BODY, True)

        @block.scalar
        def _(act):
            def unit(b, u):
                src = unit_bank(u)
                kind, i, *t = UNITS[u % NU]
                act.wait_ge(proj_ps, b * NU + u + 1)
                if kind == "c":
                    last = act.activation(cT_hi[:, i, :], src[:, :], ACT.Copy)
                elif kind == "k":
                    act.activation(keys[0:DH, 2 * i, :], src[0:DH, :], ACT.Copy)
                    last = act.activation(keys[DH:P, 2 * i + 1, :], src[DH:P, :], ACT.Copy)
                else:
                    last = act.activation(vals[:, t[0], i * (H // 2):(i + 1) * (H // 2), 0:DH],
                                          src[:, :].rearrange("p (h d) -> p h d", d=DH), ACT.Copy)
                last.then_inc(proj_hi, 1)

            def q_head(b, h):
                act.wait_ge(q_ps, b * H + h + 1)
                if h >= 2:
                    act.wait_ge(s_ps, b * H * QT + QT * (h - 1))
                act.activation(q_hi[:, h % 2, :], q_bank, ACT.Copy).then_inc(q_hi_s, 1)

            def exponential(b, h, t):
                act.wait_ge(bias_s, b * H * QT + QT * h + t + 1)
                if h >= 2:
                    act.wait_ge(p_norm_s, b * H * QT + QT * (h - 2) + t + 1)
                act.activation(p_raw[:, h % 2, t, :], s_bank[t][:, :], ACT.Exp,
                               bias=bias[:, h % H, t:t + 1], scale=X_SCALE, accum_out=row_sum[:, h % H, t:t + 1]).then_inc(p_exp, 1)

            def null_exponential(b, h):
                act.wait_ge(d0_s, b * H + h + 1)
                act.activation(e0[:, h % H, :], d0[:, h % H, :], ACT.Exp).then_inc(e0_s, 1)

            def o_head(b, h):
                act.wait_ge(o_ps, b * H + h + 1)
                if h >= 2:
                    act.wait_ge(wout_ps, b * H + h - 1)
                act.activation(o_hi[:, h % 2, :], o_bank, ACT.Copy).then_inc(o_hi_s, 1)

            def probs_head(b, h, half):
                g = 2 * h + half
                act.wait_ge(t_ps, b * 2 * H + g + 1)
                if h >= 2:
                    act.wait_ge(o_ps, b * H + h - 1)
                act.activation(pT_hi[:, h % 2, 2 * half:2 * half + 2, :],
                               t_bank[half][:, :].rearrange("p (j n) -> p j n", j=2), ACT.Copy).then_inc(t_hi_s, 1)

            def steps(b, which, last_batch=False):
                end = H if last_batch else which.stop + 3
                for h in which:
                    if 0 <= h + 3 < end:
                        q_head(b, h + 3)
                    if 0 <= h < end:
                        probs_head(b, h, 0)
                        probs_head(b, h, 1)
                    if h == H:
                        act.wait_ge(p0_ps, b + 1)
                        act.activation(p0T_hi[:, :], proj_bank[0:H, 0:N], ACT.Copy).then_inc(p0_hi_s, 1)
                    if 0 <= h + 2 < end:
                        exponential(b, h + 2, 0)
                        exponential(b, h + 2, 1)
                    for u in units(h, 0, last_batch):
                        unit(b, u)
                    if 0 <= h + 2 < end:
                        null_exponential(b, h + 2)
                    if 0 <= h - 1 < end:
                        o_head(b, h - 1)
                    for u in units(h, 1, last_batch):
                        unit(b, u)
                    if h == H + 1:
                        act.wait_ge(y_ps, b + 1)
                        act.activation(k.yT[:, bass.ts(b, N)], y_bank[:, 0:N], ACT.Copy).then_inc(y_out, 1)

            act.sem_inc(y_out, 1)
            for u in BEFORE:
                unit(0, u)
            steps(0, FIRST)
            with act.Fori(0, B - 1) as b:
                steps(b, BODY)
            steps(B - 1, BODY, True)

        @block.vector
        def _(dve):
            def unit(b, u):
                src = unit_bank(u)
                kind, i, *t = UNITS[u % NU]
                dve.wait_ge(proj_hi, b * NU + u + 1)
                if kind == "c":
                    last = dve.tensor_tensor(cT_lo[:, i, :], src[:, :], f(cT_hi[:, i, :]), ALU.subtract)
                elif kind == "k":
                    h = 2 * i
                    dve.tensor_tensor(keys[DH:P, h, :], src[0:DH, :], f(keys[0:DH, h, :]), ALU.subtract)
                    last = dve.tensor_tensor(keys[0:DH, h + 1, :], src[DH:P, :], f(keys[DH:P, h + 1, :]), ALU.subtract)
                else:
                    v = vals[:, t[0], i * (H // 2):(i + 1) * (H // 2), :]
                    last = dve.tensor_tensor(v[:, :, DH:2 * DH], src[:, :].rearrange("p (h d) -> p h d", d=DH),
                                             f(v[:, :, 0:DH]), ALU.subtract)
                last.then_inc(proj_lo, 1)

            def q_tail(b, h):
                dve.wait_ge(q_hi_s, b * H + h + 1)
                if h >= 2:
                    dve.wait_ge(s_ps, b * H * QT + QT * (h - 1))
                dve.tensor_tensor(q_lo[:, h % 2, :], q_bank, f(q_hi[:, h % 2, :]), ALU.subtract)\
                    .then_inc(q_lo_s, 1)

            def null_score(b, h, t, n=1):
                tiles = k.s0n[:, bass.ds((b + h // H) * QT + t, n), h % H:h % H + 1]
                return tiles.rearrange("p t h -> p (t h)")

            def maxima(b, h):
                at = b * H * QT + QT * h + 1
                for t in range(QT):
                    dve.wait_ge(s_ps, at + t)
                    dve.tensor_reduce(neg_max[:, h % H, t:t + 1], s_bank[t][:, :], AX_X, ALU.max, negate=True)\
                        .then_inc(max_s, 1)
                for t in range(QT):
                    dve.wait_ge(max_s, at + t)
                    dve.scalar_tensor_tensor(bias[:, h % H, t:t + 1], neg_max[:, h % H, t:t + 1], X_SCALE, null_score(b, h, t),
                                             ALU.mult, ALU.min).then_inc(bias_s, 1)

            def null_shift(b, h):
                dve.wait_ge(bias_s, b * H * QT + QT * (h + 1))
                dve.tensor_tensor(d0[:, h % H, :], bias[:, h % H, :], null_score(b, h, 0, QT), ALU.subtract).then_inc(d0_s, 1)

            def inverse_sum(b, h):
                dve.wait_ge(total_s, b * H + h + 1)
                dve.reciprocal(rinv[:, h % H, :], total[:, h % H, :]).then_inc(rinv_s, 1)

            def o_tail(b, h):
                dve.wait_ge(o_hi_s, b * H + h + 1)
                if h >= 2:
                    dve.wait_ge(wout_ps, b * H + h - 1)
                dve.tensor_tensor(o_lo[:, h % 2, :], o_bank, f(o_hi[:, h % 2, :]), ALU.subtract)\
                    .then_inc(o_lo_s, 1)

            def probs_tail(b, h, half):
                g = 2 * h + half
                dve.wait_ge(t_hi_s, b * 2 * H + g + 1)
                if h >= 2:
                    dve.wait_ge(o_ps, b * H + h - 1)
                dve.tensor_tensor(pT_lo[:, h % 2, 2 * half:2 * half + 2, :],
                                  t_bank[half][:, :].rearrange("p (j n) -> p j n", j=2),
                                  f(pT_hi[:, h % 2, 2 * half:2 * half + 2, :]), ALU.subtract).then_inc(t_lo_s, 1)

            def steps(b, which, last_batch=False):
                end = H if last_batch else which.stop + 3
                for h in which:
                    if 0 <= h + 2 < end:
                        maxima(b, h + 2)
                    if 0 <= h + 3 < end:
                        q_tail(b, h + 3)
                    if 0 <= h + 2 < end:
                        null_shift(b, h + 2)
                    if 0 <= h < end:
                        probs_tail(b, h, 0)
                        probs_tail(b, h, 1)
                    if h == H - 1:
                        dve.wait_ge(p0_s, (b + 1) * H)
                        dve.tensor_copy(p0_batch[:, :, :], p0[:, bass.ts(b, QT), :]).then_inc(p0_batch_s, 1)
                    if h == H:
                        dve.wait_ge(p0_hi_s, b + 1)
                        dve.tensor_tensor(p0T_lo[:, :], proj_bank[0:H, 0:N], f(p0T_hi[:, :]), ALU.subtract).then_inc(p0_lo_s, 1)
                    for u in units(h, 0, last_batch):
                        unit(b, u)
                    if 0 <= h + 2 < end:
                        inverse_sum(b, h + 2)
                    if 0 <= h - 1 < end:
                        o_tail(b, h - 1)
                    for u in units(h, 1, last_batch):
                        unit(b, u)

            for u in BEFORE:
                unit(0, u)
            steps(0, FIRST)
            with dve.Fori(0, B - 1) as b:
                steps(b, BODY)
            steps(B - 1, BODY, True)

        @block.gpsimd
        def _(pool):
            def normalise_probs(b, h):
                pool.wait_ge(p_exp, b * H * QT + QT * (h + 1))
                pool.wait_ge(e0_s, b * H + h + 1)
                pool.tensor_tensor(total[:, h % H, :], row_sum[:, h % H, :], e0[:, h % H, :], ALU.add).then_inc(total_s, 1)
                if h >= 2:
                    pool.wait_ge(t_ps, b * 2 * H + 2 * (h - 1))
                pool.wait_ge(rinv_s, b * H + h + 1)
                pool.tensor_tensor(p0[:, bass.ds((b + h // H) * QT, QT), h % H:h % H + 1].rearrange("p t h -> p (t h)"),
                                   e0[:, h % H, :], rinv[:, h % H, :], ALU.mult).then_inc(p0_s, 1)
                for t in range(QT):
                    pool.tensor_scalar(p_norm[:, h % 2, t, :], p_raw[:, h % 2, t, :], rinv[:, h % H, t:t + 1], 1.0,
                                       ALU.mult, ALU.mult).then_inc(p_norm_s, 1)

            for h in range(2):
                normalise_probs(0, h)
            with pool.Fori(0, B - 1) as b:
                for h in BODY:
                    normalise_probs(b, h)
            for h in range(2, H):
                normalise_probs(B - 1, h)


def stage_helpers(nc, ctx):
    def sb(name, shape, dt=F32):
        return ctx.enter_context(nc.sbuf_tensor(name, shape, dt))

    def sem(name):
        return ctx.enter_context(nc.semaphore(name))

    def bank(name, shape=(P, BANK)):
        return ctx.enter_context(nc.psum_tensor(name, list(shape), F32))

    return sb, sem, bank


def over_tiles(row, tiles=TT):
    return row[:, :].unsqueeze(1).broadcast_to([P, tiles, D])


def over_width(col, tiles=TT):
    return col[:, 0:tiles].unsqueeze(2).broadcast_to([P, tiles, D])


def residual_and_projections(nc, k, dram):
    with ExitStack() as ctx:
        sb, sem, bank = stage_helpers(nc, ctx)
        scale_row, bias_row, ln1_row = sb("scale_row", [P, D]), sb("bias_row", [P, D]), sb("ln1_row", [P, D])
        wqkv = sb("wqkv", [P, FH + 2 * KV, HD])
        cos, sin = sb("cos", [P, QT, HD]), sb("sin", [P, QT, HD])
        x_bias, yn, h, sq = (sb(n, [P, TT, D]) for n in ("x_bias", "yn", "h_rms", "sq"))
        hT = sb("hT", [P, TOK])
        stats, mean_var = sb("stats3", [P, TT, 6]), sb("mean_var3", [P, TT, 2])
        std, rstd = sb("std3", [P, TT]), sb("rstd3", [P, TT])
        sum_sq, rms, rrms = sb("sum_sq", [P, TT]), sb("rms", [P, TT]), sb("rrms", [P, TT])
        qkv = sb("qkv", [P, TT, FH + 2 * KV, HD])
        turned = sb("turned", [P, TT, FH + KV, HD])
        pY = [bank(f"p_y{i}", (P, 4, D)) for i in range(2)]
        pH = [bank(f"p_h{i}") for i in range(2)]
        pQ = [bank(f"p_qkv{i}", (P, 2, FH + 2 * KV, HD)) for i in range(4)]
        rows_in, w_in, rope_in = sem("rows_in"), sem("w_in"), sem("rope_in")
        x_bias_s, y_ps, y_var, y_std, x1_var, x1_std, sq_s, rms_s = (
            sem(n) for n in ("x_bias_s", "y_ps3", "y_var", "y_std", "x1_var", "x1_std", "sq_s", "rms_s"))
        h_s, hT_ps, hT_s, qkv_ps, qkv_s, step = (
            sem(n) for n in ("h_s", "hT_ps", "hT_s", "qkv_ps", "qkv_s", "dve_step3"))
        block = ctx.enter_context(nc.Block())

        @block.sync
        def _(sp):
            sp.dma_start(scale_row[:, :], dram["L0_xattn_ln_scale"].partition_broadcast(P)).then_inc(rows_in, 16)
            sp.dma_start(bias_row[:, :], dram["L0_xattn_ln_bias"].partition_broadcast(P)).then_inc(rows_in, 16)
            sp.dma_start(ln1_row[:, :], dram["L0_ffn_ln1_w"].partition_broadcast(P)).then_inc(rows_in, 16)
            at = 0
            for name, heads in (("L0_ffn_wq", FH), ("L0_ffn_wk", KV), ("L0_ffn_wv", KV)):
                sp.dma_start(wqkv[:, at:at + heads, :], dram[name].rearrange("c (h d) -> c h d", d=HD)).then_inc(w_in, 16)
                at += heads
            for table, name in ((cos, "rope_cos"), (sin, "rope_sin")):
                sp.dma_start(table[:, :, :], dram[name].rearrange("(t p) d -> p t d", p=P)).then_inc(rope_in, 16)

        @block.gpsimd
        def _(pool):
            pool.wait_ge(rows_in, 48)
            pool.tensor_tensor(x_bias[:, :, :], k.x[:, :, :], over_tiles(bias_row), ALU.add).then_inc(x_bias_s, 1)

        @block.scalar
        def _(act):
            act.wait_ge(y_var, 1)
            act.activation(std[:, :], mean_var[:, :, 1], ACT.Sqrt, bias=k.eps[:, 1:2]).then_inc(y_std, 1)
            act.wait_ge(x1_var, 1)
            act.activation(std[:, :], mean_var[:, :, 1], ACT.Sqrt, bias=k.eps[:, 0:1]).then_inc(x1_std, 1)
            act.wait_ge(sq_s, 1)
            act.activation(rms[:, :], sum_sq[:, :], ACT.Sqrt, bias=k.eps[:, 1:2], scale=1.0 / D).then_inc(rms_s, 1)
            for i in range(2):
                act.wait_ge(hT_ps, i + 1)
                act.activation(hT[:, i * BANK:(i + 1) * BANK], pH[i][:, :], ACT.Copy).then_inc(hT_s, 1)
            for i in range(4):
                act.wait_ge(qkv_ps, i + 1)
                act.activation(qkv[:, 2 * i:2 * i + 2, :, :], pQ[i][:, :, :, :], ACT.Copy).then_inc(qkv_s, 1)

        @block.tensor
        def _(pe):
            for t in range(TT):
                last = pe.transpose(pY[t // 4][:, t % 4, :], k.yT[:, t * P:(t + 1) * P], k.ident[:, :])
            last.then_inc(y_ps, 1)
            pe.wait_ge(h_s, 1)
            for t in range(TT):
                last = pe.transpose(pH[t // 4][:, (t % 4) * P:(t % 4 + 1) * P], h[:, t, :], k.ident[:, :])
                if t % 4 == 3:
                    last.then_inc(hT_ps, 1)
            pe.wait_ge(w_in, 48)
            for t in range(TT):
                if t % 4 == 0:
                    pe.wait_ge(hT_s, t // 4 + 1)
                last = pe.matmul(pQ[t // 2][:, t % 2, :, :], hT[:, t * P:(t + 1) * P], wqkv[:, :, :], start=True, stop=True)
                if t % 2:
                    last.then_inc(qkv_ps, 1)

        @block.vector
        def _(dve):
            count = [0]

            def link(ins):
                count[0] += 1
                ins.then_inc(step, 1)
                dve.wait_ge(step, count[0])

            def stats_of(tile):
                for t in range(TT):
                    last = dve.bn_stats(stats[:, t, :], tile(t))
                link(last)
                for t in range(TT):
                    last = dve.bn_aggr(mean_var[:, t, :], stats[:, t, :])
                return last

            def normalised(dst, tile):
                link(dve.reciprocal(rstd[:, :], std[:, :]))
                for t in range(TT):
                    last = dve.tensor_scalar(dst[:, t, :], tile(t), mean_var[:, t, 0:1], rstd[:, t:t + 1],
                                             ALU.subtract, ALU.mult)
                link(last)

            dve.wait_ge(y_ps, 1)
            stats_of(lambda t: pY[t // 4][:, t % 4, :]).then_inc(y_var, 1)
            dve.wait_ge(y_std, 1)
            normalised(yn, lambda t: pY[t // 4][:, t % 4, :])
            dve.wait_ge(rows_in, 48)
            link(dve.tensor_tensor(yn[:, :, :], yn[:, :, :], over_tiles(scale_row), ALU.mult))
            dve.wait_ge(x_bias_s, 1)
            link(dve.tensor_tensor(k.x1[:, :, :], yn[:, :, :], x_bias[:, :, :], ALU.add))
            stats_of(lambda t: k.x1[:, t, :]).then_inc(x1_var, 1)
            dve.wait_ge(x1_std, 1)
            normalised(k.z, lambda t: k.x1[:, t, :])
            link(dve.tensor_tensor(sq[:, :, :], k.z[:, :, :], k.z[:, :, :], ALU.mult))
            dve.tensor_reduce(sum_sq[:, :], sq[:, :, :], AX_X, ALU.add).then_inc(sq_s, 1)
            dve.wait_ge(rms_s, 1)
            link(dve.reciprocal(rrms[:, :], rms[:, :]))
            link(dve.tensor_tensor(sq[:, :, :], k.z[:, :, :], over_width(rrms), ALU.mult))
            dve.tensor_tensor(h[:, :, :], sq[:, :, :], over_tiles(ln1_row), ALU.mult).then_inc(h_s, 1)
            dve.wait_ge(qkv_s, 4)
            dve.wait_ge(rope_in, 32)
            NQK = FH + KV
            for par in range(QT):
                src, dst = qkv[:, par::QT, 0:NQK, :], turned[:, par::QT, :, :]
                sin_b = sin[:, par, :].unsqueeze(1).unsqueeze(1)
                for a, b in ((0, HD // 2), (HD // 2, 0)):
                    last = dve.tensor_tensor(dst[:, :, :, a:a + HD // 2], src[:, :, :, b:b + HD // 2],
                                             sin_b[:, :, :, a:a + HD // 2].broadcast_to([P, TT // QT, NQK, HD // 2]), ALU.mult)
            link(last)
            dve.tensor_copy(k.v[:, :, :, :], qkv[:, :, NQK:, :])
            for par in range(QT):
                cos_b = cos[:, par, :].unsqueeze(1).unsqueeze(1).broadcast_to([P, TT // QT, NQK, HD])
                src = qkv[:, par::QT, 0:NQK, :]
                last = dve.tensor_tensor(src, src, cos_b, ALU.mult)
            link(last)
            dve.tensor_tensor(k.rq[:, :, :, :], qkv[:, :, 0:FH, :], turned[:, :, 0:FH, :], ALU.add)
            link(dve.tensor_tensor(k.rk[:, :, :, :], qkv[:, :, FH:NQK, :], turned[:, :, FH:NQK, :], ALU.add))


def self_attention(nc, k, dram):
    with ExitStack() as ctx:
        sb, sem, bank = stage_helpers(nc, ctx)
        STACK = 4 * HD
        GROUPS = FH * STACK // P
        VW = 2 * HD + 1
        q_quad = sb("q_quad", [P, 2, QT, FH, 4, HD], F32R)
        k_quad = sb("k_quad", [P, 2, QT, FH, 4, HD], F32R)
        v_all, v_pair = sb("v_all", [P, TT, KV, VW], F32R), sb("v_pair", [P, QT, KV, VW], F32R)
        qT_all, kT_all = sb("qT_all", [P, GROUPS, TOK], F32R), sb("kT_all", [P, GROUPS, TOK], F32R)
        qT, kT = sb("qT", [P, GROUPS, N], F32R), sb("kT", [P, GROUPS, N], F32R)
        mask_f, mask = sb("mask_f", [P, BANK]), sb("mask", [P, BANK], BF16)
        ident_b = sb("ident_b", [P, P], BF16)
        neg_max, rinv = sb("neg_max4", [P, FH, QT]), sb("rinv4", [P, QT, FH])
        p_raw = sb("p_raw4", [P, 4, REP, QT, N])
        KEYS0, KEYS1 = REP * N, REP * P
        pT_hi, pT_lo = sb("pT_hi4", [P, 2, KEYS0 + KEYS1], F32R), sb("pT_lo4", [P, 2, KEYS0 + KEYS1], F32R)
        oT = sb("oT", [VW, KV, REP, N])
        ao_sum = sb("ao_sum", [P, QT, FH, HD])
        banks = [bank(f"bank4_{i}") for i in range(8)]
        s_bank, a_bank, b_bank, o_bank = banks[0:4], banks[4:6], banks[6], banks[7]
        g_bank = a_bank

        mask_in, consts_s = sem("mask_in"), sem("consts_s")
        quad_hi, quad_lo, qkT_ps, qT_all_s, kT_all_s, v_hi_s, v_lo_s, group_s, v_s = (
            sem(n) for n in ("quad_hi", "quad_lo", "qkT_ps", "qT_all_s", "kT_all_s", "v_hi_s4", "v_lo_s4", "group_s", "v_s"))
        s_ps, max_s, p_exp, t_ps, t_hi_s, t_lo_s, o_ps, o_s, g_ps, sum_s, ao_s = (
            sem(f"{n}4") for n in ("s_ps", "max_s", "p_exp", "t_ps", "t_hi_s", "t_lo_s", "o_ps", "o_s", "g_ps",
                                   "sum_s", "ao_s"))
        FIRST, BODY = range(-3, 2), range(2, KV + 2)
        block = ctx.enter_context(nc.Block())

        def keys1(ap):
            return ap.rearrange("p (j t n) -> p j t n", j=REP, t=QT)[:, :, 1, :]

        def key_slot(b, a):
            return k_quad[:, b % 2, :, :, a, :].rearrange("p t (g r) d -> p (t g) r d", r=REP)

        def key_heads(b):
            return k.rk[:, b * QT:(b + 1) * QT, :, :].rearrange("p t g d -> p (t g) d").unsqueeze(2)\
                .broadcast_to([P, QT * KV, REP, HD])

        @block.sync
        def _(sp):
            sp.dma_start(mask_f[:, :], dram["causal"]).then_inc(mask_in, 16)
            fetch_pair(sp, k, dram, 0)

        @block.gpsimd
        def _(pool):
            ones = k.eps[:, 2:3]

            def group(b, g):
                for dst, src in ((qT, qT_all), (kT, kT_all)):
                    last = pool.tensor_tensor(dst[:, g, :], f(src[:, g, bass.ds(b * N, N)]), ones.broadcast_to([P, N]), ALU.mult)
                last.then_inc(group_s, 1)

            def values(b, half):
                heads = slice(half * KV // 2, (half + 1) * KV // 2)
                pool.tensor_tensor(v_pair[:, :, heads, :], f(v_all[:, bass.ds(b * QT, QT), heads, :]),
                                   ones.unsqueeze(2).unsqueeze(3).broadcast_to([P, QT, KV // 2, VW]), ALU.mult).then_inc(v_s, 1)

            pool.wait_ge(qT_all_s, 1)
            pool.wait_ge(kT_all_s, 1)
            for g in range(GROUPS):
                group(0, g)
            pool.wait_ge(v_lo_s, 1)
            for half in range(2):
                values(0, half)
            pool.wait_ge(qT_all_s, B)
            pool.wait_ge(kT_all_s, B)
            split_pair(pool, k, 0, 0)
            with pool.Fori(0, B - 1) as b:
                for g in range(GROUPS):
                    pool.wait_ge(s_ps, b * KV + 2 * g + 2)
                    group(b + 1, g)
                for half in range(2):
                    pool.wait_ge(o_ps, b * KV + (half + 1) * (KV // 2))
                    values(b + 1, half)

        @block.tensor
        def _(pe):
            def features_first(b, u):
                src = q_quad if u < 2 else k_quad
                pe.wait_ge(quad_lo, b + 1)
                if b >= 1:
                    pe.wait_ge(qT_all_s if u < 2 else kT_all_s, b)
                for i in range(2):
                    g = 2 * (u % 2) + i
                    for t in range(QT):
                        last = pe.transpose(s_bank[u][:, i * N + t * P:i * N + (t + 1) * P],
                                            f(src[:, b % 2, t, 4 * g:4 * g + 4, :, :]).rearrange("p h a d -> p (h a d)"),
                                            k.ident[:, :])
                last.then_inc(qkT_ps, 1)

            def scores(b, p):
                if p % 2 == 0:
                    pe.wait_ge(group_s, b * GROUPS + p // 2 + 1)
                if p >= 2:
                    pe.wait_ge(p_exp, b * KV + p - 1)
                group = p % KV // 2
                for j in range(REP):
                    r = STACK * ((REP * p + j) % 4)
                    out = s_bank[(p % 2) * REP + j]
                    for t in range(QT):
                        pe.matmul(out[:, t * N:(t + 1) * N], qT[r:r + STACK, group, t * P:(t + 1) * P],
                                  kT[r:r + STACK, group, :], start=t == 0, stop=False)
                for j in range(REP):
                    last = pe.matmul(s_bank[(p % 2) * REP + j][:, :], ident_b[:, :], mask[:, :], start=False, stop=True)
                last.then_inc(s_ps, 1)

            def transpose_probs(b, p):
                pe.wait_ge(p_exp, b * KV + p + 1)
                if p >= 2:
                    pe.wait_ge(t_lo_s, b * 2 * KV + 2 * (p - 1) - 1)
                if p == KV + 1:
                    pe.wait_ge(sum_s, b + 1)
                for j in range(REP):
                    for t in range(QT):
                        last = pe.transpose(a_bank[p % 2][:, j * N + t * P:j * N + (t + 1) * P], p_raw[:, p % 4, j, t, 0:P],
                                            k.ident[:, :])
                last.then_inc(t_ps, 1)
                if p >= 1:
                    pe.wait_ge(t_lo_s, b * 2 * KV + 2 * p)
                for j in range(REP):
                    last = pe.transpose(b_bank[:, j * P:(j + 1) * P], p_raw[:, p % 4, j, 1, P:2 * P], k.ident[:, :])
                last.then_inc(t_ps, 1)

            def weighted_values(b, p):
                if p % (KV // 2) == 0:
                    pe.wait_ge(v_s, b * 2 + p // (KV // 2) + 1)
                pe.wait_ge(t_lo_s, b * 2 * KV + 2 * p + 2)
                if p >= 1:
                    pe.wait_ge(o_s, b * KV + p)
                for i, x in enumerate((pT_hi, pT_lo)):
                    pe.matmul(o_bank[0:VW, :], v_pair[:, 0, p % KV, :], x[:, p % 2, 0:KEYS0], start=i == 0, stop=False)
                for i, x in enumerate((pT_hi, pT_lo)):
                    last = pe.matmul(keys1(o_bank[0:VW, :]), v_pair[:, 1, p % KV, :], x[:, p % 2, KEYS0:],
                                     start=False, stop=i == 1)
                last.then_inc(o_ps, 1)

            def tokens_first(b, last_batch):
                pe.wait_ge(o_s, (b + 1) * KV)
                pe.wait_ge(t_lo_s, (b + 1) * 2 * KV + (0 if last_batch else 1))
                for t in range(QT):
                    for p in range(KV):
                        for j in range(REP):
                            at = (REP * p + j) * VW
                            tile = oT[:, p, j, t * P:(t + 1) * P]
                            if p + j + t == 0:
                                pe.matmul(g_bank[t][:, at:at + VW], tile, k.ident[0:VW, 0:VW], start=True, stop=True)
                            else:
                                last = pe.transpose(g_bank[t][:, at:at + VW], tile, k.ident[0:VW, 0:VW])
                last.then_inc(g_ps, 1)

            def steps(b, which, last_batch=False):
                end = KV if last_batch else which.stop + 3
                for p in which:
                    if p == KV + 1:
                        tokens_first(b, last_batch)
                    elif 0 <= p < end:
                        transpose_probs(b, p)
                    if 0 <= p - 1 < end:
                        weighted_values(b, p - 1)
                    if p + 3 < end:
                        scores(b, p + 3)
                    if p == KV + 1 < end:
                        transpose_probs(b, p)

            for b in range(B):
                for u in range(4):
                    features_first(b, u)
            pe.wait_ge(consts_s, 2)
            pe.wait_ge(kT_all_s, B)
            pe.wait_ge(qT_all_s, B)
            steps(0, FIRST)
            with pe.Fori(0, B - 1) as b:
                steps(b, BODY)
            steps(B - 1, BODY, True)

        @block.scalar
        def _(act):
            def quad_heads(b):
                if b >= 2:
                    act.wait_ge(qkT_ps, (b - 1) * 4)
                for a in (0, 2):
                    act.activation(q_quad[:, b % 2, :, :, a, :], k.rq[:, b * QT:(b + 1) * QT, :, :], ACT.Copy, scale=F_SCALE)
                for a in (0, 1):
                    last = act.activation(key_slot(b, a), key_heads(b), ACT.Copy)
                last.then_inc(quad_hi, 1)

            def queries_first(b):
                for i in range(2):
                    act.wait_ge(qkT_ps, b * 4 + i + 1)
                    last = act.activation(qT_all[:, 2 * i:2 * i + 2, b * N:(b + 1) * N],
                                          s_bank[i][:, :].rearrange("p (g n) -> p g n", g=2), ACT.Copy)
                last.then_inc(qT_all_s, 1)

            def exponentials(b, p):
                act.wait_ge(max_s, b * KV + p + 1)
                if p >= 4:
                    act.wait_ge(t_ps, b * 2 * KV + 2 * (p - 3))
                for j in range(REP):
                    for t in range(QT):
                        n = (t + 1) * P
                        last = act.activation(p_raw[:, p % 4, j, t, 0:n], s_bank[(p % 2) * REP + j][:, t * N:t * N + n], ACT.Exp,
                                              bias=neg_max[:, REP * (p % KV) + j, t:t + 1])
                last.then_inc(p_exp, 1)

            def probs_head(b, p):
                act.wait_ge(t_ps, b * 2 * KV + 2 * p + 1)
                if p >= 2:
                    act.wait_ge(o_ps, b * KV + p - 1)
                act.activation(pT_hi[:, p % 2, 0:KEYS0], a_bank[p % 2][:, :], ACT.Copy).then_inc(t_hi_s, 1)
                act.wait_ge(t_ps, b * 2 * KV + 2 * p + 2)
                act.activation(pT_hi[:, p % 2, KEYS0:], b_bank[:, 0:KEYS1], ACT.Copy).then_inc(t_hi_s, 1)

            def steps(b, which, last_batch=False):
                end = KV if last_batch else which.stop + 2
                for p in which:
                    if 0 <= p < end and p != KV + 1:
                        probs_head(b, p)
                    if 0 <= p + 2 < end:
                        exponentials(b, p + 2)
                    if p == KV + 1 < end:
                        probs_head(b, p)

            quad_heads(0)
            act.activation(v_all[:, :, :, 0:HD], k.v[:, :, :, :], ACT.Copy)
            act.activation(v_all[:, :, :, 2 * HD], k.eps[:, 2:3].unsqueeze(2).broadcast_to([P, TT, KV]), ACT.Copy)\
                .then_inc(v_hi_s, 1)
            for b in range(B):
                if b + 1 < B:
                    quad_heads(b + 1)
                queries_first(b)
            act.wait_ge(mask_in, 16)
            act.activation(mask[:, :], mask_f[:, :], ACT.Copy).then_inc(consts_s, 1)
            act.activation(ident_b[:, :], k.ident[:, :], ACT.Copy).then_inc(consts_s, 1)
            steps(0, FIRST)
            with act.Fori(0, B - 1) as b:
                steps(b, BODY)
            steps(B - 1, BODY, True)

        @block.vector
        def _(dve):
            def quad_tails(b):
                dve.wait_ge(quad_hi, b + 1)
                for a in (1, 3):
                    dve.scalar_tensor_tensor(q_quad[:, b % 2, :, :, a, :].rearrange("p t h d -> p (t h) d"),
                                             k.rq[:, b * QT:(b + 1) * QT, :, :].rearrange("p t h d -> p (t h) d"), F_SCALE,
                                             f(q_quad[:, b % 2, :, :, 0, :]).rearrange("p t h d -> p (t h) d"),
                                             ALU.mult, ALU.subtract)
                for a in (2, 3):
                    last = dve.tensor_tensor(key_slot(b, a), key_heads(b), f(key_slot(b, 0)), ALU.subtract)
                last.then_inc(quad_lo, 1)

            def keys_first(b):
                for i in range(2):
                    dve.wait_ge(qkT_ps, b * 4 + i + 3)
                    last = dve.tensor_copy(kT_all[:, 2 * i:2 * i + 2, b * N:(b + 1) * N],
                                           s_bank[2 + i][:, :].rearrange("p (g n) -> p g n", g=2))
                last.then_inc(kT_all_s, 1)

            def maxima(b, p):
                dve.wait_ge(s_ps, b * KV + p + 1)
                for j in range(REP):
                    last = dve.tensor_reduce(neg_max[:, REP * (p % KV) + j, :],
                                             s_bank[(p % 2) * REP + j][:, :].rearrange("p (t n) -> p t n", t=QT),
                                             AX_X, ALU.max, negate=True)
                last.then_inc(max_s, 1)

            def probs_tail(b, p):
                dve.wait_ge(t_hi_s, b * 2 * KV + 2 * p + 1)
                if p >= 2:
                    dve.wait_ge(o_ps, b * KV + p - 1)
                dve.tensor_tensor(pT_lo[:, p % 2, 0:KEYS0], a_bank[p % 2][:, :], f(pT_hi[:, p % 2, 0:KEYS0]), ALU.subtract)\
                    .then_inc(t_lo_s, 1)
                dve.wait_ge(t_hi_s, b * 2 * KV + 2 * p + 2)
                dve.tensor_tensor(pT_lo[:, p % 2, KEYS0:], b_bank[:, 0:KEYS1], f(pT_hi[:, p % 2, KEYS0:]), ALU.subtract)\
                    .then_inc(t_lo_s, 1)

            def output_copy(b, p):
                dve.wait_ge(o_ps, b * KV + p + 1)
                if p == KV:
                    dve.wait_ge(g_ps, b + 1)
                dve.tensor_copy(oT[:, p % KV, :, :].rearrange("p j n -> p (j n)"), o_bank[0:VW, :]).then_inc(o_s, 1)

            def attention_out(b):
                dve.wait_ge(g_ps, b + 1)
                for t in range(QT):
                    out = g_bank[t][:, 0:FH * VW].rearrange("p (h c) -> p h c", c=VW)
                    dve.tensor_reduce(ao_sum[:, t, :, :], out[:, :, 0:2 * HD].rearrange("p h (a d) -> p h d a", a=2), AX_X, ALU.add)
                    last = dve.reciprocal(rinv[:, t, :], out[:, :, 2 * HD])
                last.then_inc(sum_s, 1)
                dve.wait_ge(sum_s, b + 1)
                dve.tensor_tensor(k.ao[:, bass.ds(b * QT, QT), :, :].rearrange("p t h d -> p (t h) d"),
                                  ao_sum[:, :, :, :].rearrange("p t h d -> p (t h) d"),
                                  rinv[:, :, :].rearrange("p t h -> p (t h)").unsqueeze(2).broadcast_to([P, QT * FH, HD]),
                                  ALU.mult).then_inc(ao_s, 1)
                dve.wait_ge(ao_s, b + 1)

            def steps(b, which, last_batch=False):
                end = KV if last_batch else which.stop + 2
                for p in which:
                    if 0 <= p + 2 < end:
                        maxima(b, p + 2)
                    if p == KV + 1:
                        attention_out(b)
                    if 0 <= p < end:
                        probs_tail(b, p)
                    if 0 <= p - 1 < end:
                        output_copy(b, p - 1)

            quad_tails(0)
            dve.wait_ge(v_hi_s, 1)
            dve.tensor_tensor(v_all[:, :, :, HD:2 * HD], k.v[:, :, :, :], f(v_all[:, :, :, 0:HD]), ALU.subtract).then_inc(v_lo_s, 1)
            for b in range(B):
                if b + 1 < B:
                    quad_tails(b + 1)
                keys_first(b)
            steps(0, FIRST)
            with dve.Fori(0, B - 1) as b:
                steps(b, BODY)
            steps(B - 1, BODY, True)


def route(nc, k, dram):
    with ExitStack() as ctx:
        sb, sem, bank = stage_helpers(nc, ctx)
        wo, router, ln2_row, iota = sb("wo", [P, D]), sb("router", [P, E]), sb("ln2_row", [P, D]), sb("iota", [P, E])
        aoT, h2T = sb("aoT", [P, TOK]), sb("h2T", [P, TOK])
        sq, h2 = sb("sq5", [P, TT, D]), sb("h2", [P, TT, D])
        sum_sq, rms, rrms = sb("sum_sq5", [P, TT]), sb("rms5", [P, TT]), sb("rrms5", [P, TT])
        logits, expd, probs, pick, pick2 = (sb(n, [P, TT, E]) for n in ("logits", "expd", "probs", "pick", "pick2"))
        top, top_at, top_at_f = sb("top", [P, TT, 8]), sb("top_at", [P, TT, 8], U32), sb("top_at_f", [P, TT, 2])
        lmax, lsum, lrec, tsum, trec = (sb(n, [P, TT]) for n in ("lmax", "lsum", "lrec", "tsum", "trec"))
        topn = sb("topn", [P, TT, 2])
        pT = [bank(f"p_aoT{i}") for i in range(2)]
        pA = [bank(f"p_att{i}", (P, 4, D)) for i in range(2)]
        pH = [bank(f"p_h2T{i}") for i in range(2)]
        pL = bank("p_logits", (P, TT, E))
        w_in, aoT_ps, aoT_s, att_ps, x2_s, sq_s, rms_s, h2_s, h2T_ps, h2T_s, h2T_hi_s, logit_ps, shifted_s, exp_s, step = (
            sem(f"{n}5") for n in ("w_in", "aoT_ps", "aoT_s", "att_ps", "x2_s", "sq_s", "rms_s", "h2_s", "h2T_ps", "h2T_s",
                                   "h2T_hi_s", "logit_ps", "shifted_s", "exp_s", "step"))
        block = ctx.enter_context(nc.Block())

        @block.sync
        def _(sp):
            sp.dma_start(wo[:, :], dram["L0_ffn_wo"]).then_inc(w_in, 16)
            sp.dma_start(router[:, :], dram["L0_ffn_router_w"]).then_inc(w_in, 16)
            sp.dma_start(ln2_row[:, :], dram["L0_ffn_ln2_w"].partition_broadcast(P)).then_inc(w_in, 16)
            sp.dma_start(iota[:, :], dram["expert_ids"].partition_broadcast(P)).then_inc(w_in, 16)

        @block.tensor
        def _(pe):
            for t in range(TT):
                last = pe.transpose(pT[t // 4][:, (t % 4) * P:(t % 4 + 1) * P],
                                    k.ao[:, t, :, :].rearrange("p h d -> p (h d)"), k.ident[:, :])
            last.then_inc(aoT_ps, 1)
            pe.wait_ge(w_in, 64)
            pe.wait_ge(aoT_s, 1)
            for t in range(TT):
                last = pe.matmul(pA[t // 4][:, t % 4, :], aoT[:, t * P:(t + 1) * P], wo[:, :], start=True, stop=True)
            last.then_inc(att_ps, 1)
            pe.wait_ge(h2_s, 1)
            for t in range(TT):
                last = pe.transpose(pH[t // 4][:, (t % 4) * P:(t % 4 + 1) * P], h2[:, t, :], k.ident[:, :])
            last.then_inc(h2T_ps, 1)
            pe.wait_ge(h2T_s, 1)
            for t in range(TT):
                last = pe.matmul(pL[:, t, :], h2T[:, t * P:(t + 1) * P], router[:, :], start=True, stop=True)
            last.then_inc(logit_ps, 1)

        @block.scalar
        def _(act):
            act.wait_ge(aoT_ps, 1)
            for i in range(2):
                last = act.activation(aoT[:, i * BANK:(i + 1) * BANK], pT[i][:, :], ACT.Copy)
            last.then_inc(aoT_s, 1)
            act.wait_ge(sq_s, 1)
            act.activation(rms[:, :], sum_sq[:, :], ACT.Sqrt, bias=k.eps[:, 1:2], scale=1.0 / D).then_inc(rms_s, 1)
            act.wait_ge(h2T_ps, 1)
            for i in range(2):
                last = act.activation(h2T[:, i * BANK:(i + 1) * BANK], pH[i][:, :], ACT.Copy)
            last.then_inc(h2T_s, 1)
            for i in range(2):
                last = act.activation(k.h2T_hi[:, i * BANK:(i + 1) * BANK], pH[i][:, :], ACT.Copy)
            last.then_inc(h2T_hi_s, 1)
            act.wait_ge(shifted_s, 1)
            act.activation(expd[:, :, :], logits[:, :, :], ACT.Exp).then_inc(exp_s, 1)

        @block.vector
        def _(dve):
            count = [0]

            def link(ins):
                count[0] += 1
                ins.then_inc(step, 1)
                dve.wait_ge(step, count[0])

            dve.wait_ge(att_ps, 1)
            for i in range(2):
                last = dve.tensor_tensor(k.x2[:, 4 * i:4 * i + 4, :], k.z[:, 4 * i:4 * i + 4, :], pA[i][:, :, :], ALU.add)
            last.then_inc(x2_s, 1)
            dve.wait_ge(x2_s, 1)
            link(dve.tensor_tensor(sq[:, :, :], k.x2[:, :, :], k.x2[:, :, :], ALU.mult))
            dve.tensor_reduce(sum_sq[:, :], sq[:, :, :], AX_X, ALU.add).then_inc(sq_s, 1)
            dve.wait_ge(rms_s, 1)
            link(dve.reciprocal(rrms[:, :], rms[:, :]))
            link(dve.tensor_tensor(sq[:, :, :], k.x2[:, :, :], over_width(rrms), ALU.mult))
            dve.wait_ge(w_in, 64)
            dve.tensor_tensor(h2[:, :, :], sq[:, :, :], over_tiles(ln2_row), ALU.mult).then_inc(h2_s, 1)
            dve.wait_ge(h2T_hi_s, 1)
            for i in range(2):
                dve.tensor_tensor(k.h2T_lo[:, i * BANK:(i + 1) * BANK], pH[i][:, :], f(k.h2T_hi[:, i * BANK:(i + 1) * BANK]), ALU.subtract)

            def wide(col, n=E):
                return col.unsqueeze(2).broadcast_to([P, TT, n])

            dve.wait_ge(logit_ps, 1)
            link(dve.tensor_reduce(lmax[:, :], pL[:, :, :], AX_X, ALU.max))
            dve.tensor_tensor(logits[:, :, :], pL[:, :, :], wide(lmax[:, :]), ALU.subtract).then_inc(shifted_s, 1)
            dve.wait_ge(exp_s, 1)
            link(dve.tensor_reduce(lsum[:, :], expd[:, :, :], AX_X, ALU.add))
            link(dve.reciprocal(lrec[:, :], lsum[:, :]))
            link(dve.tensor_tensor(probs[:, :, :], expd[:, :, :], wide(lrec[:, :]), ALU.mult))
            for t in range(TT):
                last = dve.max(top[:, t, :], probs[:, t, :])
            link(last)
            for t in range(TT):
                last = dve.max_index(top_at[:, t, :], top[:, t, :], probs[:, t, :])
            link(last)
            dve.tensor_copy(top_at_f[:, :, :], top_at[:, :, 0:2])
            link(dve.tensor_tensor(tsum[:, :], top[:, :, 0], top[:, :, 1], ALU.add))
            link(dve.reciprocal(trec[:, :], tsum[:, :]))
            link(dve.tensor_tensor(topn[:, :, :], top[:, :, 0:2], wide(trec[:, :], 2), ALU.mult))
            ids = iota[:, :].unsqueeze(1).broadcast_to([P, TT, E])
            for i, one in enumerate((pick, pick2)):
                link(dve.tensor_tensor(one[:, :, :], ids, wide(top_at_f[:, :, i]), ALU.is_equal))
                link(dve.tensor_tensor(one[:, :, :], one[:, :, :], wide(topn[:, :, i]), ALU.mult))
            link(dve.tensor_tensor(k.weights[:, :, :], pick[:, :, :], pick2[:, :, :], ALU.add))


def fetch_pair(sp, k, dram, g):
    for which, name in enumerate(("L0_ffn_w_gate", "L0_ffn_w_up")):
        sp.dma_start(k.gu_raw[:, which, :, :], dram[name][bass.ds(2 * g, 2), :, :].rearrange("e d m -> d e m"))\
            .then_inc(k.raw_in, 16)
    rows = dram["L0_ffn_w_down"].rearrange("(g e) m d -> g (e m) d", e=2)
    sp.dma_start(k.dn_raw[:, :, :], rows[bass.ds(g, 1), :, :].rearrange("g (s r) d -> r (g s) d", r=P)).then_inc(k.raw_in, 16)


def split_pair(pool, k, g, slot, free=None):
    pool.wait_ge(k.raw_in, (g + 1) * 48)
    if free is not None:
        pool.wait_ge(*free)
    pool.tensor_tensor(k.dn_hi[:, slot, :, :], k.dn_raw[:, :, :], k.eps[:, 2:3].unsqueeze(2).broadcast_to([P, SLABS, D]),
                       ALU.mult)
    pool.tensor_scalar(k.gu_hi[:, slot, :, :], k.gu_raw[:, :, :, :].rearrange("p a e m -> p a (e m)"), 1.0, 1.0,
                       ALU.mult, ALU.mult).then_inc(k.hi_made, 1)
    pool.wait_ge(k.hi_made, g + 1)
    pool.tensor_tensor(k.gu_lo[:, slot, :, :], k.gu_raw[:, :, :, :].rearrange("p a e m -> p a (e m)"),
                       f(k.gu_hi[:, slot, :, :]), ALU.subtract)
    pool.tensor_tensor(k.dn_lo[:, slot, :, :], k.dn_raw[:, :, :], f(k.dn_hi[:, slot, :, :]), ALU.subtract)\
        .then_inc(k.split_s, 1)


def experts(nc, k, dram, out):
    with ExitStack() as ctx:
        sb, sem, bank = stage_helpers(nc, ctx)
        wcol = sb("wcol", [P, E, TT])
        wide = sb("wide", [P, E, TOK])
        up_w = sb("up_w", [P, 2, BANK])
        gate = sb("gate", [P, 2, BANK])
        act_f = sb("act_f", [P, 2, BANK])
        act_hi, act_lo = sb("act_hi", [P, 2, BANK], F32R), sb("act_lo", [P, 2, BANK], F32R)
        sumT, res = sb("sumT", [P, TOK]), sb("res", [P, TT, D])
        g_bank, u_bank = ([bank(f"{n}_bank{i}") for i in range(3)] for n in "gu")
        d_bank = [bank(f"d_bank{i}") for i in range(2)]
        w_bank = g_bank + u_bank
        wcol_s, w_ps, w_s, w_s2, sum_ps, out_ps, out_s = (
            sem(n) for n in ("wcol_s", "w_ps", "w_s", "w_s2", "sum_ps", "out_ps", "out_s"))
        sumT_s, res_s = ([sem(f"{n}{c}") for c in range(CH)] for n in ("sumT_s", "res_s"))
        gu_ps, silu_s, weighed_s, mul_s, a_hi_s, a_lo_s, down_ps = (
            sem(n) for n in ("gu_ps", "silu_s", "weighed_s", "mul_s", "a_hi_s", "a_lo_s", "down_ps"))
        U = CH * SLABS
        ROWS = E * CH
        block = ctx.enter_context(nc.Block())

        def where(n):
            return n // U, (n % U) // SLABS, n % SLABS

        @block.sync
        def _(sp):
            with sp.Fori(1, PAIRS) as g:
                sp.wait_ge(k.split_s, g)
                fetch_pair(sp, k, dram, g)
            for c in range(CH):
                sp.wait_ge(res_s[c], 1)
                sp.dma_start(in_tiles(out)[:, 4 * c:4 * c + 4, :], res[:, 4 * c:4 * c + 4, :]).then_inc(out_s, 16)
            sp.wait_ge(out_s, CH * 16)

        @block.gpsimd
        def _(pool):
            split_pair(pool, k, 1, 1)
            with pool.Fori(1, PAIRS // 2) as g:
                for slot in range(2):
                    split_pair(pool, k, g * 2 + slot, slot, (down_ps, (g * 2 + slot - 1) * U))

        @block.tensor
        def _(pe):
            def weight_row(r):
                e, c = divmod(r, CH)
                if r >= len(w_bank):
                    pe.wait_ge(*((w_s, (r - 6) // 2 + 1) if r % 2 == 0 else (w_s2, (r - 6) // 2 + 1)))
                for t in range(4):
                    last = pe.transpose(w_bank[r % 6][:, t * P:(t + 1) * P],
                                        wcol[:, e, 4 * c + t:4 * c + t + 1].broadcast_to([P, P]), k.ident[:, :])
                last.then_inc(w_ps, 1)

            def residual(c, x, first):
                for t in range(4):
                    last = pe.matmul(d_bank[c][:, t * P:(t + 1) * P], x[:, 4 * c + t, :], k.ident[:, :],
                                     start=first and t == 0, stop=not first and t == 3)
                return last

            for c in range(CH):
                residual(c, k.x2, True)
            pe.wait_ge(wcol_s, 1)
            for r in range(ROWS):
                weight_row(r)
            pe.wait_ge(w_s, ROWS // 2)
            pe.wait_ge(w_s2, ROWS // 2)
            with pe.Fori(0, PAIRS // 2) as g:
                def gate_up(n):
                    slot, c, s = where(n)
                    if n >= 3:
                        pe.wait_ge(silu_s, g * 2 * U + n - 2)
                        pe.wait_ge(weighed_s, g * 2 * U + n - 2)
                    for which, out in ((0, g_bank[n % 3]), (1, u_bank[n % 3])):
                        for m, (w, x) in enumerate(((k.gu_hi, k.h2T_hi), (k.gu_hi, k.h2T_lo), (k.gu_lo, k.h2T_hi))):
                            last = pe.matmul(out[:, :], w[:, slot, which, s * P:(s + 1) * P],
                                             x[:, c * BANK:(c + 1) * BANK], start=m == 0, stop=m == 2)
                    last.then_inc(gu_ps, 1)

                def down(n):
                    slot, c, s = where(n)
                    pe.wait_ge(a_lo_s, g * 2 * U + n + 1)
                    for m, (w, x) in enumerate(((k.dn_hi, act_hi), (k.dn_hi, act_lo), (k.dn_lo, act_hi))):
                        last = pe.matmul(d_bank[c][:, :], w[:, slot, s, :], x[:, n % 2, :], start=False, stop=False)
                    last.then_inc(down_ps, 1)

                for n in range(2 * U + 2):
                    if n < 2 * U:
                        if n % U == 0:
                            pe.wait_ge(k.split_s, g * 2 + n // U + 1)
                        gate_up(n)
                    if n >= 2:
                        down(n - 2)
            for c in range(CH):
                residual(c, k.x1, False).then_inc(sum_ps, 1)
            for c in range(CH):
                pe.wait_ge(sumT_s[c], 1)
                for t in range(4):
                    last = pe.transpose(g_bank[c][:, t * P:(t + 1) * P], sumT[:, c * BANK + t * P:c * BANK + (t + 1) * P],
                                        k.ident[:, :])
                last.then_inc(out_ps, 1)

        @block.scalar
        def _(act):
            for r in range(0, ROWS, 2):
                e, c = divmod(r, CH)
                act.wait_ge(w_ps, r + 1)
                act.activation(wide[:, e, c * BANK:(c + 1) * BANK], w_bank[r % 6][:, :], ACT.Copy).then_inc(w_s, 1)
            with act.Fori(0, PAIRS // 2) as g:
                def silu(n):
                    act.wait_ge(gu_ps, g * 2 * U + n + 1)
                    if n >= 2:
                        act.wait_ge(mul_s, g * 2 * U + n - 1)
                    act.activation(gate[:, n % 2, :], g_bank[n % 3][:, :], ACT.Silu).then_inc(silu_s, 1)

                def head(n):
                    act.wait_ge(mul_s, g * 2 * U + n + 1)
                    if n >= 2:
                        act.wait_ge(down_ps, g * 2 * U + n - 1)
                    act.activation(act_hi[:, n % 2, :], act_f[:, n % 2, :], ACT.Copy).then_inc(a_hi_s, 1)

                for n in range(2 * U + 1):
                    if n >= 1:
                        head(n - 1)
                    if n < 2 * U:
                        silu(n)
            act.wait_ge(sum_ps, 1)
            act.activation(sumT[:, 0:BANK], d_bank[0][:, :], ACT.Copy).then_inc(sumT_s[0], 1)
            act.wait_ge(out_ps, 1)
            act.activation(res[:, 0:4, :], g_bank[0][:, :].rearrange("p (t d) -> p t d", t=4), ACT.Copy).then_inc(res_s[0], 1)

        @block.vector
        def _(dve):
            dve.tensor_copy(wcol[:, :, :], k.weights[:, :, :].rearrange("p t e -> p e t")).then_inc(wcol_s, 1)
            for r in range(1, ROWS, 2):
                e, c = divmod(r, CH)
                dve.wait_ge(w_ps, r + 1)
                dve.tensor_copy(wide[:, e, c * BANK:(c + 1) * BANK], w_bank[r % 6][:, :]).then_inc(w_s2, 1)
            dve.wait_ge(w_s, ROWS // 2)
            dve.wait_ge(w_s2, ROWS // 2)
            with dve.Fori(0, PAIRS // 2) as g:
                def weigh(n):
                    slot, c, s = where(n)
                    dve.wait_ge(gu_ps, g * 2 * U + n + 1)
                    if n >= 2:
                        dve.wait_ge(mul_s, g * 2 * U + n - 1)
                    first = min(max(HID - s * P, 0), P)
                    for i, rows in ((0, slice(0, first)), (1, slice(first, P))):
                        if rows.stop > rows.start:
                            w = wide[rows, bass.ds(g * 4 + slot * 2 + i, 1), c * BANK:(c + 1) * BANK]
                            last = dve.tensor_tensor(up_w[rows, n % 2, :], u_bank[n % 3][rows, :],
                                                     w.rearrange("p e n -> p (e n)"), ALU.mult)
                    last.then_inc(weighed_s, 1)

                def product(n):
                    if n >= 2:
                        dve.wait_ge(a_lo_s, g * 2 * U + n - 1)
                    dve.wait_ge(silu_s, g * 2 * U + n + 1)
                    dve.wait_ge(weighed_s, g * 2 * U + n + 1)
                    dve.tensor_tensor(act_f[:, n % 2, :], up_w[:, n % 2, :], gate[:, n % 2, :], ALU.mult).then_inc(mul_s, 1)

                def tail(n):
                    dve.wait_ge(a_hi_s, g * 2 * U + n + 1)
                    dve.tensor_tensor(act_lo[:, n % 2, :], act_f[:, n % 2, :], f(act_hi[:, n % 2, :]), ALU.subtract).then_inc(a_lo_s, 1)

                for n in range(2 * U + 1):
                    if n < 2 * U:
                        weigh(n)
                    if n >= 1:
                        tail(n - 1)
                    if n < 2 * U:
                        product(n)
            dve.wait_ge(sum_ps, 2)
            dve.tensor_copy(sumT[:, BANK:TOK], d_bank[1][:, :]).then_inc(sumT_s[1], 1)
            dve.wait_ge(out_ps, 2)
            dve.tensor_copy(res[:, 4:8, :], g_bank[1][:, :].rearrange("p (t d) -> p t d", t=4)).then_inc(res_s[1], 1)


def build(nc, dram, out):
    k = Kernel()
    with ExitStack() as ctx:
        def sb(name, shape, dt=F32):
            return ctx.enter_context(nc.sbuf_tensor(name, shape, dt))

        k.x, k.ident, k.eps = sb("x", [P, TT, D]), sb("ident", [P, P]), sb("eps", [P, 3])
        k.yT = sb("yT", [P, TOK])
        with ExitStack() as own:
            def sw(name, shape, dt=F32R):
                return own.enter_context(nc.sbuf_tensor(name, shape, dt))

            k.wq_hi, k.wq_lo = (sw(f"wq_{s}", [P, H, 2, DH]) for s in ("hi", "lo"))
            k.wkv_hi, k.wkv_lo = (sw(f"wkv_{s}", [P, CT, 2 * INNER]) for s in ("hi", "lo"))
            k.wout_hi, k.wout_lo = (sw(f"wout_{s}", [P, H, D]) for s in ("hi", "lo"))
            k.xnT_hi, k.xnT_lo = (sw(f"xnT_{s}", [P, TOK]) for s in ("hi", "lo"))
            k.u_hi, k.u_lo = (sw(f"u_{s}", [H, D]) for s in ("hi", "lo"))
            k.s0n = sw("s0n", [P, TT, H], F32)
            load_and_split(nc, k, dram)
            cross_attention(nc, k, dram)
        k.x1, k.x2, k.z = (sb(n, [P, TT, D]) for n in ("x1", "x2", "z"))
        k.rq, k.rk, k.v = sb("rq", [P, TT, FH, HD]), sb("rk", [P, TT, KV, HD]), sb("v", [P, TT, KV, HD])
        k.ao = sb("ao", [P, TT, FH, HD])
        k.h2T_hi, k.h2T_lo = sb("h2T_hi", [P, TOK], F32R), sb("h2T_lo", [P, TOK], F32R)
        k.weights = sb("weights", [P, TT, E])
        k.gu_raw, k.dn_raw = sb("gu_raw", [P, 2, 2, HID]), sb("dn_raw", [P, SLABS, D])
        k.gu_hi, k.gu_lo = (sb(f"gu_{s}", [P, 2, 2, 2 * HID], F32R) for s in ("hi", "lo"))
        k.dn_hi, k.dn_lo = (sb(f"dn_{s}", [P, 2, SLABS, D], F32R) for s in ("hi", "lo"))
        k.raw_in, k.hi_made, k.split_s = (ctx.enter_context(nc.semaphore(n)) for n in ("raw_in", "hi_made", "split_s"))
        residual_and_projections(nc, k, dram)
        self_attention(nc, k, dram)
        route(nc, k, dram)
        experts(nc, k, dram, out)


def shape_constants():
    import numpy as np

    angle = np.arange(N, dtype=np.float32)[:, None] * (1.0 / 10000.0 ** (np.arange(0, HD, 2, dtype=np.float32) / HD)).astype(np.float32)
    cos, sin = np.cos(angle), np.sin(angle)
    hidden = np.triu(np.full((P, P), MASKED, np.float32), 1)
    none, every = np.zeros((P, P), np.float32), np.full((P, P), MASKED, np.float32)
    return {
        "identity": np.eye(P, dtype=np.float32),
        "rope_cos": np.concatenate([cos, cos], -1).astype(np.float32),
        "rope_sin": np.concatenate([-sin, sin], -1).astype(np.float32),
        "causal": np.concatenate([hidden, every, none, hidden], -1),
        "expert_ids": np.arange(E, dtype=np.float32),
    }


def kernel(**inputs):
    import numpy as np
    import concourse.bacc as bacc
    from concourse.bass_utils import run_bass_kernel_spmd

    nc = bacc.Bacc("TRN2", target_bir_lowering=False, num_devices=1)
    arrays = {name: np.ascontiguousarray(a) for name, a in {**inputs, **shape_constants()}.items()}
    dram = {name: nc.dram_tensor(f"in_{name}", a.shape, mybir.dt.from_np(a.dtype), kind="ExternalInput").ap()
            for name, a in arrays.items()}
    out = nc.dram_tensor("out", (B, N, D), F32, kind="ExternalOutput").ap()
    build(nc, dram, out)
    r = run_bass_kernel_spmd(nc, [{f"in_{name}": a for name, a in arrays.items()}], core_ids=[0])
    return r.results[0]["out"]
```

```python
from contextlib import ExitStack

import concourse.bass as bass
from concourse import mybir

F32 = mybir.dt.float32
F32R = mybir.dt.float32r
BF16 = mybir.dt.bfloat16
U32 = mybir.dt.uint32
ALU = mybir.AluOpType
ACT = mybir.ActivationFunctionType
AX_X = mybir.AxisListType.X

P = 128
BANK = 512

B, N, D = 4, 256, 128
TOK = B * N
TT = TOK // P
QT = N // P
M, C = 512, 256
KT = M // P
CT = C // P
H, DH = 16, 64
INNER = H * DH
X_SCALE = DH ** -0.5
PROJ = 5

FH, KV, HD = 16, 8, 8
REP = FH // KV
F_SCALE = float(HD) ** -0.5
E, HID = 8, 448
PAIRS = E // 2
SLABS = 2 * HID // P
CH = TOK // BANK
LN_EPS, RMS_EPS = 1e-5, 1e-6
MASKED = -1e30


def f(ap):
    return ap.bitcast(F32)


def in_tiles(dram):
    return dram.rearrange("b (t p) d -> p (b t) d", p=P)


class Kernel:
    pass


def token_stats(dve, tiles, src, stats, mean_var, done, aggregated):
    for t in tiles:
        last = dve.bn_stats(stats[:, t, :], src(t))
    last.then_inc(done, 1)
    dve.wait_ge(done, aggregated - 1)
    for t in tiles:
        last = dve.bn_aggr(mean_var[:, t, :], stats[:, t, :])
    last.then_inc(done, 1)


UNITS = [("c", 0), ("c", 1), ("k", 0), ("v", 0, 0), ("v", 0, 1), ("k", 1), ("v", 0, 2), ("k", 2), ("v", 0, 3), ("k", 3),
         ("k", 4), ("v", 1, 0), ("k", 5), ("v", 1, 1), ("k", 6), ("v", 1, 2), ("v", 1, 3), ("k", 7)]
NU = len(UNITS)
FIRST_UNITS = [0, 1, 2, 5, 7, 3, 4, 6, 8]


def project(pe, k, b, u, out):
    kind, i, *t = UNITS[u % NU]
    if kind == "c":
        if i == 0:
            pe.wait_ge(k.ctx_in, (b + u // NU + 1) * 16)
        for t in range(KT):
            last = pe.transpose(out[:, t * P:(t + 1) * P], k.ctx_raw[:, t, i * P:(i + 1) * P], k.ident[:, :])
        last.then_inc(k.proj_ps, 1)
        return
    n = 0
    for c in range(CT):
        for x, w in ((k.cT_hi, k.wkv_hi), (k.cT_lo, k.wkv_hi), (k.cT_hi, k.wkv_lo)):
            if kind == "k":
                last = pe.matmul(out[:, :], w[:, c, i * P:(i + 1) * P], x[:, c, :], start=n == 0, stop=n == 3 * CT - 1)
            else:
                last = pe.matmul(out[:, :], x[:, c, t[0] * P:(t[0] + 1) * P],
                                 w[:, c, INNER + i * BANK:INNER + (i + 1) * BANK], start=n == 0, stop=n == 3 * CT - 1)
            n += 1
    last.then_inc(k.proj_ps, 1)


def projected_heads(act, k, u, src, before):
    kind, i, *t = UNITS[u % NU]
    act.wait_ge(k.proj_ps, before + 1)
    if kind == "c":
        last = act.activation(k.cT_hi[:, i, :], src[:, :], ACT.Copy)
    elif kind == "k":
        act.activation(k.keys[0:DH, 2 * i, :], src[0:DH, :], ACT.Copy)
        last = act.activation(k.keys[DH:P, 2 * i + 1, :], src[DH:P, :], ACT.Copy)
    else:
        last = act.activation(k.vals[:, t[0], i * (H // 2):(i + 1) * (H // 2), 0:DH],
                              src[:, :].rearrange("p (h d) -> p h d", d=DH), ACT.Copy)
    last.then_inc(k.proj_hi, 1)


def projected_tails(dve, k, u, src, before):
    kind, i, *t = UNITS[u % NU]
    dve.wait_ge(k.proj_hi, before + 1)
    if kind == "c":
        last = dve.tensor_tensor(k.cT_lo[:, i, :], src[:, :], f(k.cT_hi[:, i, :]), ALU.subtract)
    elif kind == "k":
        h = 2 * i
        dve.tensor_tensor(k.keys[DH:P, h, :], src[0:DH, :], f(k.keys[0:DH, h, :]), ALU.subtract)
        last = dve.tensor_tensor(k.keys[0:DH, h + 1, :], src[DH:P, :], f(k.keys[DH:P, h + 1, :]), ALU.subtract)
    else:
        v = k.vals[:, t[0], i * (H // 2):(i + 1) * (H // 2), :]
        last = dve.tensor_tensor(v[:, :, DH:2 * DH], src[:, :].rearrange("p (h d) -> p h d", d=DH),
                                 f(v[:, :, 0:DH]), ALU.subtract)
    last.then_inc(k.proj_lo, 1)


def load_and_split(nc, k, dram):
    with ExitStack() as ctx:
        def sb(name, shape, dt=F32):
            return ctx.enter_context(nc.sbuf_tensor(name, shape, dt))

        def sem(name):
            return ctx.enter_context(nc.semaphore(name))

        wq_raw = sb("wq_raw", [P, H, DH])
        wkv_raw = sb("wkv_raw", [P, CT, 2 * INNER])
        wout_raw = sb("wout_raw", [P, H, D])
        nk_row = sb("nk_row", [P, DH])
        nv_col = sb("nv_col", [DH, 1])
        nv_diag = sb("nv_diag", [DH, H, H])
        nk_wq = sb("nk_wq", [P, H, DH])
        w0 = sb("w0", [P, H])
        xn = sb("xn", [P, TT, D])
        xnT = sb("xnT", [P, TOK])
        stats = sb("stats1", [P, TT, 6])
        mean_var = sb("mean_var1", [P, TT, 2])
        shifted, rstd = sb("shifted1", [P, TT]), sb("rstd1", [P, TT])
        pT = [ctx.enter_context(nc.psum_tensor(f"p_xnT{i}", [P, BANK], F32)) for i in range(2)]
        proj_bank = [ctx.enter_context(nc.psum_tensor(f"p_proj{i}", [P, BANK], F32)) for i in range(4)]
        pS0 = ctx.enter_context(nc.psum_tensor("p_s0", [P, TT, H], F32))
        pU = ctx.enter_context(nc.psum_tensor("p_u", [H, D], F32))

        x_in, wq_in, wk_in, wv_in = sem("x_in"), sem("wq_in"), sem("wk_in"), sem("wv_in")
        wout_in, null_in, const_in = sem("wout_in"), sem("null_in"), sem("const_in")
        diag_zero, diag_set = sem("diag_zero"), sem("diag_set")
        x_var, x_shifted, x_rstd = sem("x_var"), sem("x_shifted"), sem("x_rstd")
        xn_ready, xnT_ps, xnT_ready, xnT_hi = sem("xn_ready"), sem("xnT_ps"), sem("xnT_ready"), sem("xnT_hi_s")
        w0_mul, w0_ready, s0_ps, u_ps, u_hi_s = sem("w0_mul"), sem("w0_ready"), sem("s0_ps"), sem("u_ps"), sem("u_hi_s")
        wq_hi_s, wk_hi_s, wk_lo_s, wv_hi_s, wv_lo_s, wout_hi_s = (
            sem(n) for n in ("wq_hi_s", "wk_hi_s", "wk_lo_s", "wv_hi_s", "wv_lo_s", "wout_hi_s"))

        block = ctx.enter_context(nc.Block())

        def first(n):
            return FIRST_UNITS[n], proj_bank[n % 4], n

        KEY_COLS, VALUE_COLS = slice(0, INNER), slice(INNER, 2 * INNER)

        def twice(ap):
            return ap.unsqueeze(2).broadcast_to([P, H, 2, DH])

        @block.sync
        def _(sp):
            sp.dma_start(k.x[:, :, :], in_tiles(dram["x"])).then_inc(x_in, 16)
            sp.dma_start(k.ident[:, :], dram["identity"]).then_inc(const_in, 16)
            sp.dma_start(k.ctx_raw[:, :, :], dram["ctx_2048"][0, :, :].rearrange("(t p) c -> p t c", p=P)).then_inc(k.ctx_in, 16)
            for cols, done in ((KEY_COLS, wk_in), (VALUE_COLS, wv_in)):
                sp.dma_start(wkv_raw[:, :, cols], dram["L0_xattn_Wkv"][:, cols].rearrange("(c p) n -> p c n", p=P)).then_inc(done, 16)
                if cols is KEY_COLS:
                    sp.dma_start(wq_raw[:, :, :], dram["L0_xattn_Wq"].rearrange("c (h d) -> c h d", h=H)).then_inc(wq_in, 16)
            for half in range(2):
                sp.dma_start(wout_raw[half * DH:(half + 1) * DH, :, :],
                             dram["L0_xattn_Wout"].rearrange("(h r) d -> r h d", h=H)).then_inc(wout_in, 16)

        @block.scalar
        def _(act):
            act.dma_start(nk_row[:, :], dram["L0_xattn_null_kv"][0, :].partition_broadcast(P)).then_inc(null_in, 16)
            act.dma_start(nv_col[:, :], dram["L0_xattn_null_kv"][1, :].rearrange("(d o) -> d o", o=1)).then_inc(null_in, 16)
            for n in range(CT):
                projected_heads(act, k, *first(n))
            act.wait_ge(wk_in, 16)
            act.activation(k.wkv_hi[:, :, KEY_COLS], wkv_raw[:, :, KEY_COLS], ACT.Copy).then_inc(wk_hi_s, 1)
            act.wait_ge(xnT_ps, 2)
            for i in range(2):
                last = act.activation(xnT[:, i * BANK:(i + 1) * BANK], pT[i][:, :], ACT.Copy)
            last.then_inc(xnT_ready, 1)
            act.wait_ge(wv_in, 16)
            act.activation(k.wkv_hi[:, :, VALUE_COLS], wkv_raw[:, :, VALUE_COLS], ACT.Copy).then_inc(wv_hi_s, 1)
            for n in range(CT, CT + 2):
                projected_heads(act, k, *first(n))
            act.wait_ge(wq_in, 16)
            act.activation(k.wq_hi[:, :, :, :], twice(wq_raw[:, :, :]), ACT.Copy).then_inc(wq_hi_s, 1)
            for n in range(CT + 2, CT + 3):
                projected_heads(act, k, *first(n))
            act.wait_ge(xnT_ready, 1)
            act.activation(k.xnT_hi[:, :], xnT[:, :], ACT.Copy).then_inc(xnT_hi, 1)
            act.wait_ge(wout_in, 32)
            act.activation(k.wout_hi[:, :, :], wout_raw[:, :, :], ACT.Copy).then_inc(wout_hi_s, 1)
            for n in range(CT + 3, len(FIRST_UNITS)):
                projected_heads(act, k, *first(n))
            act.wait_ge(u_ps, 1)
            act.activation(k.u_hi[:, :], pU[:, :], ACT.Copy).then_inc(u_hi_s, 1)

        @block.gpsimd
        def _(pool):
            pool.memset(k.one[:, :], 1.0)
            pool.memset(k.inv_root[:, :], -0.5)
            pool.memset(nv_diag[:, :, :], 0.0).then_inc(diag_zero, 1)
            pool.wait_ge(x_var, 2)
            pool.tensor_scalar(shifted[:, :], mean_var[:, :, 1], LN_EPS, 1.0, ALU.add, ALU.mult).then_inc(x_shifted, 1)
            pool.wait_ge(x_shifted, 1)
            pool.tensor_tensor(rstd[:, :], shifted[:, :], k.inv_root[:, :].broadcast_to([P, TT]), ALU.pow).then_inc(x_rstd, 1)
            pool.wait_ge(wq_hi_s, 1)
            pool.tensor_tensor(k.wq_lo[:, :, :, :], twice(wq_raw[:, :, :]), f(k.wq_hi[:, :, :, :]), ALU.subtract)
            pool.wait_ge(wout_hi_s, 1)
            pool.tensor_tensor(k.wout_lo[:, :, :], wout_raw[:, :, :], f(k.wout_hi[:, :, :]), ALU.subtract)

        @block.vector
        def _(dve):
            dve.wait_ge(x_in, 16)
            token_stats(dve, range(TT), lambda t: k.x[:, t, :], stats, mean_var, x_var, 2)
            projected_tails(dve, k, *first(0))
            dve.wait_ge(x_rstd, 1)
            for t in range(TT):
                last = dve.tensor_scalar(xn[:, t, :], k.x[:, t, :], mean_var[:, t, 0:1], rstd[:, t:t + 1],
                                         ALU.subtract, ALU.mult)
            last.then_inc(xn_ready, 1)
            projected_tails(dve, k, *first(1))
            dve.wait_ge(wk_hi_s, 1)
            dve.tensor_tensor(k.wkv_lo[:, :, KEY_COLS], wkv_raw[:, :, KEY_COLS], f(k.wkv_hi[:, :, KEY_COLS]), ALU.subtract)\
                .then_inc(wk_lo_s, 1)
            dve.wait_ge(null_in, 32)
            dve.wait_ge(diag_zero, 1)
            diagonal = nv_diag[:, :, :].rearrange("p a b -> p (a b)")[:, 0:H * H:H + 1]
            dve.tensor_copy(diagonal, nv_col[:, :].broadcast_to([DH, H])).then_inc(diag_set, 1)
            dve.wait_ge(wq_in, 16)
            dve.tensor_tensor(nk_wq[:, :, :], wq_raw[:, :, :], nk_row[:, :].unsqueeze(1).broadcast_to([P, H, DH]),
                              ALU.mult).then_inc(w0_mul, 1)
            dve.wait_ge(w0_mul, 1)
            dve.tensor_reduce(w0[:, :], nk_wq[:, :, :], AX_X, ALU.add).then_inc(w0_ready, 1)
            dve.wait_ge(wv_hi_s, 1)
            dve.tensor_tensor(k.wkv_lo[:, :, VALUE_COLS], wkv_raw[:, :, VALUE_COLS], f(k.wkv_hi[:, :, VALUE_COLS]), ALU.subtract)\
                .then_inc(wv_lo_s, 1)
            for n in range(CT, CT + 3):
                projected_tails(dve, k, *first(n))
            dve.wait_ge(xnT_hi, 1)
            dve.tensor_tensor(k.xnT_lo[:, :], xnT[:, :], f(k.xnT_hi[:, :]), ALU.subtract)
            dve.wait_ge(s0_ps, 1)
            dve.tensor_scalar(k.s0n[:, :, :], pS0[:, :, :], -X_SCALE, None, ALU.mult)
            for n in range(CT + 3, len(FIRST_UNITS)):
                projected_tails(dve, k, *first(n))
            dve.wait_ge(u_hi_s, 1)
            dve.tensor_tensor(k.u_lo[:, :], pU[:, :], f(k.u_hi[:, :]), ALU.subtract)

        @block.tensor
        def _(pe):
            def unit(n):
                u, out, _ = first(n)
                if n >= 4:
                    pe.wait_ge(k.proj_lo, n - 3)
                if n == CT:
                    pe.wait_ge(k.proj_lo, CT)
                    pe.wait_ge(wk_lo_s, 1)
                if n == CT + 3:
                    pe.wait_ge(wv_lo_s, 1)
                project(pe, k, 0, u, out)

            pe.wait_ge(const_in, 16)
            for n in range(CT):
                unit(n)
            pe.wait_ge(xn_ready, 1)
            for t in range(TT):
                last = pe.transpose(pT[t // 4][:, (t % 4) * P:(t % 4 + 1) * P], xn[:, t, :], k.ident[:, :])
                if t % 4 == 3:
                    last.then_inc(xnT_ps, 1)
            for n in range(CT, CT + 3):
                unit(n)
            pe.wait_ge(w0_ready, 1)
            pe.wait_ge(xnT_ready, 1)
            for t in range(TT):
                last = pe.matmul(pS0[:, t, :], xnT[:, t * P:(t + 1) * P], w0[:, :], start=True, stop=True)
            last.then_inc(s0_ps, 1)
            pe.wait_ge(diag_set, 1)
            pe.wait_ge(wout_in, 32)
            for h in range(H):
                last = pe.matmul(pU[:, :], nv_diag[:, h, :], wout_raw[0:DH, h, :], start=h == 0, stop=h == H - 1)
            last.then_inc(u_ps, 1)
            for n in range(CT + 3, len(FIRST_UNITS)):
                unit(n)


def cross_attention(nc, k, dram):
    with ExitStack() as ctx:
        def sb(name, shape, dt=F32):
            return ctx.enter_context(nc.sbuf_tensor(name, shape, dt))

        def sem(name):
            return ctx.enter_context(nc.semaphore(name))

        def bank(name):
            return ctx.enter_context(nc.psum_tensor(name, [P, BANK], F32))

        keys, vals = k.keys, k.vals
        q_hi, q_lo = (sb(f"q_{s}", [P, 2, N], F32R) for s in ("hi", "lo"))
        neg_max, bias, d0, e0, row_sum, total, rinv = (
            sb(n, [P, H, QT]) for n in ("neg_max", "bias", "d0", "e0", "row_sum", "total", "rinv"))
        p0, p0_batch = sb("p0", [P, TT, H]), sb("p0_batch", [P, QT, H])
        p0T_hi, p0T_lo = (sb(f"p0T_{s}", [H, N], F32R) for s in ("hi", "lo"))
        p_raw = sb("p_raw", [P, 2, QT, M])
        p_norm = sb("p_norm", [P, 2, QT, M])
        pT_hi, pT_lo = (sb(f"pT_{s}", [P, 2, KT, N], F32R) for s in ("hi", "lo"))
        o_hi, o_lo = (sb(f"o_{s}", [P, 2, N], F32R) for s in ("hi", "lo"))

        banks = [bank(f"bank{i}") for i in range(8)]
        s_bank, t_bank, y_bank, proj_bank = banks[0:2], banks[2:4], banks[6], banks[7]
        q_whole, q_bank, o_bank = banks[4], banks[4][:, 0:N], banks[5][:, 0:N]

        bias_in, w_in, tables_in = sem("bias_in"), sem("w_in"), sem("tables_in")
        q_ps, q_hi_s, q_lo_s = sem("q_ps"), sem("q_hi_s"), sem("q_lo_s")
        s_ps, max_s, bias_s, d0_s = (sem(n) for n in ("s_ps", "max_s", "bias_s", "d0_s"))
        p_exp, e0_s, total_s, rinv_s, p0_s, p0_batch_s, p_norm_s = (
            sem(n) for n in ("p_exp", "e0_s", "total_s", "rinv_s", "p0_s", "p0_batch_s", "p_norm_s"))
        t_ps, t_hi_s, t_lo_s = sem("t_ps"), sem("t_hi_s"), sem("t_lo_s")
        o_ps, o_hi_s, o_lo_s, wout_ps = sem("o_ps"), sem("o_hi_s"), sem("o_lo_s"), sem("wout_ps")
        p0_ps, p0_hi_s, p0_lo_s, y_ps, y_out = (sem(n) for n in ("p0_ps", "p0_hi_s", "p0_lo_s", "y_ps", "y_out"))

        FIRST, BODY = range(-4, 2), range(2, H + 2)
        AT = {2: (None, 9), 3: (None, 10), 4: (None, 11), 5: (None, 12), 6: (None, 13), 7: (14, 15), 8: (None, 16), 9: (None, 17),
              10: (NU, NU + 1), 11: (None, NU + 2), 12: (None, NU + 3), 13: (None, NU + 4), 14: (None, NU + 5),
              15: (None, NU + 6), 16: (NU + 7, NU + 8)}

        def units(h, last_batch):
            return [(u, (q_whole, proj_bank)[i]) for i, u in enumerate(AT.get(h, ())) if u is not None and not (last_batch and u >= NU)]

        block = ctx.enter_context(nc.Block())

        def null_score(b, h, t, n=1):
            tiles = k.s0n[:, bass.ds((b + h // H) * QT + t, n), h % H:h % H + 1]
            return tiles.rearrange("p t h -> p (t h)")

        @block.sync
        def _(sp):
            context = dram["ctx_2048"].rearrange("b (t p) c -> p b t c", p=P)
            sp.dma_start(k.bias_row[:, :], dram["L0_xattn_ln_bias"].partition_broadcast(P)).then_inc(bias_in, 16)
            at = 0
            for name, heads in (("L0_ffn_wq", FH), ("L0_ffn_wk", KV), ("L0_ffn_wv", KV)):
                sp.dma_start(k.wqkv[:, at:at + heads, :], dram[name].rearrange("c (h d) -> c h d", d=HD)).then_inc(w_in, 16)
                at += heads
            sp.dma_start(k.ln1_col[:, :], dram["L0_ffn_ln1_w"].rearrange("(d o) -> d o", o=1)).then_inc(w_in, 16)
            sp.dma_start(k.scale_row[:, :], dram["L0_xattn_ln_scale"].partition_broadcast(P)).then_inc(tables_in, 16)
            for table, name in ((k.cos, "rope_cos"), (k.sin, "rope_sin")):
                sp.dma_start(table[:, :, :], dram[name].rearrange("(t p) d -> p t d", p=P)).then_inc(tables_in, 16)
            sp.dma_start(k.wo[:, :], dram["L0_ffn_wo"]).then_inc(tables_in, 16)
            sp.dma_start(k.router[:, :], dram["L0_ffn_router_w"]).then_inc(tables_in, 16)
            sp.dma_start(k.ln2_row[:, :], dram["L0_ffn_ln2_w"].partition_broadcast(P)).then_inc(tables_in, 16)
            sp.dma_start(k.iota[:, :], dram["expert_ids"].partition_broadcast(P)).then_inc(tables_in, 16)
            with sp.Fori(0, B - 1) as b:
                sp.wait_ge(k.proj_ps, b * NU + CT)
                sp.dma_start(k.ctx_raw[:, :, :], context[:, bass.ds(b + 1, 1), :, :].rearrange("p b t c -> p (b t) c")).then_inc(k.ctx_in, 16)
            sp.wait_ge(tables_in, 7 * 16)

        @block.tensor
        def _(pe):
            def unit(b, h, u, out):
                if out is q_whole:
                    pe.wait_ge(q_lo_s, b * H + h + 4)
                elif AT[h][0] is not None:
                    pe.wait_ge(k.proj_lo, b * NU + u - 1)
                else:
                    pe.wait_ge(k.proj_lo, b * NU + u)
                if h == 2:
                    pe.wait_ge(p0_lo_s, b + 1)
                project(pe, k, b, u, out)

            def project_q(b, h, last_batch):
                if h >= 1:
                    pe.wait_ge(q_lo_s, b * H + h)
                for u, out in units(h - 4, last_batch):
                    if out is q_whole:
                        pe.wait_ge(k.proj_lo, b * NU + u + 1)
                for i, (w, x) in enumerate(((k.wq_hi, k.xnT_hi), (k.wq_hi, k.xnT_lo), (k.wq_lo, k.xnT_hi))):
                    last = pe.matmul(q_bank, w[:, h % H, :, :].rearrange("p a d -> p (a d)"),
                                     x[:, bass.ts(b + h // H, N)], start=i == 0, stop=i == 2)
                last.then_inc(q_ps, 1)

            def scores(b, h):
                pe.wait_ge(q_lo_s, b * H + h + 1)
                if h % 2 == 0:
                    pe.wait_ge(k.proj_lo, (b + h // H) * NU + UNITS.index(("k", h % H // 2)) + 1)
                for t in range(QT):
                    if h >= 1:
                        pe.wait_ge(p_exp, b * H * QT + QT * (h - 1) + t + 1)
                    for i, q in enumerate((q_hi, q_lo)):
                        last = pe.matmul(s_bank[t][:, :], q[:, h % 2, t * P:(t + 1) * P], keys[:, h % H, :],
                                         start=i == 0, stop=i == 1)
                    last.then_inc(s_ps, 1)

            def transpose_probs(b, h):
                pe.wait_ge(p_norm_s, b * H * QT + QT * (h + 1))
                for half in range(2):
                    g = 2 * h + half
                    if h >= 1:
                        pe.wait_ge(t_lo_s, b * 2 * H + g - 1)
                    for j in range(2):
                        for t in range(QT):
                            kt = 2 * half + j
                            last = pe.transpose(t_bank[half][:, j * N + t * P:j * N + (t + 1) * P],
                                                p_norm[:, h % 2, t, kt * P:(kt + 1) * P], k.ident[:, :])
                    last.then_inc(t_ps, 1)

            def weighted_values(b, h):
                pe.wait_ge(t_lo_s, b * 2 * H + 2 * h + 2)
                if h % (H // 2) == 0:
                    pe.wait_ge(k.proj_lo, (b + h // H) * NU + UNITS.index(("v", h % H // (H // 2), KT - 1)) + 1)
                if h >= 1:
                    pe.wait_ge(o_lo_s, b * H + h)
                for kt in range(KT):
                    for i, x in enumerate((pT_hi, pT_lo)):
                        last = pe.matmul(o_bank, vals[:, kt, h % H, :], x[:, h % 2, kt, :],
                                         start=kt == 0 and i == 0, stop=kt == KT - 1 and i == 1)
                last.then_inc(o_ps, 1)

            def project_out(b, h):
                pe.wait_ge(o_lo_s, b * H + h + 1)
                if h == 0:
                    pe.wait_ge(y_out, b + 1)
                for i, (w, x) in enumerate(((k.wout_hi, o_hi), (k.wout_hi, o_lo), (k.wout_lo, o_hi))):
                    last = pe.matmul(y_bank[:, 0:N], w[:, h, :], x[:, h % 2, :],
                                     start=h == 0 and i == 0, stop=False)
                last.then_inc(wout_ps, 1)

            def null_probs(b, last_batch):
                pe.wait_ge(p0_batch_s, b + 1)
                pe.wait_ge(k.proj_lo, (b + 1) * NU + (0 if last_batch else 9))
                for t in range(QT):
                    last = pe.transpose(proj_bank[0:H, t * P:(t + 1) * P], p0_batch[:, t, :], k.ident[:, :])
                last.then_inc(p0_ps, 1)

            def null_values(b):
                pe.wait_ge(p0_lo_s, b + 2)
                for i, (w, x) in enumerate(((k.u_hi, p0T_hi), (k.u_hi, p0T_lo), (k.u_lo, p0T_hi))):
                    last = pe.matmul(y_bank[:, 0:N], w[:, :], x[:, :], start=False, stop=i == 2)
                last.then_inc(y_ps, 1)

            def steps(b, which, last_batch=False):
                end = H if last_batch else which.stop + 4
                for h in which:
                    if 0 <= h < end:
                        transpose_probs(b, h)
                    if h == H + 1:
                        null_probs(b, last_batch)
                    for u, out in units(h, last_batch):
                        unit(b, h, u, out)
                    if 0 <= h - 1 < end:
                        weighted_values(b, h - 1)
                    if 0 <= h - 2 < end:
                        project_out(b, h - 2)
                    if h + 4 < end:
                        project_q(b, h + 4, last_batch)
                    if 0 <= h + 3 < end:
                        scores(b, h + 3)
                    if h == H + 1:
                        null_values(b)

            steps(0, FIRST)
            with pe.Fori(0, B - 1) as b:
                steps(b, BODY)
            steps(B - 1, BODY, True)

        @block.scalar
        def _(act):
            def q_head(b, h):
                act.wait_ge(q_ps, b * H + h + 1)
                if h >= 2:
                    act.wait_ge(s_ps, b * H * QT + QT * (h - 1))
                act.activation(q_hi[:, h % 2, :], q_bank, ACT.Copy).then_inc(q_hi_s, 1)

            def exponential(b, h, t):
                act.wait_ge(bias_s, b * H * QT + QT * h + t + 1)
                if h >= 2:
                    act.wait_ge(p_norm_s, b * H * QT + QT * (h - 2) + t + 1)
                act.activation(p_raw[:, h % 2, t, :], s_bank[t][:, :], ACT.Exp,
                               bias=bias[:, h % H, t:t + 1], scale=X_SCALE, accum_out=row_sum[:, h % H, t:t + 1]).then_inc(p_exp, 1)

            def null_exponential(b, h):
                act.wait_ge(d0_s, b * H + h + 1)
                act.activation(e0[:, h % H, :], d0[:, h % H, :], ACT.Exp).then_inc(e0_s, 1)

            def o_head(b, h):
                act.wait_ge(o_ps, b * H + h + 1)
                if h >= 2:
                    act.wait_ge(wout_ps, b * H + h - 1)
                act.activation(o_hi[:, h % 2, :], o_bank, ACT.Copy).then_inc(o_hi_s, 1)

            def probs_head(b, h, half):
                g = 2 * h + half
                act.wait_ge(t_ps, b * 2 * H + g + 1)
                if h >= 2:
                    act.wait_ge(o_ps, b * H + h - 1)
                act.activation(pT_hi[:, h % 2, 2 * half:2 * half + 2, :],
                               t_bank[half][:, :].rearrange("p (j n) -> p j n", j=2), ACT.Copy).then_inc(t_hi_s, 1)

            def steps(b, which, last_batch=False):
                end = H if last_batch else which.stop + 3
                for h in which:
                    if 0 <= h + 3 < end:
                        q_head(b, h + 3)
                    if 0 <= h < end:
                        probs_head(b, h, 0)
                        probs_head(b, h, 1)
                    if h == H + 1:
                        act.wait_ge(p0_ps, b + 1)
                        act.activation(p0T_hi[:, :], proj_bank[0:H, 0:N], ACT.Copy).then_inc(p0_hi_s, 1)
                    for u, src in units(h, last_batch):
                        if src is q_whole:
                            projected_heads(act, k, u, src, b * NU + u)
                    if 0 <= h + 2 < end:
                        exponential(b, h + 2, 0)
                        exponential(b, h + 2, 1)
                    for u, src in units(h, last_batch):
                        if src is proj_bank:
                            projected_heads(act, k, u, src, b * NU + u)
                    if 0 <= h + 2 < end:
                        null_exponential(b, h + 2)
                    if 0 <= h - 1 < end:
                        o_head(b, h - 1)
                    if h == H + 1:
                        act.wait_ge(y_ps, b + 1)
                        act.activation(k.yT[:, bass.ts(b, N)], y_bank[:, 0:N], ACT.Copy).then_inc(y_out, 1)

            act.sem_inc(y_out, 1)
            steps(0, FIRST)
            with act.Fori(0, B - 1) as b:
                steps(b, BODY)
            steps(B - 1, BODY, True)

        @block.vector
        def _(dve):
            def q_tail(b, h):
                dve.wait_ge(q_hi_s, b * H + h + 1)
                if h >= 2:
                    dve.wait_ge(s_ps, b * H * QT + QT * (h - 1))
                dve.tensor_tensor(q_lo[:, h % 2, :], q_bank, f(q_hi[:, h % 2, :]), ALU.subtract)\
                    .then_inc(q_lo_s, 1)

            def maximum(b, h, t):
                dve.wait_ge(s_ps, b * H * QT + QT * h + t + 1)
                dve.tensor_reduce(neg_max[:, h % H, t:t + 1], s_bank[t][:, :], AX_X, ALU.max, negate=True).then_inc(max_s, 1)

            def shift(b, h, t):
                dve.wait_ge(max_s, b * H * QT + QT * h + t + 1)
                dve.scalar_tensor_tensor(bias[:, h % H, t:t + 1], neg_max[:, h % H, t:t + 1], X_SCALE, null_score(b, h, t),
                                         ALU.mult, ALU.min).then_inc(bias_s, 1)

            def inverse_sum(b, h):
                dve.wait_ge(total_s, b * H + h + 1)
                dve.reciprocal(rinv[:, h % H, :], total[:, h % H, :]).then_inc(rinv_s, 1)

            def o_tail(b, h):
                dve.wait_ge(o_hi_s, b * H + h + 1)
                if h >= 2:
                    dve.wait_ge(wout_ps, b * H + h - 1)
                dve.tensor_tensor(o_lo[:, h % 2, :], o_bank, f(o_hi[:, h % 2, :]), ALU.subtract)\
                    .then_inc(o_lo_s, 1)

            def probs_tail(b, h, half):
                g = 2 * h + half
                dve.wait_ge(t_hi_s, b * 2 * H + g + 1)
                if h >= 2:
                    dve.wait_ge(o_ps, b * H + h - 1)
                dve.tensor_tensor(pT_lo[:, h % 2, 2 * half:2 * half + 2, :],
                                  t_bank[half][:, :].rearrange("p (j n) -> p j n", j=2),
                                  f(pT_hi[:, h % 2, 2 * half:2 * half + 2, :]), ALU.subtract).then_inc(t_lo_s, 1)

            def steps(b, which, last_batch=False):
                end = H if last_batch else which.stop + 3
                for h in which:
                    if 0 <= h + 2 < end:
                        maximum(b, h + 2, 0)
                    if 0 <= h + 3 < end:
                        q_tail(b, h + 3)
                    if 0 <= h + 2 < end:
                        shift(b, h + 2, 0)
                        maximum(b, h + 2, 1)
                        shift(b, h + 2, 1)
                    if 0 <= h < end:
                        probs_tail(b, h, 0)
                        probs_tail(b, h, 1)
                    if h == H - 1:
                        dve.wait_ge(p0_s, (b + 1) * H)
                        dve.tensor_copy(p0_batch[:, :, :], p0[:, bass.ts(b, QT), :]).then_inc(p0_batch_s, 1)
                    if h == H + 1:
                        dve.wait_ge(p0_hi_s, b + 1)
                        dve.tensor_tensor(p0T_lo[:, :], proj_bank[0:H, 0:N], f(p0T_hi[:, :]), ALU.subtract).then_inc(p0_lo_s, 1)
                    for u, src in units(h, last_batch):
                        projected_tails(dve, k, u, src, b * NU + u)
                    if 0 <= h + 2 < end:
                        inverse_sum(b, h + 2)
                    if 0 <= h - 1 < end:
                        o_tail(b, h - 1)

            dve.sem_inc(p0_lo_s, 1)
            steps(0, FIRST)
            with dve.Fori(0, B - 1) as b:
                steps(b, BODY)
            steps(B - 1, BODY, True)

        @block.gpsimd
        def _(pool):
            def normalise_probs(b, h):
                pool.wait_ge(bias_s, b * H * QT + QT * (h + 1))
                pool.tensor_tensor(d0[:, h % H, :], bias[:, h % H, :], null_score(b, h, 0, QT), ALU.subtract).then_inc(d0_s, 1)
                pool.wait_ge(p_exp, b * H * QT + QT * (h + 1))
                pool.wait_ge(e0_s, b * H + h + 1)
                pool.tensor_tensor(total[:, h % H, :], row_sum[:, h % H, :], e0[:, h % H, :], ALU.add).then_inc(total_s, 1)
                if h >= 2:
                    pool.wait_ge(t_ps, b * 2 * H + 2 * (h - 1))
                pool.wait_ge(rinv_s, b * H + h + 1)
                pool.tensor_tensor(p0[:, bass.ds((b + h // H) * QT, QT), h % H:h % H + 1].rearrange("p t h -> p (t h)"),
                                   e0[:, h % H, :], rinv[:, h % H, :], ALU.mult).then_inc(p0_s, 1)
                for t in range(QT):
                    pool.tensor_scalar(p_norm[:, h % 2, t, :], p_raw[:, h % 2, t, :], rinv[:, h % H, t:t + 1], 1.0,
                                       ALU.mult, ALU.mult).then_inc(p_norm_s, 1)

            pool.wait_ge(bias_in, 16)
            pool.tensor_tensor(k.x[:, :, :], k.x[:, :, :], over_tiles(k.bias_row), ALU.add)
            pool.wait_ge(w_in, 4 * 16)
            pool.tensor_tensor(k.wqkv[:, :, :], k.wqkv[:, :, :], k.ln1_col[:, :].unsqueeze(2).broadcast_to([P, FH + 2 * KV, HD]),
                               ALU.mult)
            for h in range(2):
                normalise_probs(0, h)
            with pool.Fori(0, B - 1) as b:
                for h in BODY:
                    normalise_probs(b, h)
            for h in range(2, H):
                normalise_probs(B - 1, h)


def stage_helpers(nc, ctx):
    def sb(name, shape, dt=F32):
        return ctx.enter_context(nc.sbuf_tensor(name, shape, dt))

    def sem(name):
        return ctx.enter_context(nc.semaphore(name))

    def bank(name, shape=(P, BANK)):
        return ctx.enter_context(nc.psum_tensor(name, list(shape), F32))

    return sb, sem, bank


def over_tiles(row, tiles=TT):
    return row[:, :].unsqueeze(1).broadcast_to([P, tiles, D])


def residual_and_projections(nc, k, dram):
    with ExitStack() as ctx:
        sb, sem, bank = stage_helpers(nc, ctx)
        yn, h = sb("yn", [P, TT, D]), sb("h_rms", [P, TT, D])
        hT = sb("hT", [P, TOK])
        stats_y, stats_x = sb("stats_y", [P, TT, 6]), sb("stats_x", [P, TT, 6])
        mv_y, mv_x = sb("mv_y", [P, TT, 2]), k.mv_x
        rstd_y, square, var_z, rms_z, to_h = (sb(n, [P, TT]) for n in ("rstd_y", "square", "var_z", "rms_z", "to_h"))
        rstd_x = k.rstd_x
        turned = sb("turned", [P, TT, FH + KV, HD])
        pY = [bank(f"p_y{i}", (P, 4, D)) for i in range(2)]
        pH = [bank(f"p_h{i}") for i in range(2)]
        pQ = [bank(f"p_qkv{i}", (P, 2, FH + 2 * KV, HD)) for i in range(4)]
        y_ps, y_var, y_rstd, yn_s, x1_s, x1_var, to_h_s, pool_step = (
            sem(n) for n in ("y_ps3", "y_var", "y_rstd", "yn_s", "x1_s", "x1_var", "to_h_s", "pool_step3"))
        h_s, hT_ps, hT_s, qkv_ps, qkv_s = (sem(n) for n in ("h_s", "hT_ps", "hT_s", "qkv_ps", "qkv_s"))
        turned_s = [sem(f"turned_{e}") for e in ("dve", "pool")]
        cos_s = [sem(f"cos_{e}") for e in ("dve", "pool")]
        block = ctx.enter_context(nc.Block())

        def half(i):
            return range(4 * i, 4 * i + 4)

        def rotate(engine, which, i, heads, dst):
            n = heads.stop - heads.start
            engine.wait_ge(qkv_s, 2 * i + 2)
            for par in range(QT):
                tiles = slice(4 * i + par, 4 * i + 4, QT)
                src, out = k.qkv[:, tiles, heads, :], turned[:, tiles, heads, :]
                sin_b = k.sin[:, par, :].unsqueeze(1).unsqueeze(1)
                for a, b in ((0, HD // 2), (HD // 2, 0)):
                    last = engine.tensor_tensor(out[:, :, :, a:a + HD // 2], src[:, :, :, b:b + HD // 2],
                                                sin_b[:, :, :, a:a + HD // 2].broadcast_to([P, 2, n, HD // 2]), ALU.mult)
            last.then_inc(turned_s[which], 1)
            engine.wait_ge(turned_s[which], i + 1)
            for par in range(QT):
                src = k.qkv[:, 4 * i + par:4 * i + 4:QT, heads, :]
                last = engine.tensor_tensor(src, src, k.cos[:, par, :].unsqueeze(1).unsqueeze(1).broadcast_to([P, 2, n, HD]), ALU.mult)
            last.then_inc(cos_s[which], 1)
            engine.wait_ge(cos_s[which], i + 1)
            tiles = slice(4 * i, 4 * i + 4)
            engine.tensor_tensor(dst[:, tiles, :, :], k.qkv[:, tiles, heads, :], turned[:, tiles, heads, :], ALU.add)

        @block.gpsimd
        def _(pool):
            count = [0]

            def link(ins):
                count[0] += 1
                ins.then_inc(pool_step, 1)
                pool.wait_ge(pool_step, count[0])

            def inverse_root(dst, src, eps):
                link(pool.tensor_scalar(dst, src, eps, 1.0, ALU.add, ALU.mult))
                return pool.tensor_tensor(dst, dst, k.inv_root[:, :].broadcast_to([P, TT // 2]), ALU.pow)

            for i in range(2):
                t = slice(4 * i, 4 * i + 4)
                pool.wait_ge(y_var, 2 * i + 2)
                inverse_root(rstd_y[:, t], mv_y[:, t, 1], RMS_EPS).then_inc(y_rstd, 1)
            for i in range(2):
                t = slice(4 * i, 4 * i + 4)
                pool.wait_ge(x1_var, 2 * i + 2)
                link(inverse_root(rstd_x[:, t], mv_x[:, t, 1], LN_EPS))
                link(pool.tensor_tensor(square[:, t], rstd_x[:, t], rstd_x[:, t], ALU.mult))
                link(pool.tensor_tensor(var_z[:, t], square[:, t], mv_x[:, t, 1], ALU.mult))
                link(inverse_root(rms_z[:, t], var_z[:, t], RMS_EPS))
                pool.tensor_tensor(to_h[:, t], rms_z[:, t], rstd_x[:, t], ALU.mult).then_inc(to_h_s, 1)
            for i in range(2):
                rotate(pool, 1, i, slice(FH, FH + KV), k.rk)

        @block.scalar
        def _(act):
            for i in range(2):
                act.wait_ge(hT_ps, i + 1)
                act.activation(hT[:, i * BANK:(i + 1) * BANK], pH[i][:, :], ACT.Copy).then_inc(hT_s, 1)
            for i in range(4):
                act.wait_ge(qkv_ps, i + 1)
                act.activation(k.qkv[:, 2 * i:2 * i + 2, :, :], pQ[i][:, :, :, :], ACT.Copy).then_inc(qkv_s, 1)

        @block.tensor
        def _(pe):
            for t in range(TT):
                last = pe.transpose(pY[t // 4][:, t % 4, :], k.yT[:, t * P:(t + 1) * P], k.ident[:, :])
                if t % 4 == 3:
                    last.then_inc(y_ps, 1)
            for i in range(2):
                pe.wait_ge(h_s, i + 1)
                for t in half(i):
                    last = pe.transpose(pH[i][:, (t % 4) * P:(t % 4 + 1) * P], h[:, t, :], k.ident[:, :])
                last.then_inc(hT_ps, 1)
            for t in range(TT):
                if t % 4 == 0:
                    pe.wait_ge(hT_s, t // 4 + 1)
                last = pe.matmul(pQ[t // 2][:, t % 2, :, :], hT[:, t * P:(t + 1) * P], k.wqkv[:, :, :], start=True, stop=True)
                if t % 2:
                    last.then_inc(qkv_ps, 1)

        @block.vector
        def _(dve):
            for i in range(2):
                dve.wait_ge(y_ps, i + 1)
                token_stats(dve, half(i), lambda t: pY[i][:, t % 4, :], stats_y, mv_y, y_var, 2 * i + 2)
            for i in range(2):
                for t in half(i):
                    last = dve.scalar_tensor_tensor(yn[:, t, :], pY[i][:, t % 4, :], mv_y[:, t, 0:1], k.scale_row[:, :],
                                                    ALU.subtract, ALU.mult)
                last.then_inc(yn_s, 1)
                dve.wait_ge(yn_s, i + 1)
                dve.wait_ge(y_rstd, i + 1)
                for t in half(i):
                    last = dve.scalar_tensor_tensor(k.x1[:, t, :], yn[:, t, :], rstd_y[:, t:t + 1], k.x[:, t, :],
                                                    ALU.mult, ALU.add)
                last.then_inc(x1_s, 1)
                dve.wait_ge(x1_s, i + 1)
                token_stats(dve, half(i), lambda t: k.x1[:, t, :], stats_x, mv_x, x1_var, 2 * i + 2)
            for i in range(2):
                dve.wait_ge(to_h_s, i + 1)
                for t in half(i):
                    last = dve.tensor_scalar(h[:, t, :], k.x1[:, t, :], mv_x[:, t, 0:1], to_h[:, t:t + 1], ALU.subtract, ALU.mult)
                last.then_inc(h_s, 1)
            for i in range(2):
                rotate(dve, 0, i, slice(0, FH), k.rq)


def self_attention(nc, k, dram):
    with ExitStack() as ctx:
        sb, sem, bank = stage_helpers(nc, ctx)
        STACK = 4 * HD
        GROUPS = FH * STACK // P
        VW = 2 * HD + 1
        q_quad = sb("q_quad", [P, 2, QT, FH, 4, HD], F32R)
        k_quad = sb("k_quad", [P, 2, QT, FH, 4, HD], F32R)
        v_all, v_pair = sb("v_all", [P, TT, KV, VW], F32R), sb("v_pair", [P, QT, KV, VW], F32R)
        qT_all, kT_all = sb("qT_all", [P, GROUPS, TOK], F32R), sb("kT_all", [P, GROUPS, TOK], F32R)
        qT, kT = sb("qT", [P, GROUPS, N], F32R), sb("kT", [P, GROUPS, N], F32R)
        mask_f, mask = sb("mask_f", [P, 2 * P]), sb("mask", [P, 2 * P], BF16)
        ident_b = sb("ident_b", [P, P], BF16)
        neg_max, rinv = sb("neg_max4", [P, QT, FH]), sb("rinv4", [P, QT * REP])
        p_raw = sb("p_raw4", [P, 4, REP, QT, N])
        KEYS0, KEYS1 = REP * N, REP * P
        pT_hi, pT_lo = sb("pT_hi4", [P, 2, KEYS0 + KEYS1], F32R), sb("pT_lo4", [P, 2, KEYS0 + KEYS1], F32R)
        oT = sb("oT", [VW, KV, REP, N])
        ao_sum = sb("ao_sum", [P, QT * REP, HD])
        s_pair = [bank(f"s_pair{i}", (P, REP, BANK)) for i in range(2)]
        s_bank = [s[:, j, :] for s in s_pair for j in range(REP)]
        a_bank, b_bank, o_bank = [bank(f"a_bank{i}") for i in range(2)], bank("b_bank"), bank("o_bank4")
        G = KEYS1

        mask_in, consts_s = sem("mask_in"), sem("consts_s")
        quad_hi, quad_lo, qkT_ps, qT_all_s, kT_all_s, v_hi_s, v_lo_s, group_s, v_s = (
            sem(n) for n in ("quad_hi", "quad_lo", "qkT_ps", "qT_all_s", "kT_all_s", "v_hi_s4", "v_lo_s4", "group_s", "v_s"))
        s_ps, max_s, p_exp, t_ps, t_hi_s, t_lo_s, o_ps, o_s, g_ps, sum_s, ao_s = (
            sem(f"{n}4") for n in ("s_ps", "max_s", "p_exp", "t_ps", "t_hi_s", "t_lo_s", "o_ps", "o_s", "g_ps",
                                   "sum_s", "ao_s"))
        FIRST, BODY = range(-3, 3), range(3, KV + 3)
        block = ctx.enter_context(nc.Block())

        def keys1(ap):
            return ap.rearrange("p (j t n) -> p j t n", j=REP, t=QT)[:, :, 1, :]

        def diagonal(ap):
            return ap.rearrange("p (c n) -> p c n", n=P)[:, 0::QT + 1, :]

        def key_slot(b, a):
            return k_quad[:, b % 2, :, :, a, :].rearrange("p t (g r) d -> p (t g) r d", r=REP)

        def key_heads(b):
            return k.rk[:, b * QT:(b + 1) * QT, :, :].rearrange("p t g d -> p (t g) d").unsqueeze(2)\
                .broadcast_to([P, QT * KV, REP, HD])

        @block.sync
        def _(sp):
            sp.dma_start(mask_f[:, :], dram["causal"]).then_inc(mask_in, 16)
            fetch_pair(sp, k, dram, 0)

        @block.gpsimd
        def _(pool):
            ones = k.one[:, :]

            def group(b, g):
                for dst, src in ((qT, qT_all), (kT, kT_all)):
                    last = pool.tensor_tensor(dst[:, g, :], f(src[:, g, bass.ds(b * N, N)]), ones.broadcast_to([P, N]), ALU.mult)
                last.then_inc(group_s, 1)

            def values(b, half):
                heads = slice(half * KV // 2, (half + 1) * KV // 2)
                pool.tensor_tensor(v_pair[:, :, heads, :], f(v_all[:, bass.ds(b * QT, QT), heads, :]),
                                   ones.unsqueeze(2).unsqueeze(3).broadcast_to([P, QT, KV // 2, VW]), ALU.mult).then_inc(v_s, 1)

            pool.wait_ge(qT_all_s, 1)
            pool.wait_ge(kT_all_s, 1)
            for g in range(GROUPS):
                group(0, g)
            pool.wait_ge(v_lo_s, 1)
            for half in range(2):
                values(0, half)
            pool.wait_ge(qT_all_s, B)
            pool.wait_ge(kT_all_s, B)
            split_pair(pool, k, 0, 0)
            with pool.Fori(0, B - 1) as b:
                for g in range(GROUPS):
                    pool.wait_ge(s_ps, b * KV + 2 * g + 2)
                    group(b + 1, g)
                for half in range(2):
                    pool.wait_ge(o_ps, b * KV + (half + 1) * (KV // 2))
                    values(b + 1, half)
            for t in range(TT):
                pool.tensor_scalar(k.z[:, t, :], k.x1[:, t, :], k.mv_x[:, t, 0:1], k.rstd_x[:, t:t + 1], ALU.subtract, ALU.mult)

        @block.tensor
        def _(pe):
            def features_first(b, u):
                src = q_quad if u < 2 else k_quad
                pe.wait_ge(quad_lo, b + 1)
                if b >= 1:
                    pe.wait_ge(qT_all_s if u < 2 else kT_all_s, b)
                for i in range(2):
                    g = 2 * (u % 2) + i
                    for t in range(QT):
                        last = pe.transpose(s_bank[u][:, i * N + t * P:i * N + (t + 1) * P],
                                            f(src[:, b % 2, t, 4 * g:4 * g + 4, :, :]).rearrange("p h a d -> p (h a d)"),
                                            k.ident[:, :])
                last.then_inc(qkT_ps, 1)

            def scores(b, p):
                if p % 2 == 0:
                    pe.wait_ge(group_s, b * GROUPS + p // 2 + 1)
                if p >= 2:
                    pe.wait_ge(p_exp, b * KV + p - 1)
                group = p % KV // 2
                for j in range(REP):
                    r = STACK * ((REP * p + j) % 4)
                    out = s_bank[(p % 2) * REP + j]
                    for t in range(QT):
                        pe.matmul(out[:, t * N:(t + 1) * N], qT[r:r + STACK, group, t * P:(t + 1) * P],
                                  kT[r:r + STACK, group, :], start=t == 0, stop=False)
                for j in range(REP):
                    last = pe.matmul(diagonal(s_bank[(p % 2) * REP + j]), ident_b[:, :], mask[:, :], start=False, stop=True)
                last.then_inc(s_ps, 1)

            def transpose_probs(b, p):
                pe.wait_ge(p_exp, b * KV + p + 1)
                if p >= 2:
                    pe.wait_ge(t_lo_s, b * 2 * KV + 2 * (p - 1) - 1)
                for j in range(REP):
                    for t in range(QT):
                        last = pe.transpose(a_bank[p % 2][:, j * N + t * P:j * N + (t + 1) * P], p_raw[:, p % 4, j, t, 0:P],
                                            k.ident[:, :])
                last.then_inc(t_ps, 1)
                if p >= 1:
                    pe.wait_ge(t_lo_s, b * 2 * KV + 2 * p)
                if p >= 3:
                    pe.wait_ge(o_s, b * KV + p - 2)
                    tokens_first(b, p - 3)
                for j in range(REP):
                    last = pe.transpose(b_bank[:, j * P:(j + 1) * P], p_raw[:, p % 4, j, 1, P:2 * P], k.ident[:, :])
                last.then_inc(t_ps, 1)

            def tokens_first(b, p):
                for t in range(QT):
                    for j in range(REP):
                        out, tile = b_bank[:, G + (t * REP + j) * VW:G + (t * REP + j + 1) * VW], oT[:, p, j, t * P:(t + 1) * P]
                        if t + j == 0:
                            pe.matmul(out, tile, k.ident[0:VW, 0:VW], start=True, stop=True)
                        else:
                            last = pe.transpose(out, tile, k.ident[0:VW, 0:VW])
                last.then_inc(g_ps, 1)

            def weighted_values(b, p):
                if p % (KV // 2) == 0:
                    pe.wait_ge(v_s, b * 2 + p // (KV // 2) + 1)
                pe.wait_ge(t_lo_s, b * 2 * KV + 2 * p + 2)
                if p >= 1:
                    pe.wait_ge(o_s, b * KV + p)
                for i, x in enumerate((pT_hi, pT_lo)):
                    pe.matmul(o_bank[0:VW, :], v_pair[:, 0, p % KV, :], x[:, p % 2, 0:KEYS0], start=i == 0, stop=False)
                for i, x in enumerate((pT_hi, pT_lo)):
                    last = pe.matmul(keys1(o_bank[0:VW, :]), v_pair[:, 1, p % KV, :], x[:, p % 2, KEYS0:],
                                     start=False, stop=i == 1)
                last.then_inc(o_ps, 1)

            def steps(b, which, last_batch=False):
                end = KV if last_batch else which.stop + 3
                for p in which:
                    if 0 <= p < end:
                        transpose_probs(b, p)
                    elif p >= end:
                        pe.wait_ge(o_s, b * KV + p - 2)
                        pe.wait_ge(t_lo_s, (b + 1) * 2 * KV)
                        pe.wait_ge(sum_s, b * KV + p - 3)
                        tokens_first(b, p - 3)
                    if 0 <= p - 1 < end:
                        weighted_values(b, p - 1)
                    if p + 3 < end:
                        scores(b, p + 3)

            for b in range(B):
                for u in range(4):
                    features_first(b, u)
            pe.wait_ge(consts_s, 2)
            pe.wait_ge(kT_all_s, B)
            pe.wait_ge(qT_all_s, B)
            steps(0, FIRST)
            with pe.Fori(0, B - 1) as b:
                steps(b, BODY)
            steps(B - 1, BODY, True)

        @block.scalar
        def _(act):
            def quad_heads(b):
                if b >= 2:
                    act.wait_ge(qkT_ps, (b - 1) * 4)
                for a in (0, 2):
                    act.activation(q_quad[:, b % 2, :, :, a, :], k.rq[:, b * QT:(b + 1) * QT, :, :], ACT.Copy, scale=F_SCALE)
                for a in (0, 1):
                    last = act.activation(key_slot(b, a), key_heads(b), ACT.Copy)
                last.then_inc(quad_hi, 1)

            def queries_first(b):
                for i in range(2):
                    act.wait_ge(qkT_ps, b * 4 + i + 1)
                    last = act.activation(qT_all[:, 2 * i:2 * i + 2, b * N:(b + 1) * N],
                                          s_bank[i][:, :].rearrange("p (g n) -> p g n", g=2), ACT.Copy)
                last.then_inc(qT_all_s, 1)

            def exponentials(b, p):
                act.wait_ge(max_s, b * KV + p + 1)
                if p >= 4:
                    act.wait_ge(t_ps, b * 2 * KV + 2 * (p - 3))
                for j in range(REP):
                    for t in range(QT):
                        n = (t + 1) * P
                        last = act.activation(p_raw[:, p % 4, j, t, 0:n], s_bank[(p % 2) * REP + j][:, t * N:t * N + n], ACT.Exp,
                                              bias=neg_max[:, t, REP * (p % KV) + j:REP * (p % KV) + j + 1])
                last.then_inc(p_exp, 1)

            def probs_head(b, p):
                act.wait_ge(t_ps, b * 2 * KV + 2 * p + 1)
                if p >= 2:
                    act.wait_ge(o_ps, b * KV + p - 1)
                act.activation(pT_hi[:, p % 2, 0:KEYS0], a_bank[p % 2][:, :], ACT.Copy).then_inc(t_hi_s, 1)
                act.wait_ge(t_ps, b * 2 * KV + 2 * p + 2)
                act.activation(pT_hi[:, p % 2, KEYS0:], b_bank[:, 0:KEYS1], ACT.Copy).then_inc(t_hi_s, 1)

            def output_copy(b, p):
                act.wait_ge(o_ps, b * KV + p + 1)
                act.activation(oT[:, p % KV, :, :].rearrange("p j n -> p (j n)"), o_bank[0:VW, :], ACT.Copy).then_inc(o_s, 1)

            def steps(b, which, last_batch=False):
                end = KV if last_batch else which.stop + 2
                for p in which:
                    if 0 <= p < end:
                        probs_head(b, p)
                    if 0 <= p + 2 < end:
                        exponentials(b, p + 2)
                    if 0 <= p - 1 < end and p % 2:
                        output_copy(b, p - 1)

            quad_heads(0)
            act.activation(v_all[:, :, :, 0:HD], k.qkv[:, :, FH + KV:, :], ACT.Copy)
            act.activation(v_all[:, :, :, 2 * HD], k.one[:, :].unsqueeze(2).broadcast_to([P, TT, KV]), ACT.Copy)\
                .then_inc(v_hi_s, 1)
            for b in range(B):
                if b + 1 < B:
                    quad_heads(b + 1)
                queries_first(b)
            act.wait_ge(mask_in, 16)
            act.activation(mask[:, :], mask_f[:, :], ACT.Copy).then_inc(consts_s, 1)
            act.activation(ident_b[:, :], k.ident[:, :], ACT.Copy).then_inc(consts_s, 1)
            steps(0, FIRST)
            with act.Fori(0, B - 1) as b:
                steps(b, BODY)
            steps(B - 1, BODY, True)

        @block.vector
        def _(dve):
            def quad_tails(b):
                dve.wait_ge(quad_hi, b + 1)
                for a in (1, 3):
                    dve.scalar_tensor_tensor(q_quad[:, b % 2, :, :, a, :].rearrange("p t h d -> p (t h) d"),
                                             k.rq[:, b * QT:(b + 1) * QT, :, :].rearrange("p t h d -> p (t h) d"), F_SCALE,
                                             f(q_quad[:, b % 2, :, :, 0, :]).rearrange("p t h d -> p (t h) d"),
                                             ALU.mult, ALU.subtract)
                for a in (2, 3):
                    last = dve.tensor_tensor(key_slot(b, a), key_heads(b), f(key_slot(b, 0)), ALU.subtract)
                last.then_inc(quad_lo, 1)

            def keys_first(b):
                for i in range(2):
                    dve.wait_ge(qkT_ps, b * 4 + i + 3)
                    last = dve.tensor_copy(kT_all[:, 2 * i:2 * i + 2, b * N:(b + 1) * N],
                                           s_bank[2 + i][:, :].rearrange("p (g n) -> p g n", g=2))
                last.then_inc(kT_all_s, 1)

            def maxima(b, p):
                dve.wait_ge(s_ps, b * KV + p + 1)
                for t in range(QT):
                    last = dve.tensor_reduce(neg_max[:, t, REP * (p % KV):REP * (p % KV) + REP],
                                             s_pair[p % 2][:, :, t * N:t * N + (t + 1) * P], AX_X, ALU.max, negate=True)
                last.then_inc(max_s, 1)

            def probs_tail(b, p):
                dve.wait_ge(t_hi_s, b * 2 * KV + 2 * p + 1)
                if p >= 2:
                    dve.wait_ge(o_ps, b * KV + p - 1)
                dve.tensor_tensor(pT_lo[:, p % 2, 0:KEYS0], a_bank[p % 2][:, :], f(pT_hi[:, p % 2, 0:KEYS0]), ALU.subtract)\
                    .then_inc(t_lo_s, 1)

            def probs_tail_1(b, p):
                dve.wait_ge(t_hi_s, b * 2 * KV + 2 * p + 2)
                dve.tensor_tensor(pT_lo[:, p % 2, KEYS0:], b_bank[:, 0:KEYS1], f(pT_hi[:, p % 2, KEYS0:]), ALU.subtract)\
                    .then_inc(t_lo_s, 1)

            def output_copy(b, p):
                dve.wait_ge(o_ps, b * KV + p + 1)
                dve.tensor_copy(oT[:, p % KV, :, :].rearrange("p j n -> p (j n)"), o_bank[0:VW, :]).then_inc(o_s, 1)

            def attention_sums(b, p, alone):
                if not alone:
                    dve.wait_ge(t_hi_s, b * 2 * KV + 2 * (p + 3) + 2)
                dve.wait_ge(g_ps, b * KV + p + 1)
                dve.wait_ge(ao_s, b * KV + p + 1)
                out = b_bank[:, G:G + QT * REP * VW].rearrange("p (h c) -> p h c", c=VW)
                dve.tensor_reduce(ao_sum[:, :, :], out[:, :, 0:2 * HD].rearrange("p h (a d) -> p h d a", a=2), AX_X, ALU.add)
                dve.reciprocal(rinv[:, :], out[:, :, 2 * HD]).then_inc(sum_s, 1)

            def attention_out(b, p):
                dve.wait_ge(sum_s, b * KV + p + 1)
                dve.tensor_tensor(k.ao[:, bass.ds(b * QT, QT), REP * p:REP * (p + 1), :],
                                  ao_sum[:, :, :].rearrange("p (t h) d -> p t h d", t=QT),
                                  rinv[:, :].rearrange("p (t h) -> p t h", t=QT).unsqueeze(3).broadcast_to([P, QT, REP, HD]),
                                  ALU.mult).then_inc(ao_s, 1)

            def steps(b, which, last_batch=False):
                end = KV if last_batch else which.stop + 2
                for p in which:
                    if 0 <= p + 2 < end:
                        maxima(b, p + 2)
                    if 0 <= p < end:
                        probs_tail(b, p)
                    if 0 <= p - 3:
                        attention_sums(b, p - 3, p >= end)
                    if 0 <= p < end:
                        probs_tail_1(b, p)
                    if 0 <= p - 3:
                        attention_out(b, p - 3)
                    if 0 <= p - 1 < end and p % 2 == 0:
                        output_copy(b, p - 1)

            dve.sem_inc(ao_s, 1)
            quad_tails(0)
            dve.wait_ge(v_hi_s, 1)
            dve.tensor_tensor(v_all[:, :, :, HD:2 * HD], k.qkv[:, :, FH + KV:, :], f(v_all[:, :, :, 0:HD]), ALU.subtract).then_inc(v_lo_s, 1)
            for b in range(B):
                if b + 1 < B:
                    quad_tails(b + 1)
                keys_first(b)
            steps(0, FIRST)
            with dve.Fori(0, B - 1) as b:
                steps(b, BODY)
            steps(B - 1, BODY, True)


def residual(pe, k, c, x, first):
    for t in range(4):
        last = pe.matmul(k.d_bank[c][:, t * P:(t + 1) * P], x[:, 4 * c + t, :], k.ident[:, :],
                         start=first and t == 0, stop=not first and t == 3)
    return last


def route(nc, k, dram):
    with ExitStack() as ctx:
        sb, sem, bank = stage_helpers(nc, ctx)
        aoT, h2T = sb("aoT", [P, TOK]), sb("h2T", [P, TOK])
        sq, h2 = sb("sq5", [P, TT, D]), sb("h2", [P, TT, D])
        sum_sq, mean_sq, rrms = sb("sum_sq5", [P, TT]), sb("mean_sq5", [P, TT]), sb("rrms5", [P, TT])
        logits, expd, probs, pick, pick2 = (sb(n, [P, TT, E]) for n in ("logits", "expd", "probs", "pick", "pick2"))
        top, top_at, top_at_f = sb("top", [P, TT, 8]), sb("top_at", [P, TT, 8], U32), sb("top_at_f", [P, TT, 2])
        lmax, lsum, lrec, tsum, trec = (sb(n, [P, TT]) for n in ("lmax", "lsum", "lrec", "tsum", "trec"))
        topn = sb("topn", [P, TT, 2])
        pT = [bank(f"p_aoT{i}") for i in range(2)]
        pA = [bank(f"p_att{i}", (P, 4, D)) for i in range(2)]
        pH = pT
        pL = bank("p_logits", (P, TT, E))
        aoT_ps, aoT_s, att_ps, x2_s, sq_s, mean_s, rrms_s, h2_s, h2T_ps, h2T_s, h2T_hi_s, logit_ps, shifted_s, exp_s, step = (
            sem(f"{n}5") for n in ("aoT_ps", "aoT_s", "att_ps", "x2_s", "sq_s", "mean_s", "rrms_s", "h2_s", "h2T_ps", "h2T_s",
                                   "h2T_hi_s", "logit_ps", "shifted_s", "exp_s", "step"))
        block = ctx.enter_context(nc.Block())

        def half(i):
            return range(4 * i, 4 * i + 4)

        @block.tensor
        def _(pe):
            for i in range(2):
                for t in half(i):
                    last = pe.transpose(pT[i][:, (t % 4) * P:(t % 4 + 1) * P],
                                        k.ao[:, t, :, :].rearrange("p h d -> p (h d)"), k.ident[:, :])
                last.then_inc(aoT_ps, 1)
            for i in range(2):
                pe.wait_ge(aoT_s, i + 1)
                for t in half(i):
                    last = pe.matmul(pA[i][:, t % 4, :], aoT[:, t * P:(t + 1) * P], k.wo[:, :], start=True, stop=True)
                last.then_inc(att_ps, 1)
            for i in range(2):
                pe.wait_ge(x2_s, i + 1)
                residual(pe, k, i, k.x2, True)
            for i in range(2):
                pe.wait_ge(h2_s, i + 1)
                for t in half(i):
                    last = pe.transpose(pH[i][:, (t % 4) * P:(t % 4 + 1) * P], h2[:, t, :], k.ident[:, :])
                last.then_inc(h2T_ps, 1)
            for i in range(2):
                pe.wait_ge(h2T_s, i + 1)
                for t in half(i):
                    last = pe.matmul(pL[:, t, :], h2T[:, t * P:(t + 1) * P], k.router[:, :], start=True, stop=True)
            last.then_inc(logit_ps, 1)

        @block.scalar
        def _(act):
            for i in range(2):
                act.wait_ge(aoT_ps, i + 1)
                act.activation(aoT[:, i * BANK:(i + 1) * BANK], pT[i][:, :], ACT.Copy).then_inc(aoT_s, 1)
            for i in range(2):
                act.wait_ge(x2_s, i + 1)
                for t in half(i):
                    last = act.activation(sq[:, t, :], k.x2[:, t, :], ACT.Square, accum_out=sum_sq[:, t:t + 1])
                last.then_inc(sq_s, 1)
            for i in range(2):
                act.wait_ge(h2T_ps, i + 1)
                act.activation(h2T[:, i * BANK:(i + 1) * BANK], pH[i][:, :], ACT.Copy).then_inc(h2T_s, 1)
            act.wait_ge(h2T_s, 2)
            for i in range(2):
                last = act.activation(k.h2T_hi[:, i * BANK:(i + 1) * BANK], h2T[:, i * BANK:(i + 1) * BANK], ACT.Copy)
                last.then_inc(h2T_hi_s, 1)
            act.wait_ge(shifted_s, 1)
            act.activation(expd[:, :, :], logits[:, :, :], ACT.Exp).then_inc(exp_s, 1)

        @block.gpsimd
        def _(pool):
            for i in range(2):
                t = slice(4 * i, 4 * i + 4)
                pool.wait_ge(sq_s, i + 1)
                pool.tensor_scalar(mean_sq[:, t], sum_sq[:, t], 1.0 / D, RMS_EPS, ALU.mult, ALU.add).then_inc(mean_s, 1)
                pool.wait_ge(mean_s, i + 1)
                pool.tensor_tensor(rrms[:, t], mean_sq[:, t], k.inv_root[:, :].broadcast_to([P, TT // 2]), ALU.pow).then_inc(rrms_s, 1)
            for i in range(2):
                cols = slice(i * BANK, (i + 1) * BANK)
                pool.wait_ge(h2T_hi_s, i + 1)
                pool.tensor_tensor(k.h2T_lo[:, cols], h2T[:, cols], f(k.h2T_hi[:, cols]), ALU.subtract)

        @block.vector
        def _(dve):
            count = [0]

            def link(ins):
                count[0] += 1
                ins.then_inc(step, 1)
                dve.wait_ge(step, count[0])

            for i in range(2):
                dve.wait_ge(att_ps, i + 1)
                dve.tensor_tensor(k.x2[:, 4 * i:4 * i + 4, :], k.z[:, 4 * i:4 * i + 4, :], pA[i][:, :, :], ALU.add).then_inc(x2_s, 1)
            for i in range(2):
                dve.wait_ge(x2_s, i + 1)
                dve.wait_ge(rrms_s, i + 1)
                for t in half(i):
                    last = dve.scalar_tensor_tensor(h2[:, t, :], k.x2[:, t, :], rrms[:, t:t + 1], k.ln2_row[:, :], ALU.mult, ALU.mult)
                last.then_inc(h2_s, 1)

            def wide(col, n=E):
                return col.unsqueeze(2).broadcast_to([P, TT, n])

            dve.wait_ge(logit_ps, 1)
            link(dve.tensor_reduce(lmax[:, :], pL[:, :, :], AX_X, ALU.max))
            dve.tensor_tensor(logits[:, :, :], pL[:, :, :], wide(lmax[:, :]), ALU.subtract).then_inc(shifted_s, 1)
            dve.wait_ge(exp_s, 1)
            link(dve.tensor_reduce(lsum[:, :], expd[:, :, :], AX_X, ALU.add))
            link(dve.reciprocal(lrec[:, :], lsum[:, :]))
            link(dve.tensor_tensor(probs[:, :, :], expd[:, :, :], wide(lrec[:, :]), ALU.mult))
            for t in range(TT):
                last = dve.max(top[:, t, :], probs[:, t, :])
            link(last)
            for t in range(TT):
                last = dve.max_index(top_at[:, t, :], top[:, t, :], probs[:, t, :])
            link(last)
            dve.tensor_copy(top_at_f[:, :, :], top_at[:, :, 0:2])
            link(dve.tensor_tensor(tsum[:, :], top[:, :, 0], top[:, :, 1], ALU.add))
            link(dve.reciprocal(trec[:, :], tsum[:, :]))
            link(dve.tensor_tensor(topn[:, :, :], top[:, :, 0:2], wide(trec[:, :], 2), ALU.mult))
            ids = k.iota[:, :].unsqueeze(1).broadcast_to([P, TT, E])
            for i, one in enumerate((pick, pick2)):
                last = dve.tensor_tensor(one[:, :, :], ids, wide(top_at_f[:, :, i]), ALU.is_equal)
            link(last)
            for i, one in enumerate((pick, pick2)):
                last = dve.tensor_tensor(one[:, :, :], one[:, :, :], wide(topn[:, :, i]), ALU.mult)
            link(last)
            link(dve.tensor_tensor(k.weights[:, :, :], pick[:, :, :], pick2[:, :, :], ALU.add))


def fetch_pair(sp, k, dram, g):
    for which, name in enumerate(("L0_ffn_w_gate", "L0_ffn_w_up")):
        sp.dma_start(k.gu_raw[:, which, :, :], dram[name][bass.ds(2 * g, 2), :, :].rearrange("e d m -> d e m"))\
            .then_inc(k.raw_in, 16)
    rows = dram["L0_ffn_w_down"].rearrange("(g e) m d -> g (e m) d", e=2)
    sp.dma_start(k.dn_raw[:, :, :], rows[bass.ds(g, 1), :, :].rearrange("g (s r) d -> r (g s) d", r=P)).then_inc(k.raw_in, 16)


def split_pair(pool, k, g, slot, free=None):
    pool.wait_ge(k.raw_in, (g + 1) * 48)
    if free is not None:
        pool.wait_ge(*free)
    pool.tensor_tensor(k.dn_hi[:, slot, :, :], k.dn_raw[:, :, :], k.one[:, :].unsqueeze(2).broadcast_to([P, SLABS, D]),
                       ALU.mult)
    pool.tensor_scalar(k.gu_hi[:, slot, :, :], k.gu_raw[:, :, :, :].rearrange("p a e m -> p a (e m)"), 1.0, 1.0,
                       ALU.mult, ALU.mult).then_inc(k.hi_made, 1)
    pool.wait_ge(k.hi_made, g + 1)
    pool.tensor_tensor(k.gu_lo[:, slot, :, :], k.gu_raw[:, :, :, :].rearrange("p a e m -> p a (e m)"),
                       f(k.gu_hi[:, slot, :, :]), ALU.subtract)
    pool.tensor_tensor(k.dn_lo[:, slot, :, :], k.dn_raw[:, :, :], f(k.dn_hi[:, slot, :, :]), ALU.subtract)\
        .then_inc(k.split_s, 1)


def experts(nc, k, dram, out):
    with ExitStack() as ctx:
        sb, sem, bank = stage_helpers(nc, ctx)
        wcol = sb("wcol", [P, E, TT])
        wide = sb("wide", [P, E, TOK])
        wide_mix = sb("wide_mix", [P, 2, TOK])
        up_w = sb("up_w", [P, 2, BANK])
        gate = sb("gate", [P, 2, BANK])
        act_f = sb("act_f", [P, 2, BANK])
        act_hi, act_lo = sb("act_hi", [P, 2, BANK], F32R), sb("act_lo", [P, 2, BANK], F32R)
        warm = sb("warm", [P, 1])
        sumT, res = sb("sumT", [P, TOK]), sb("res", [P, TT, D])
        g_bank, u_bank = ([bank(f"{n}_bank{i}") for i in range(3)] for n in "gu")
        d_bank = k.d_bank
        w_bank = g_bank + u_bank
        wcol_s, w_ps, w_s, w_s2, mix_s, sum_ps, out_ps, out_s = (
            sem(n) for n in ("wcol_s", "w_ps", "w_s", "w_s2", "mix_s", "sum_ps", "out_ps", "out_s"))
        sumT_s, res_s = ([sem(f"{n}{c}") for c in range(CH)] for n in ("sumT_s", "res_s"))
        gu_ps, silu_s, weighed_s, mul_s, a_hi_s, a_lo_s, down_ps = (
            sem(n) for n in ("gu_ps", "silu_s", "weighed_s", "mul_s", "a_hi_s", "a_lo_s", "down_ps"))
        U = CH * SLABS
        ROWS = E * CH
        block = ctx.enter_context(nc.Block())

        MIXED, SPLIT = HID // P, HID % P
        PARTS = (slice(0, SPLIT), slice(SPLIT, P))

        def where(n):
            return n // U, (n % U) // SLABS, n % SLABS

        @block.sync
        def _(sp):
            with sp.Fori(1, PAIRS) as g:
                sp.wait_ge(k.split_s, g)
                fetch_pair(sp, k, dram, g)
            for c in range(CH):
                sp.wait_ge(res_s[c], 1)
                sp.dma_start(in_tiles(out)[:, 4 * c:4 * c + 4, :], res[:, 4 * c:4 * c + 4, :]).then_inc(out_s, 16)
            sp.wait_ge(out_s, CH * 16)

        @block.gpsimd
        def _(pool):
            split_pair(pool, k, 1, 1)
            with pool.Fori(1, PAIRS // 2) as g:
                for slot in range(2):
                    split_pair(pool, k, g * 2 + slot, slot, (down_ps, (g * 2 + slot - 1) * U))

        @block.tensor
        def _(pe):
            def weight_row(r):
                e, c = divmod(r, CH)
                if r >= len(w_bank):
                    pe.wait_ge(*((w_s, (r - 6) // 2 + 1) if r % 2 == 0 else (w_s2, (r - 6) // 2 + 1)))
                for t in range(4):
                    last = pe.transpose(w_bank[r % 6][:, t * P:(t + 1) * P],
                                        wcol[:, e, 4 * c + t:4 * c + t + 1].broadcast_to([P, P]), k.ident[:, :])
                last.then_inc(w_ps, 1)

            pe.wait_ge(wcol_s, 1)
            for r in range(ROWS):
                weight_row(r)
            pe.wait_ge(w_s, ROWS // 2)
            pe.wait_ge(w_s2, ROWS // 2)
            with pe.Fori(0, PAIRS // 2) as g:
                def gate_up(n):
                    slot, c, s = where(n)
                    if n >= 3:
                        pe.wait_ge(silu_s, g * 2 * U + n - 2)
                        pe.wait_ge(weighed_s, g * 2 * U + n - 2)
                    for which, out in ((0, g_bank[n % 3]), (1, u_bank[n % 3])):
                        for m, (w, x) in enumerate(((k.gu_hi, k.h2T_hi), (k.gu_hi, k.h2T_lo), (k.gu_lo, k.h2T_hi))):
                            last = pe.matmul(out[:, :], w[:, slot, which, s * P:(s + 1) * P],
                                             x[:, c * BANK:(c + 1) * BANK], start=m == 0, stop=m == 2)
                    last.then_inc(gu_ps, 1)

                def down(n):
                    slot, c, s = where(n)
                    pe.wait_ge(a_lo_s, g * 2 * U + n + 1)
                    for m, (w, x) in enumerate(((k.dn_hi, act_hi), (k.dn_hi, act_lo), (k.dn_lo, act_hi))):
                        last = pe.matmul(d_bank[c][:, :], w[:, slot, s, :], x[:, n % 2, :], start=False, stop=False)
                    last.then_inc(down_ps, 1)

                for n in range(2 * U + 2):
                    if n < 2 * U:
                        if n % U == 0:
                            pe.wait_ge(k.split_s, g * 2 + n // U + 1)
                        gate_up(n)
                    if n >= 2:
                        down(n - 2)
            for c in range(CH):
                residual(pe, k, c, k.x1, False).then_inc(sum_ps, 1)
            for c in range(CH):
                pe.wait_ge(sumT_s[c], 1)
                for t in range(4):
                    last = pe.transpose(g_bank[c][:, t * P:(t + 1) * P], sumT[:, c * BANK + t * P:c * BANK + (t + 1) * P],
                                        k.ident[:, :])
                last.then_inc(out_ps, 1)

        @block.scalar
        def _(act):
            act.activation(warm[:, :], k.one[:, :], ACT.Silu)
            for r in range(0, ROWS, 2):
                e, c = divmod(r, CH)
                act.wait_ge(w_ps, r + 1)
                act.activation(wide[:, e, c * BANK:(c + 1) * BANK], w_bank[r % 6][:, :], ACT.Copy).then_inc(w_s, 1)
            act.wait_ge(w_s, ROWS // 2)
            act.wait_ge(w_s2, ROWS // 2)
            with act.Fori(0, PAIRS // 2) as g:
                def mix(slot, i):
                    w = wide[PARTS[i], bass.ds(g * 4 + slot * 2 + i, 1), :].rearrange("p e n -> p (e n)")
                    act.activation(wide_mix[PARTS[i], slot, :], w, ACT.Copy).then_inc(mix_s, 1)

                def silu(n):
                    act.wait_ge(gu_ps, g * 2 * U + n + 1)
                    if n >= 2:
                        act.wait_ge(mul_s, g * 2 * U + n - 1)
                    act.activation(gate[:, n % 2, :], g_bank[n % 3][:, :], ACT.Silu).then_inc(silu_s, 1)

                def head(n):
                    act.wait_ge(mul_s, g * 2 * U + n + 1)
                    if n >= 2:
                        act.wait_ge(down_ps, g * 2 * U + n - 1)
                    act.activation(act_hi[:, n % 2, :], act_f[:, n % 2, :], ACT.Copy).then_inc(a_hi_s, 1)

                for n in range(2 * U + 1):
                    if n >= 1:
                        head(n - 1)
                    if n < 2 * U:
                        silu(n)
                        if n % U < 2:
                            mix(n // U, n % U)
            act.wait_ge(sum_ps, 1)
            act.activation(sumT[:, 0:BANK], d_bank[0][:, :], ACT.Copy).then_inc(sumT_s[0], 1)
            act.wait_ge(out_ps, 1)
            act.activation(res[:, 0:4, :], g_bank[0][:, :].rearrange("p (t d) -> p t d", t=4), ACT.Copy).then_inc(res_s[0], 1)

        @block.vector
        def _(dve):
            dve.tensor_copy(wcol[:, :, :], k.weights[:, :, :].rearrange("p t e -> p e t")).then_inc(wcol_s, 1)
            for r in range(1, ROWS, 2):
                e, c = divmod(r, CH)
                dve.wait_ge(w_ps, r + 1)
                dve.tensor_copy(wide[:, e, c * BANK:(c + 1) * BANK], w_bank[r % 6][:, :]).then_inc(w_s2, 1)
            dve.wait_ge(w_s, ROWS // 2)
            dve.wait_ge(w_s2, ROWS // 2)
            with dve.Fori(0, PAIRS // 2) as g:
                def weigh(n):
                    slot, c, s = where(n)
                    dve.wait_ge(gu_ps, g * 2 * U + n + 1)
                    if n >= 2:
                        dve.wait_ge(mul_s, g * 2 * U + n - 1)
                    if s == MIXED:
                        dve.wait_ge(mix_s, g * 4 + slot * 2 + 2)
                        w = wide_mix[:, slot, c * BANK:(c + 1) * BANK]
                    else:
                        w = wide[:, bass.ds(g * 4 + slot * 2 + (s > MIXED), 1), c * BANK:(c + 1) * BANK].rearrange("p e n -> p (e n)")
                    last = dve.tensor_tensor(up_w[:, n % 2, :], u_bank[n % 3][:, :], w, ALU.mult)
                    last.then_inc(weighed_s, 1)

                def product(n):
                    if n >= 2:
                        dve.wait_ge(a_lo_s, g * 2 * U + n - 1)
                    dve.wait_ge(silu_s, g * 2 * U + n + 1)
                    dve.wait_ge(weighed_s, g * 2 * U + n + 1)
                    dve.tensor_tensor(act_f[:, n % 2, :], up_w[:, n % 2, :], gate[:, n % 2, :], ALU.mult).then_inc(mul_s, 1)

                def tail(n):
                    dve.wait_ge(a_hi_s, g * 2 * U + n + 1)
                    dve.tensor_tensor(act_lo[:, n % 2, :], act_f[:, n % 2, :], f(act_hi[:, n % 2, :]), ALU.subtract).then_inc(a_lo_s, 1)

                for n in range(2 * U + 1):
                    if n < 2 * U:
                        weigh(n)
                    if n >= 1:
                        tail(n - 1)
                    if n < 2 * U:
                        product(n)
            dve.wait_ge(sum_ps, 2)
            dve.tensor_copy(sumT[:, BANK:TOK], d_bank[1][:, :]).then_inc(sumT_s[1], 1)
            dve.wait_ge(out_ps, 2)
            dve.tensor_copy(res[:, 4:8, :], g_bank[1][:, :].rearrange("p (t d) -> p t d", t=4)).then_inc(res_s[1], 1)


def build(nc, dram, out):
    k = Kernel()
    with ExitStack() as ctx:
        def sb(name, shape, dt=F32):
            return ctx.enter_context(nc.sbuf_tensor(name, shape, dt))

        k.x, k.ident = sb("x", [P, TT, D]), sb("ident", [P, P])
        k.one, k.inv_root = sb("one", [P, 1]), sb("inv_root", [P, 1])
        k.yT = sb("yT", [P, TOK])
        k.bias_row, k.scale_row, k.ln2_row = (sb(n, [P, D]) for n in ("bias_row", "scale_row", "ln2_row"))
        k.wqkv, k.ln1_col = sb("wqkv", [P, FH + 2 * KV, HD]), sb("ln1_col", [P, 1])
        k.cos, k.sin = sb("cos", [P, QT, HD]), sb("sin", [P, QT, HD])
        k.wo, k.router, k.iota = sb("wo", [P, D]), sb("router", [P, E]), sb("iota", [P, E])
        with ExitStack() as own:
            def sw(name, shape, dt=F32R):
                return own.enter_context(nc.sbuf_tensor(name, shape, dt))

            k.wq_hi, k.wq_lo = (sw(f"wq_{s}", [P, H, 2, DH]) for s in ("hi", "lo"))
            k.wkv_hi, k.wkv_lo = (sw(f"wkv_{s}", [P, CT, 2 * INNER]) for s in ("hi", "lo"))
            k.wout_hi, k.wout_lo = (sw(f"wout_{s}", [P, H, D]) for s in ("hi", "lo"))
            k.xnT_hi, k.xnT_lo = (sw(f"xnT_{s}", [P, TOK]) for s in ("hi", "lo"))
            k.u_hi, k.u_lo = (sw(f"u_{s}", [H, D]) for s in ("hi", "lo"))
            k.s0n = sw("s0n", [P, TT, H], F32)
            k.ctx_raw = sw("ctx_raw", [P, KT, C], F32)
            k.cT_hi, k.cT_lo = (sw(f"cT_{s}", [P, CT, M]) for s in ("hi", "lo"))
            k.keys = sw("keys", [P, H, M])
            k.vals = sw("vals", [P, KT, H, 2 * DH])
            k.ctx_in, k.proj_ps, k.proj_hi, k.proj_lo = (
                own.enter_context(nc.semaphore(n)) for n in ("ctx_in", "proj_ps", "proj_hi", "proj_lo"))
            load_and_split(nc, k, dram)
            cross_attention(nc, k, dram)
        k.x1, k.z = (sb(n, [P, TT, D]) for n in ("x1", "z"))
        k.mv_x, k.rstd_x = sb("mv_x", [P, TT, 2]), sb("rstd_x", [P, TT])
        k.rq, k.rk = sb("rq", [P, TT, FH, HD]), sb("rk", [P, TT, KV, HD])
        k.qkv = sb("qkv", [P, TT, FH + 2 * KV, HD])
        k.ao = sb("ao", [P, TT, FH, HD])
        k.gu_raw, k.dn_raw = sb("gu_raw", [P, 2, 2, HID]), sb("dn_raw", [P, SLABS, D])
        k.gu_hi, k.gu_lo = (sb(f"gu_{s}", [P, 2, 2, 2 * HID], F32R) for s in ("hi", "lo"))
        k.dn_hi, k.dn_lo = (sb(f"dn_{s}", [P, 2, SLABS, D], F32R) for s in ("hi", "lo"))
        k.raw_in, k.hi_made, k.split_s = (ctx.enter_context(nc.semaphore(n)) for n in ("raw_in", "hi_made", "split_s"))
        residual_and_projections(nc, k, dram)
        self_attention(nc, k, dram)
        k.d_bank = [ctx.enter_context(nc.psum_tensor(f"d_bank{c}", [P, BANK], F32)) for c in range(CH)]
        k.x2, k.weights = sb("x2", [P, TT, D]), sb("weights", [P, TT, E])
        k.h2T_hi, k.h2T_lo = sb("h2T_hi", [P, TOK], F32R), sb("h2T_lo", [P, TOK], F32R)
        route(nc, k, dram)
        experts(nc, k, dram, out)


def shape_constants():
    import numpy as np

    angle = np.arange(N, dtype=np.float32)[:, None] * (1.0 / 10000.0 ** (np.arange(0, HD, 2, dtype=np.float32) / HD)).astype(np.float32)
    cos, sin = np.cos(angle), np.sin(angle)
    hidden = np.triu(np.full((P, P), MASKED, np.float32), 1)
    return {
        "identity": np.eye(P, dtype=np.float32),
        "rope_cos": np.concatenate([cos, cos], -1).astype(np.float32),
        "rope_sin": np.concatenate([-sin, sin], -1).astype(np.float32),
        "causal": np.concatenate([hidden] * QT, -1),
        "expert_ids": np.arange(E, dtype=np.float32),
    }


def kernel(**inputs):
    import numpy as np
    import concourse.bacc as bacc
    from concourse.bass_utils import run_bass_kernel_spmd

    nc = bacc.Bacc("TRN2", target_bir_lowering=False, num_devices=1)
    arrays = {name: np.ascontiguousarray(a) for name, a in {**inputs, **shape_constants()}.items()}
    dram = {name: nc.dram_tensor(f"in_{name}", a.shape, mybir.dt.from_np(a.dtype), kind="ExternalInput").ap()
            for name, a in arrays.items()}
    out = nc.dram_tensor("out", (B, N, D), F32, kind="ExternalOutput").ap()
    build(nc, dram, out)
    r = run_bass_kernel_spmd(nc, [{f"in_{name}": a for name, a in arrays.items()}], core_ids=[0])
    return r.results[0]["out"]
```
